# Optimizing a Trainium2 kernel written in Bass

```python
import numpy as np
import jax
import jax.numpy as jnp

def _softmax(x, axis=-1):
    return jax.nn.softmax(x, axis=axis)

def _gelu(x):
    return jax.nn.gelu(x, approximate=True)

def _silu(x):
    return jax.nn.silu(x)

def _sigmoid(x):
    return jax.nn.sigmoid(x)

def _layernorm(x, axis=-1, eps=1e-05):
    m = jnp.mean(x, axis=axis, keepdims=True)
    v = jnp.var(x, axis=axis, keepdims=True)
    return (x - m) / jnp.sqrt(v + eps)

def _scatter_add(tgt, idx, src, axis=0):
    return tgt.at[idx].add(src)

def _segment_sum(src, seg, n):
    return jax.ops.segment_sum(src, seg, n)
kernel_name = 'mk_hybrid_d1_jaxref_r8_a5a37f'

def setup_inputs(seed: int=0):
    np.random.seed(seed)
    _w = jnp.asarray

    def _L0_attn_a_setup():
        import jax, jax.numpy as jnp
        import numpy as np
        B, T, D = (2, 256, 128)
        HEAD_DIM, N_HEADS, N_HH, HEAD_V_DIM, CONV_SIZE = (128, 8, 3, 128, 4)

        def _short_conv(x, w):
            cs = w.shape[-1]
            t = x.shape[1]
            xp = jnp.pad(x, ((0, 0), (cs - 1, 0), (0, 0)))
            y = sum((xp[:, i:i + t, :] * w[:, i] for i in range(cs)))
            return jax.nn.silu(y)

        def _l2norm(x, eps=1e-06):
            return x * jax.lax.rsqrt(jnp.sum(x * x, -1, keepdims=True) + eps)

        def _forward(x, Wq, Wk, Wv, Wb, Wa, A_log, dt_bias, conv_q, conv_k, conv_v, Wg, rms_weight, Wo):
            b, t, _ = x.shape
            h, d, dv, nh = (N_HEADS, HEAD_DIM, HEAD_V_DIM, N_HH)
            q = _short_conv(x @ Wq, conv_q).reshape(b, t, h, d)
            k = _short_conv(x @ Wk, conv_k).reshape(b, t, nh, h, d).transpose(0, 1, 3, 2, 4)
            v = _short_conv(x @ Wv, conv_v).reshape(b, t, nh, h, dv).transpose(0, 1, 3, 2, 4)
            beta = 2.0 * jax.nn.sigmoid(x @ Wb).reshape(b, t, nh, h).transpose(0, 1, 3, 2)
            g = -jnp.exp(A_log) * jax.nn.softplus(x @ Wa + dt_bias)
            q = _l2norm(q) * d ** (-0.5)
            k = _l2norm(k)

            def step(S, inp):
                qt, kt, vt, bt, gt = inp
                S = S * jnp.exp(gt)[..., None, None]
                for i in range(nh):
                    ki, vi, bi = (kt[:, :, i], vt[:, :, i], bt[:, :, i])
                    kS = jnp.einsum('bhd,bhde->bhe', ki, S)
                    S = S + bi[..., None, None] * (ki[..., None] * (vi - kS)[:, :, None, :])
                o = jnp.einsum('bhd,bhde->bhe', qt, S)
                return (S, o)
            xs = tuple((jnp.moveaxis(a, 1, 0) for a in (q, k, v, beta, g)))
            S0 = jnp.zeros((b, h, d, dv), x.dtype)
            _, o = jax.lax.scan(step, S0, xs)
            o = jnp.moveaxis(o, 0, 1)
            gate = (x @ Wg).reshape(b, t, h, dv)
            o = o * jax.lax.rsqrt(jnp.mean(o * o, -1, keepdims=True) + 1e-05) * rms_weight
            o = o * jax.nn.silu(gate)
            return o.reshape(b, t, h * dv) @ Wo
        key = jax.random.key(seed)
        ks = jax.random.split(key, 16)
        h, d, dv, nh, cs = (N_HEADS, HEAD_DIM, HEAD_V_DIM, N_HH, CONV_SIZE)
        f = lambda k, shape, s=0.02: jax.random.normal(k, shape, jnp.float32) * s
        return {'x': f(ks[0], (B, T, D), 1.0), 'cos': f(ks[1], (T, d), 1.0), 'sin': f(ks[2], (T, d), 1.0), 'Wq': f(ks[3], (D, h * d)), 'Wk': f(ks[4], (D, h * d * nh)), 'Wv': f(ks[5], (D, h * dv * nh)), 'Wb': f(ks[6], (D, h * nh)), 'Wa': f(ks[7], (D, h)), 'A_log': jnp.log(jax.random.uniform(ks[8], (h,), jnp.float32, 0.5, 8.0)), 'dt_bias': f(ks[9], (h,), 0.1), 'conv_q': f(ks[10], (h * d, cs), 0.5), 'conv_k': f(ks[11], (h * d * nh, cs), 0.5), 'conv_v': f(ks[12], (h * dv * nh, cs), 0.5), 'Wg': f(ks[13], (D, h * dv)), 'rms_weight': jnp.ones((dv,), jnp.float32), 'Wo': f(ks[14], (h * dv, D))}
    _L0_attn_a_in = _L0_attn_a_setup()

    def _L0_attn_b_setup():
        import jax, jax.numpy as jnp
        import numpy as np
        D = 128
        HS = 64
        H = D // HS
        B, T = (4, 256)
        EPS = 1e-05

        def _reference_tuple_inner(x, ln_g, ln_b, Wx, Ww, bw, Wk, Wv, Wr, Wo):
            Bb, Tt, C = x.shape
            nh, hs = (C // HS, HS)
            mu = x.mean(-1, keepdims=True)
            var = x.var(-1, keepdims=True)
            xn = (x - mu) / jnp.sqrt(var + EPS) * ln_g + ln_b
            w = jax.nn.sigmoid(xn @ Wx @ Ww + bw).reshape(Bb, Tt, nh, hs)
            k = (xn @ Wk).reshape(Bb, Tt, nh, hs)
            v = (xn @ Wv).reshape(Bb, Tt, nh, hs)
            r = jax.nn.sigmoid(xn @ Wr).reshape(Bb, Tt, nh, hs)

            def step(state, inp):
                kt, vt, wt, rt = inp
                state = (1.0 - wt)[..., None] * state + kt[..., None] * vt[..., None, :]
                out = jnp.einsum('bhd,bhde->bhe', rt, state)
                return (state, out)
            init = jnp.zeros((Bb, nh, hs, hs), x.dtype)
            tm = lambda a: jnp.moveaxis(a, 1, 0)
            state, outs = jax.lax.scan(step, init, (tm(k), tm(v), tm(w), tm(r)))
            y = jnp.moveaxis(outs, 0, 1).reshape(Bb, Tt, C) @ Wo
            return (y, state)
        key = jax.random.key(seed)
        ks = jax.random.split(key, 8)
        s = 1.0 / np.sqrt(D)
        mk = lambda k: jax.random.normal(k, (D, D), jnp.float32) * s
        return {'x': jax.random.normal(ks[0], (B, T, D), jnp.float32), 'ln_g': jnp.ones((D,), jnp.float32), 'ln_b': jnp.zeros((D,), jnp.float32), 'Wx': mk(ks[1]), 'Ww': mk(ks[2]), 'bw': jnp.zeros((D,), jnp.float32), 'Wk': mk(ks[3]), 'Wv': mk(ks[4]), 'Wr': mk(ks[5]), 'Wo': mk(ks[6])}
    _L0_attn_b_in = _L0_attn_b_setup()

    def _L0_ffn_setup():
        import jax, jax.numpy as jnp
        import numpy as np
        B, L, D = (2, 256, 128)
        E = 15
        H = D * 1
        K = 3
        T = 1.0
        key = jax.random.key(seed)
        ks = jax.random.split(key, 12)
        s = 0.02
        return {'x': jax.random.normal(ks[0], (B, L, D), dtype=jnp.float32), 'router_W': jax.random.normal(ks[1], (D, E), dtype=jnp.float32) * s, 'router_b': jnp.zeros((E,), dtype=jnp.float32), 'sW1': jax.random.normal(ks[2], (D, H), dtype=jnp.float32) * s, 'sb1': jnp.zeros((H,), dtype=jnp.float32), 'sW2': jax.random.normal(ks[3], (H, D), dtype=jnp.float32) * s, 'sb2': jnp.zeros((D,), dtype=jnp.float32), 'eW1': jax.random.normal(ks[4], (E, D, H), dtype=jnp.float32) * s, 'eb1': jnp.zeros((E, H), dtype=jnp.float32), 'eW2': jax.random.normal(ks[5], (E, H, D), dtype=jnp.float32) * s, 'eb2': jnp.zeros((E, D), dtype=jnp.float32)}
    _L0_ffn_in = _L0_ffn_setup()
    _d = {'L0_attn_a_x': _L0_attn_a_in['x'], 'L0_attn_a_cos': _L0_attn_a_in['cos'], 'L0_attn_a_sin': _L0_attn_a_in['sin'], 'L0_attn_a_Wq': _L0_attn_a_in['Wq'], 'L0_attn_a_Wk': _L0_attn_a_in['Wk'], 'L0_attn_a_Wv': _L0_attn_a_in['Wv'], 'L0_attn_a_Wb': _L0_attn_a_in['Wb'], 'L0_attn_a_Wa': _L0_attn_a_in['Wa'], 'L0_attn_a_A_log': _L0_attn_a_in['A_log'], 'L0_attn_a_dt_bias': _L0_attn_a_in['dt_bias'], 'L0_attn_a_conv_q': _L0_attn_a_in['conv_q'], 'L0_attn_a_conv_k': _L0_attn_a_in['conv_k'], 'L0_attn_a_conv_v': _L0_attn_a_in['conv_v'], 'L0_attn_a_Wg': _L0_attn_a_in['Wg'], 'L0_attn_a_rms_weight': _L0_attn_a_in['rms_weight'], 'L0_attn_a_Wo': _L0_attn_a_in['Wo'], 'L0_attn_b_ln_g': _L0_attn_b_in['ln_g'], 'L0_attn_b_ln_b': _L0_attn_b_in['ln_b'], 'L0_attn_b_Wx': _L0_attn_b_in['Wx'], 'L0_attn_b_Ww': _L0_attn_b_in['Ww'], 'L0_attn_b_bw': _L0_attn_b_in['bw'], 'L0_attn_b_Wk': _L0_attn_b_in['Wk'], 'L0_attn_b_Wv': _L0_attn_b_in['Wv'], 'L0_attn_b_Wr': _L0_attn_b_in['Wr'], 'L0_attn_b_Wo': _L0_attn_b_in['Wo'], 'L0_ffn_router_W': _L0_ffn_in['router_W'], 'L0_ffn_router_b': _L0_ffn_in['router_b'], 'L0_ffn_sW1': _L0_ffn_in['sW1'], 'L0_ffn_sb1': _L0_ffn_in['sb1'], 'L0_ffn_sW2': _L0_ffn_in['sW2'], 'L0_ffn_sb2': _L0_ffn_in['sb2'], 'L0_ffn_eW1': _L0_ffn_in['eW1'], 'L0_ffn_eb1': _L0_ffn_in['eb1'], 'L0_ffn_eW2': _L0_ffn_in['eW2'], 'L0_ffn_eb2': _L0_ffn_in['eb2']}
    _x0 = _d['L0_attn_a_x']
    _d['L0_attn_a_x'] = jax.random.normal(jax.random.fold_in(jax.random.key(seed), 1), (4, 1024, 128), dtype=_x0.dtype)
    del _x0
    return _d

def reference(L0_attn_a_x, L0_attn_a_cos, L0_attn_a_sin, L0_attn_a_Wq, L0_attn_a_Wk, L0_attn_a_Wv, L0_attn_a_Wb, L0_attn_a_Wa, L0_attn_a_A_log, L0_attn_a_dt_bias, L0_attn_a_conv_q, L0_attn_a_conv_k, L0_attn_a_conv_v, L0_attn_a_Wg, L0_attn_a_rms_weight, L0_attn_a_Wo, L0_attn_b_ln_g, L0_attn_b_ln_b, L0_attn_b_Wx, L0_attn_b_Ww, L0_attn_b_bw, L0_attn_b_Wk, L0_attn_b_Wv, L0_attn_b_Wr, L0_attn_b_Wo, L0_ffn_router_W, L0_ffn_router_b, L0_ffn_sW1, L0_ffn_sb1, L0_ffn_sW2, L0_ffn_sb2, L0_ffn_eW1, L0_ffn_eb1, L0_ffn_eW2, L0_ffn_eb2):

    def _L0_attn_a_ref(x, cos, sin, Wq, Wk, Wv, Wb, Wa, A_log, dt_bias, conv_q, conv_k, conv_v, Wg, rms_weight, Wo):
        import jax, jax.numpy as jnp
        import numpy as np
        B, T, D = (2, 256, 128)
        HEAD_DIM, N_HEADS, N_HH, HEAD_V_DIM, CONV_SIZE = (128, 8, 3, 128, 4)

        def _short_conv(x, w):
            cs = w.shape[-1]
            t = x.shape[1]
            xp = jnp.pad(x, ((0, 0), (cs - 1, 0), (0, 0)))
            y = sum((xp[:, i:i + t, :] * w[:, i] for i in range(cs)))
            return jax.nn.silu(y)

        def _l2norm(x, eps=1e-06):
            return x * jax.lax.rsqrt(jnp.sum(x * x, -1, keepdims=True) + eps)

        def _forward(x, Wq, Wk, Wv, Wb, Wa, A_log, dt_bias, conv_q, conv_k, conv_v, Wg, rms_weight, Wo):
            b, t, _ = x.shape
            h, d, dv, nh = (N_HEADS, HEAD_DIM, HEAD_V_DIM, N_HH)
            q = _short_conv(x @ Wq, conv_q).reshape(b, t, h, d)
            k = _short_conv(x @ Wk, conv_k).reshape(b, t, nh, h, d).transpose(0, 1, 3, 2, 4)
            v = _short_conv(x @ Wv, conv_v).reshape(b, t, nh, h, dv).transpose(0, 1, 3, 2, 4)
            beta = 2.0 * jax.nn.sigmoid(x @ Wb).reshape(b, t, nh, h).transpose(0, 1, 3, 2)
            g = -jnp.exp(A_log) * jax.nn.softplus(x @ Wa + dt_bias)
            q = _l2norm(q) * d ** (-0.5)
            k = _l2norm(k)

            def step(S, inp):
                qt, kt, vt, bt, gt = inp
                S = S * jnp.exp(gt)[..., None, None]
                for i in range(nh):
                    ki, vi, bi = (kt[:, :, i], vt[:, :, i], bt[:, :, i])
                    kS = jnp.einsum('bhd,bhde->bhe', ki, S)
                    S = S + bi[..., None, None] * (ki[..., None] * (vi - kS)[:, :, None, :])
                o = jnp.einsum('bhd,bhde->bhe', qt, S)
                return (S, o)
            xs = tuple((jnp.moveaxis(a, 1, 0) for a in (q, k, v, beta, g)))
            S0 = jnp.zeros((b, h, d, dv), x.dtype)
            _, o = jax.lax.scan(step, S0, xs)
            o = jnp.moveaxis(o, 0, 1)
            gate = (x @ Wg).reshape(b, t, h, dv)
            o = o * jax.lax.rsqrt(jnp.mean(o * o, -1, keepdims=True) + 1e-05) * rms_weight
            o = o * jax.nn.silu(gate)
            return o.reshape(b, t, h * dv) @ Wo
        return _forward(x, Wq, Wk, Wv, Wb, Wa, A_log, dt_bias, conv_q, conv_k, conv_v, Wg, rms_weight, Wo)

    def _L0_attn_b_ref(x, ln_g, ln_b, Wx, Ww, bw, Wk, Wv, Wr, Wo):
        import jax, jax.numpy as jnp
        import numpy as np
        D = 128
        HS = 64
        H = D // HS
        B, T = (4, 256)
        EPS = 1e-05

        def _reference_tuple_inner(x, ln_g, ln_b, Wx, Ww, bw, Wk, Wv, Wr, Wo):
            Bb, Tt, C = x.shape
            nh, hs = (C // HS, HS)
            mu = x.mean(-1, keepdims=True)
            var = x.var(-1, keepdims=True)
            xn = (x - mu) / jnp.sqrt(var + EPS) * ln_g + ln_b
            w = jax.nn.sigmoid(xn @ Wx @ Ww + bw).reshape(Bb, Tt, nh, hs)
            k = (xn @ Wk).reshape(Bb, Tt, nh, hs)
            v = (xn @ Wv).reshape(Bb, Tt, nh, hs)
            r = jax.nn.sigmoid(xn @ Wr).reshape(Bb, Tt, nh, hs)

            def step(state, inp):
                kt, vt, wt, rt = inp
                state = (1.0 - wt)[..., None] * state + kt[..., None] * vt[..., None, :]
                out = jnp.einsum('bhd,bhde->bhe', rt, state)
                return (state, out)
            init = jnp.zeros((Bb, nh, hs, hs), x.dtype)
            tm = lambda a: jnp.moveaxis(a, 1, 0)
            state, outs = jax.lax.scan(step, init, (tm(k), tm(v), tm(w), tm(r)))
            y = jnp.moveaxis(outs, 0, 1).reshape(Bb, Tt, C) @ Wo
            return (y, state)
        return _reference_tuple_inner(x, ln_g, ln_b, Wx, Ww, bw, Wk, Wv, Wr, Wo)[0]

    def _L0_ffn_ref(x, router_W, router_b, sW1, sb1, sW2, sb2, eW1, eb1, eW2, eb2):
        import jax, jax.numpy as jnp
        import numpy as np
        B, L, D = (2, 256, 128)
        E = 15
        H = D * 1
        K = 3
        T = 1.0
        b, l, d = x.shape
        n = b * l
        xt = x.reshape(n, d)
        shared = jax.nn.relu(xt @ sW1 + sb1) @ sW2 + sb2
        logits = xt @ router_W + router_b
        probs = jax.nn.softmax(logits / T, axis=-1)
        top_p, top_i = jax.lax.top_k(probs, K)
        cw = jnp.zeros((n, E), dtype=probs.dtype)
        cw = cw.at[jnp.arange(n)[:, None], top_i].set(top_p)
        h = jax.nn.relu(jnp.einsum('nd,edh->neh', xt, eW1) + eb1)
        ye = jnp.einsum('neh,ehd->ned', h, eW2) + eb2
        routed = jnp.einsum('ned,ne->nd', ye, cw)
        return (shared + routed).reshape(b, l, d)
    x = L0_attn_a_x
    x = x + _L0_attn_a_ref(_layernorm(x, axis=-1), L0_attn_a_cos, L0_attn_a_sin, L0_attn_a_Wq, L0_attn_a_Wk, L0_attn_a_Wv, L0_attn_a_Wb, L0_attn_a_Wa, L0_attn_a_A_log, L0_attn_a_dt_bias, L0_attn_a_conv_q, L0_attn_a_conv_k, L0_attn_a_conv_v, L0_attn_a_Wg, L0_attn_a_rms_weight, L0_attn_a_Wo)
    x = x + _L0_ffn_ref(_layernorm(x, axis=-1), L0_ffn_router_W, L0_ffn_router_b, L0_ffn_sW1, L0_ffn_sb1, L0_ffn_sW2, L0_ffn_sb2, L0_ffn_eW1, L0_ffn_eb1, L0_ffn_eW2, L0_ffn_eb2)
    x = x + _L0_attn_b_ref(_layernorm(x, axis=-1), L0_attn_b_ln_g, L0_attn_b_ln_b, L0_attn_b_Wx, L0_attn_b_Ww, L0_attn_b_bw, L0_attn_b_Wk, L0_attn_b_Wv, L0_attn_b_Wr, L0_attn_b_Wo)
    x = x + _L0_ffn_ref(_layernorm(x, axis=-1), L0_ffn_router_W, L0_ffn_router_b, L0_ffn_sW1, L0_ffn_sb1, L0_ffn_sW2, L0_ffn_sb2, L0_ffn_eW1, L0_ffn_eb1, L0_ffn_eW2, L0_ffn_eb2)
    return x

_drawn_inputs = setup_inputs


def setup_inputs(seed=0):
    import zlib

    import numpy as np

    out = dict(_drawn_inputs(seed))
    spreads = {'L0_attn_a_rms_weight': (1.0, 0.6),
     'L0_attn_b_ln_g': (1.0, 0.2),
     'L0_attn_b_ln_b': (0.0, 0.1),
     'L0_attn_b_bw': (0.0, 0.1),
     'L0_ffn_router_b': (0.0, 0.559),
     'L0_ffn_sb1': (0.0, 0.34),
     'L0_ffn_sb2': (0.0, 0.1),
     'L0_ffn_eb1': (0.0, 0.8),
     'L0_ffn_eb2': (0.0, 0.352)}
    factors = {'L0_attn_a_Wb': 8.0,
     'L0_attn_a_Wa': 8.0,
     'L0_attn_a_A_log': 3.308,
     'L0_attn_a_dt_bias': 8.0,
     'L0_ffn_eW1': 7.968,
     'L0_ffn_eW2': 5.836}
    for name, (base, spread) in spreads.items():
        noise = np.random.default_rng([zlib.crc32(name.encode()), seed]).standard_normal(out[name].shape)
        drawn = base * np.exp(spread * noise) if base else spread * noise
        out[name] = jnp.asarray(drawn.astype(out[name].dtype))
    for name, factor in factors.items():
        out[name] = (out[name] * factor).astype(out[name].dtype)
    return out
```

```python
import math
from contextlib import ExitStack

import numpy as np
import concourse.bass as bass
from concourse import mybir

F32 = mybir.dt.float32
BF16 = mybir.dt.bfloat16
F32R = mybir.dt.float32r
ALU = mybir.AluOpType
ACT = mybir.ActivationFunctionType
AX = mybir.AxisListType

B, T, D = 4, 1024, 128
NTOK = B * T
NH, NHH, TAPS = 8, 3, 4
TC = 32
R = NHH * TC
NCC = 2
SPAN = NCC * TC
U = B * NCC
KSTEPS = T // SPAN
PAD = TAPS - 1
LEVELS = 5
CREDIT = 2
TILE = 512
NT = NTOK // TILE
E_N, TOPK = 15, 3


class Shared:

    dram = h = None


def done(n):
    return n + 1 + CREDIT


def constants():
    i, t = np.divmod(np.arange(R), TC)
    tau = NHH * t + i
    later = tau[None, :] > tau[:, None]
    tri = np.arange(TC)[None, :] >= t[:, None]
    mask4 = np.concatenate([later, tri], axis=1).astype(np.float32)
    lev = []
    for l in range(LEVELS):
        s = 1 << l
        same = (tau[:, None] // (2 * s)) == (tau[None, :] // (2 * s))
        lev.append(-(same & (tau[:, None] // s > tau[None, :] // s)).astype(np.float32))
    j = np.arange(TC)
    after_m = (j[:, None] > t[None, :]).astype(np.float32)
    upto = (j[:, None] <= j[None, :]).astype(np.float32)
    c = {
        "c_ident": np.eye(128, dtype=np.float32),
        "c_mean": np.full((128, 128), 1.0 / D, np.float32),
        "c_mask4": mask4,
        "c_lev": np.concatenate(lev, axis=1),
        "c_after": after_m,
        "c_upto": upto,
    }
    sel = np.zeros((96, E_N, 128), np.float32)
    for part in range(3):
        for e in range(E_N):
            sel[32 * part + e, e] = 1
    c["c_sel"] = sel.reshape(96, -1)
    a = np.arange(128)
    bm = [np.eye(128, dtype=np.float32)]
    for l in range(5):
        s = 1 << l
        same = (a[:, None] // (2 * s)) == (a[None, :] // (2 * s))
        bm.append((same & (a[:, None] // s < a[None, :] // s)).astype(np.float32))
    c["c_bmasks"] = np.stack(bm, 1).reshape(128, -1)
    c["c_bdiag"] = (a[:, None] // 64 == a[None, :] // 64).astype(np.float32)
    return c


def semaphores(nc, ctx):
    held = []

    def sem(name):
        held.append(nc.alloc_semaphore(name))
        return held[-1]

    def end():
        nc.clear_and_free_semaphores(held)
        nc.all_engine_barrier()

    ctx.callback(end)
    return sem


def load_rows(nc, g):
    with ExitStack() as ctx:
        new_sem = semaphores(nc, ctx)
        xin = ctx.enter_context(nc.sbuf_tensor("xin", [128, NTOK // 128, D], F32))
        ps = [ctx.enter_context(nc.psum_tensor(f"ld{i}", [128, TILE], F32)) for i in range(4)]
        loaded, cst, turned, kept = (new_sem(n) for n in ("ld_x", "ld_cst", "ld_turned", "ld_kept"))
        block = ctx.enter_context(nc.Block())
        src = g.dram["x"].rearrange("b t d -> (b t) d").rearrange("(j p) d -> p j d", p=128)

        @block.sync
        def _(sp):
            n = 0
            for name, dst in g.const_loads:
                sp.dma_start(dst, g.dram[name]).then_inc(cst, 16)
                n += 16
            sp.wait_ge(cst, n)
            for q in range(4):
                sp.dma_start(xin[:, 8 * q:8 * q + 8, :], src[:, 8 * q:8 * q + 8, :]).then_inc(loaded, 16)
                sp.wait_ge(loaded, 16 * (q + 1))

        @block.tensor
        def _(pe):
            pe.wait_ge(cst, 16 * len(g.const_loads))
            for i in range(NT):
                pe.wait_ge(loaded, 16 * (i // 2 + 1))
                if i >= 4:
                    pe.wait_ge(kept, i - 3)
                for a in range(4):
                    last = nc.tensor.transpose(ps[i % 4][:, 128 * a:128 * a + 128], xin[:, 4 * i + a, :], g.ident[:, :])
                last.then_inc(turned, 1)

        @block.scalar
        def _(act):
            for i in range(NT):
                act.wait_ge(turned, i + 1)
                nc.scalar.activation(g.xT[:, i // 2, TILE * (i % 2):TILE * (i % 2 + 1)], ps[i % 4][:, :], ACT.Copy).then_inc(kept, 1)


def store_rows(nc, g):
    with ExitStack() as ctx:
        new_sem = semaphores(nc, ctx)
        xo = ctx.enter_context(nc.sbuf_tensor("xout", [128, NTOK // 128, D], F32))
        ps = [ctx.enter_context(nc.psum_tensor(f"st{i}", [128, TILE], F32)) for i in range(4)]
        turned, kept, stored = (new_sem(n) for n in ("st_turned", "st_kept", "st_stored"))
        block = ctx.enter_context(nc.Block())
        dst = g.dram["out"].rearrange("b t d -> (b t) d").rearrange("(j p) d -> p j d", p=128)

        @block.tensor
        def _(pe):
            for i in range(NT):
                if i >= 4:
                    pe.wait_ge(kept, i - 3)
                for a in range(4):
                    o = TILE * (i % 2) + 128 * a
                    last = nc.tensor.transpose(ps[i % 4][:, 128 * a:128 * a + 128], g.xT[:, i // 2, o:o + 128], g.ident[:, :])
                last.then_inc(turned, 1)

        @block.scalar
        def _(act):
            for i in range(NT):
                act.wait_ge(turned, i + 1)
                nc.scalar.activation(xo[:, 4 * i:4 * i + 4, :], ps[i % 4][:, :].rearrange("p (a d) -> p a d", a=4), ACT.Copy).then_inc(kept, 1)

        @block.sync
        def _(sp):
            for q in range(4):
                sp.wait_ge(kept, 2 * q + 2)
                sp.dma_start(dst[:, 8 * q:8 * q + 8, :], xo[:, 8 * q:8 * q + 8, :]).then_inc(stored, 16)
            sp.wait_ge(stored, 64)


def layernorm(nc, g, tag, src, affine=None):
    with ExitStack() as ctx:
        new_sem = semaphores(nc, ctx)
        sb = lambda n, s: ctx.enter_context(nc.sbuf_tensor(tag + n, s, F32))
        mean = [ctx.enter_context(nc.psum_tensor(f"{tag}mean{i}", [128, TILE], F32)) for i in range(2)]
        var = [ctx.enter_context(nc.psum_tensor(f"{tag}var{i}", [128, TILE], F32)) for i in range(2)]
        xc = sb("xc", [128, 2, TILE])
        sq = sb("sq", [128, 2, TILE])
        rs = sb("rs", [128, 2, TILE])
        sem = lambda n: new_sem(tag + n)
        meaned, centred, squared, varied, rooted, scaled, normed = (sem(n) for n in ("meaned", "centred", "squared", "varied", "rooted", "scaled", "normed"))
        eps = ctx.enter_context(nc.sbuf_tensor(tag + "eps", [128, 1], F32))
        eps_ready = sem("eps_ready")
        block = ctx.enter_context(nc.Block())

        @block.tensor
        def _(pe):
            def mean_of(i):
                if i >= 2:
                    pe.wait_ge(centred, i - 1)
                nc.tensor.matmul(mean[i % 2][:, :], g.mean[:, :], src(i), start=True, stop=True).then_inc(meaned, 1)
            mean_of(0)
            for i in range(NT):
                if i + 1 < NT:
                    mean_of(i + 1)
                pe.wait_ge(squared, i + 1)
                if i >= 2:
                    pe.wait_ge(rooted, i - 1)
                nc.tensor.matmul(var[i % 2][:, :], g.mean[:, :], sq[:, i % 2, :], start=True, stop=True).then_inc(varied, 1)

        @block.scalar
        def _(act):
            act.wait_ge(eps_ready, 1)

            def square(i):
                act.wait_ge(centred, i + 1)
                if i >= 2:
                    act.wait_ge(varied, i - 1)
                nc.scalar.activation(sq[:, i % 2, :], xc[:, i % 2, :], ACT.Square).then_inc(squared, 1)
            square(0)
            for i in range(NT):
                if i + 1 < NT:
                    square(i + 1)
                act.wait_ge(varied, i + 1)
                if i >= 2:
                    act.wait_ge(normed, i - 1)
                nc.scalar.activation(rs[:, i % 2, :], var[i % 2][:, :], ACT.Sqrt, bias=eps[:, :]).then_inc(rooted, 1)

        @block.vector
        def _(dve):
            def centre(i):
                dve.wait_ge(meaned, i + 1)
                if i >= 2:
                    dve.wait_ge(squared, i - 1)
                    dve.wait_ge(normed, i - 1)
                nc.vector.tensor_tensor(xc[:, i % 2, :], src(i), mean[i % 2][:, :], ALU.subtract).then_inc(centred, 1)
            nc.vector.memset(eps[:, :], 1e-5).then_inc(eps_ready, 1)
            centre(0)
            for i in range(NT):
                if i + 1 < NT:
                    centre(i + 1)
                dve.wait_ge(rooted, i + 1)
                nc.vector.reciprocal(rs[:, i % 2, :], rs[:, i % 2, :]).then_inc(scaled, 1)
                dve.wait_ge(scaled, i + 1)
                dst = g.xn[:, i // 2, PAD + TILE * (i % 2):PAD + TILE * (i % 2 + 1)]
                if affine is None:
                    nc.vector.tensor_tensor(dst, xc[:, i % 2, :], rs[:, i % 2, :], ALU.mult).then_inc(normed, 1)
                else:
                    nc.vector.tensor_tensor(rs[:, i % 2, :], xc[:, i % 2, :], rs[:, i % 2, :], ALU.mult).then_inc(normed, 1)
                    dve.wait_ge(normed, i + 1)
                    nc.vector.tensor_scalar(dst, rs[:, i % 2, :], affine[0], affine[1], ALU.mult, ALU.add)


def decay_gates(nc, g):
    with ExitStack() as ctx:
        new_sem = semaphores(nc, ctx)
        sb = lambda n, s: ctx.enter_context(nc.sbuf_tensor(n, s, F32))
        wba = sb("wba", [128, 2, 32])
        bg = sb("bg", [32, 2, NTOK])
        turned = sb("bg_turned", [32, 2, NTOK])
        small = sb("small", [32, 3, NH])
        z, m, e, s, s2, p = (sb("sp_" + n, [32, NTOK // TC, NH]) for n in ("z", "m", "e", "s", "s2", "p"))
        ps = [[ctx.enter_context(nc.psum_tensor(f"bg{i}{j}", [32, TILE], F32)) for j in range(2)] for i in range(2)]
        sem = new_sem
        w_in, w_zero, mm, kept, chain, ex, al = (sem(n) for n in ("bg_w", "bg_zero", "bg_mm", "bg_kept", "bg_chain", "bg_exp", "bg_alog"))
        block = ctx.enter_context(nc.Block())

        @block.sync
        def _(sp):
            sp.wait_ge(w_zero, 1)
            sp.dma_start(wba[:, 0, 0:NHH * NH], g.dram["Wb"]).then_inc(w_in, 16)
            sp.dma_start(wba[:, 1, 0:NH], g.dram["Wa"]).then_inc(w_in, 16)
            sp.dma_start(small[:, 0, :], g.dram["dt_bias"].partition_broadcast(32)).then_inc(w_in, 16)
            sp.dma_start(small[:, 1, :], g.dram["A_log"].partition_broadcast(32)).then_inc(w_in, 16)

        @block.tensor
        def _(pe):
            pe.wait_ge(w_in, 64)
            for i in range(NT):
                if i >= 2:
                    pe.wait_ge(kept, i - 1)
                rhs = g.xn[:, i // 2, PAD + TILE * (i % 2):PAD + TILE * (i % 2 + 1)]
                for j in range(2):
                    last = nc.tensor.matmul(ps[j][i % 2][:, :], wba[:, j, :], rhs, start=True, stop=True)
                last.then_inc(mm, 1)

        @block.scalar
        def _(act):
            for i in range(NT):
                act.wait_ge(mm, i + 1)
                nc.scalar.activation(bg[:, 0, TILE * i:TILE * (i + 1)], ps[0][i % 2][:, :], ACT.Sigmoid)
                nc.scalar.activation(bg[:, 1, TILE * i:TILE * (i + 1)], ps[1][i % 2][:, :], ACT.Copy).then_inc(kept, 1)
            act.wait_ge(w_in, 64)
            nc.scalar.activation(small[:, 2, :], small[:, 1, :], ACT.Exp).then_inc(al, 1)
            act.wait_ge(chain, 3)
            nc.scalar.activation(e[:, :, :], e[:, :, :], ACT.Exp).then_inc(ex, 1)

        @block.vector
        def _(dve):
            nc.vector.memset(wba[:, :, :], 0.0).then_inc(w_zero, 1)
            n = [0]

            def link(ins):
                n[0] += 1
                ins.then_inc(chain, 1)
                dve.wait_ge(chain, n[0])

            dve.wait_ge(kept, NT)
            nc.vector.transpose(turned[:, 0, :], bg[:, 0, :])
            link(nc.vector.transpose(turned[:, 1, :], bg[:, 1, :]))
            dve.wait_ge(w_in, 64)
            a = turned[:, 1, :].rearrange("t (k r) -> t k r", r=32)[:, :, 0:NH]
            bias = small[:, 0, :].unsqueeze(1).broadcast_to([32, NTOK // TC, NH])
            link(nc.vector.tensor_tensor(z[:, :, :], a, bias, ALU.add))
            link(nc.vector.scalar_tensor_tensor(e[:, :, :], z[:, :, :], -1.0, z[:, :, :], ALU.mult, ALU.min))
            for i in range(NHH):
                bt = turned[:, 0, :].rearrange("t (k r) -> t r k", r=32)[:, NH * i:NH * (i + 1), :]
                nc.vector.tensor_scalar(g.beta[TC * i:TC * (i + 1), :, :], bt, 2.0, None, ALU.mult)
            link(nc.vector.tensor_scalar(m[:, :, :], z[:, :, :], 0.0, None, ALU.max))
            dve.wait_ge(ex, 1)
            link(nc.vector.tensor_scalar(s[:, :, :], e[:, :, :], 2.0, None, ALU.add))
            link(nc.vector.reciprocal(s[:, :, :], s[:, :, :]))
            link(nc.vector.tensor_tensor(s[:, :, :], s[:, :, :], e[:, :, :], ALU.mult))
            link(nc.vector.tensor_tensor(s2[:, :, :], s[:, :, :], s[:, :, :], ALU.mult))
            link(nc.vector.tensor_scalar(p[:, :, :], s2[:, :, :], 2.0 / 17, 2.0 / 15, ALU.mult, ALU.add))
            for c in (13, 11, 9, 7, 5, 3, 1):
                link(nc.vector.tensor_tensor(p[:, :, :], p[:, :, :], s2[:, :, :], ALU.mult))
                link(nc.vector.tensor_scalar(p[:, :, :], p[:, :, :], 2.0 / c, None, ALU.add))
            link(nc.vector.tensor_tensor(p[:, :, :], p[:, :, :], s[:, :, :], ALU.mult))
            link(nc.vector.tensor_tensor(p[:, :, :], p[:, :, :], m[:, :, :], ALU.add))
            dve.wait_ge(al, 1)
            ea = small[:, 2, :].unsqueeze(1).broadcast_to([32, NTOK // TC, NH])
            nc.vector.scalar_tensor_tensor(g.gt[:, :, :], p[:, :, :], -1.0, ea, ALU.mult, ALU.mult)


def delta_attention(nc, g):
    with ExitStack() as ctx:
        new_sem = semaphores(nc, ctx)
        sb = lambda n, s, dt=F32: ctx.enter_context(nc.sbuf_tensor(n, s, dt))
        stage_w = sb("stage_w", [128, 9, 128])
        stage_c = sb("stage_c", [128, 7, 128, TAPS])
        wt = sb("wt", [128, 7, TAPS, 128])
        wgo = sb("wgo", [128, 2, 128])
        rmsw = sb("rmsw", [128, 1])
        edec = sb("edec", [R, B, T])
        gdec = sb("gdec", [128, B, T])
        kqs = sb("kqs", [128, 4, U, 4, TC])
        kq = [kqs[:, i] for i in range(2)]
        vt = [sb(f"vt{i}", [128, U, NHH, TC]) for i in range(2)]
        gate = [sb(f"gate{i}", [128, U, TC]) for i in range(2)]
        kqg = [kqs[:, 2 + i] for i in range(2)]
        gm = kqs[0:TC].rearrange("p a u i t -> p (a u i) t")
        sq = sb("sq", [128, U, NHH, TC])
        sqq = sb("sqq", [128, NCC, B, TC])
        ss = sb("ss", [R, U])
        rk = [sb(f"rk{i}", [R, U]) for i in range(2)]
        rinv = sb("rinv", [R, U])
        step_s = sb("step_s", [R, U])
        q2 = [sb(f"q2{i}", [128, NCC]) for i in range(2)]
        es = [sb(f"es{i}", [R, U, TC]) for i in range(2)]
        es4 = sb("es4", [R, U, 4, TC])
        krow = [sb(f"krow{i}", [R, U, 128]) for i in range(2)]
        vrow = [sb(f"vrow{i}", [R, U, 128]) for i in range(2)]
        ap = [sb(f"ap{i}", [R, U, 128]) for i in range(2)]
        X = sb("X", [R, U, R])
        Y = sb("Y", [R, U, R])
        Z = sb("Z", [R, U, R])
        ix = sb("ix", [R, U, R])
        ar = sb("ar", [R, U, R], F32R)
        Xr = sb("Xr", [R, U, R], F32R)
        Yr = sb("Yr", [R, U, R], F32R)
        Zr = sb("Zr", [R, U, R], F32R)
        ident_r = sb("ident_r", [R, R], F32R)
        yf = [sb(f"yf{i}", [R, U, R]) for i in range(2)]
        S = sb("S", [128, B, 128])
        rhs = sb("rhs", [R, B, 128])
        ws = sb("ws", [R, B, 128])
        mo = sb("mo", [128, NCC])
        fo = sb("fo", [128, NCC])
        osq = sb("osq", [128, 128])
        osb = sb("osb", [128, NCC, 128])
        og = sb("og", [128, NCC, 128])

        PP = [ctx.enter_context(nc.psum_tensor(f"PP{i}", [128, TILE], F32)) for i in range(2)]
        G2 = ctx.enter_context(nc.psum_tensor("G2", [128, 2, TILE], F32))
        L2 = ctx.enter_context(nc.psum_tensor("L2", [128, 2, TILE], F32))
        RA = ctx.enter_context(nc.psum_tensor("RA", [128, TILE], F32))
        RB = ctx.enter_context(nc.psum_tensor("RB", [128, TILE], F32))
        side = L2[:, 1, 384:512]

        evs = []

        def ev(name):
            s = new_sem(name)
            evs.append(s)
            return s

        proj = [ev(f"proj_mm{q}") for q in range(4)]
        silu = [ev(f"silu{q}") for q in range(4)]
        rk_ev, ss_ev, sq_ev, ss_mm, sc_ev, rinv_ev, s_ev, es_ev, es4_ev = (ev(n) for n in ("rk_ready", "ss_ready", "sq_ready", "ss_mm", "norms_read", "rinv_ready", "step_s_ready", "es_ready", "es4_ready"))
        ktr_mm, vtr_mm, gram_mm, kr_ev, vr_ev, ap_ev, ar_ev, kqg_ev = (ev(n) for n in ("ktr_mm", "vtr_mm", "gram_mm", "krow_ready", "vrow_ready", "ap_ready", "ar_ready", "kqg_ready"))
        z_mm, z_ev, x_mm, x_ev, y_mm, y_ev = ([ev(f"{n}{l}") for l in range(LEVELS)] for n in ("z_mm", "z_ready", "x_mm", "x_ready", "y_mm", "y_ready"))
        m_mm, ix_ev, r_ev = ([ev(f"{n}{l}") for l in range(2)] for n in ("m_mm", "ix_ready", "resid_ready"))
        xn_mm, yn_mm, xn_ev, yn_ev, yf_mm, yf_ev = (ev(n) for n in ("xn_mm", "yn_mm", "xn_ready", "yn_ready", "yf_mm", "yf_ready"))
        ks_mm, rhs_ev, w_mm, w_ev, s_mm, o_mm, sup_ev, mo_ev, fs_ev, fo_ev, osb_ev, ot_mm, og_ev, out_mm, acc_ev = (
            [ev(f"{n}{c}") for c in range(NCC)] for n in ("ks_mm", "rhs_ready", "w_mm", "w_ready", "snew_mm", "o_mm", "state_ready", "osum_ready", "osum_eps_ready", "oscale_ready", "o_ready", "ot_mm", "og_ready", "out_mm", "acc_ready"))
        staged, wt_ready, gm_ready, zero_ready, rms_ready, identr_ready = (new_sem(n) for n in ("staged", "wt_ready", "gm_ready", "state_zeroed", "rms_ready", "identr_ready"))
        e_mm, g_mm, e_ex, g_ex = (new_sem(n) for n in ("e_mm", "g_mm", "e_exp", "g_exp"))

        with nc.Block() as b0:
            @b0.gpsimd
            def _(pool):
                for s in evs:
                    pool.sem_inc(s, CREDIT)

        NDMA = 7
        block = ctx.enter_context(nc.Block())
        LAST = KSTEPS - 1

        def weave(order, segs, base, k, par, now):
            shift = {"P": 1, "I": 0, "R": -1}
            for part, name, *args in order:
                if part in now and name in segs:
                    d = shift[part]
                    segs[name](base + k + d, k + d, (par + d) % 2, now, *args)

        def program(eng, order, segs, prep):
            with eng.Fori(0, NH) as h:
                prep(h)
                base = h * KSTEPS
                weave(order, segs, base, -1, 1, "P")
                weave(order, segs, base, 0, 0, "PI")
                with eng.Fori(0, (KSTEPS - 2) // 2) as j:
                    weave(order, segs, base, j * 2 + 1, 1, "PIR")
                    weave(order, segs, base, j * 2 + 2, 0, "PIR")
                weave(order, segs, base, LAST, LAST % 2, "IR")
                weave(order, segs, base, LAST + 1, (LAST + 1) % 2, "R")

        ORDER = [
            ("I", "sq"), ("R", "ks", 0), ("I", "ss"), ("I", "sc"), ("I", "rk"), ("I", "es4"), ("I", "ktr"), ("I", "kr"), ("R", "rhs", 0), ("R", "w", 0), ("R", "wev", 0),
            ("I", "kqg"),
            ("I", "vtr"), ("I", "vr"), ("R", "so", 0), ("R", "sup", 0), ("I", "gram"), ("I", "ap"), ("I", "ar"), ("R", "mo", 0), ("R", "fo", 0), ("R", "osb", 0),
            ("P", "pt", 0, 0), ("R", "ks", 1), ("R", "rhs", 1),
            ("R", "ot", 0), ("I", "z", 0), ("I", "zev", 0), ("R", "og", 0), ("R", "w", 1), ("R", "wev", 1), ("P", "pt", 0, 1), ("P", "silu", 0),
            ("I", "x", 0), ("I", "xev", 0), ("I", "y", 0), ("I", "yev", 0), ("R", "so", 1), ("R", "sup", 1), ("R", "mo", 1), ("R", "fo", 1), ("R", "osb", 1),
            ("R", "out", 0), ("I", "z", 1), ("I", "zev", 1), ("R", "acc", 0), ("P", "pt", 1, 0),
            ("I", "x", 1), ("I", "xev", 1), ("I", "y", 1), ("I", "yev", 1),
            ("R", "ot", 1), ("I", "z", 2), ("I", "zev", 2), ("R", "og", 1), ("P", "pt", 1, 1), ("P", "silu", 1),
            ("I", "x", 2), ("I", "xev", 2), ("I", "y", 2), ("I", "yev", 2),
            ("R", "out", 1), ("I", "z", 3), ("I", "zev", 3), ("R", "acc", 1), ("P", "pt", 2, 0),
            ("I", "x", 3), ("I", "xev", 3), ("I", "y", 3), ("I", "yev", 3),
            ("I", "z", 4), ("I", "zev", 4), ("P", "pt", 2, 1), ("P", "silu", 2),
            ("I", "x", 4), ("I", "xev", 4), ("I", "ix", 0), ("I", "y", 4), ("I", "yev", 4), ("I", "m", 0), ("I", "res", 0), ("P", "pt", 3, 0),
            ("I", "xn"), ("I", "xnev"), ("I", "ix", 1), ("I", "yn"), ("I", "ynev"), ("I", "m", 1), ("I", "res", 1), ("P", "pt", 3, 1), ("P", "silu", 3),
            ("I", "yf"), ("I", "yfev"),
        ]

        def flat2(ps):
            return ps[0:R, :, 0:4 * R].rearrange("p a (c n) -> p a c n", n=R)

        def units(t):
            return t[:, :, :].rearrange("p (a c) n -> p a c n", c=4)

        def slot(ps, u, n):
            return ps[0:R, u // 4, (u % 4) * n:(u % 4 + 1) * n]

        @block.sync
        def _(sp):
            with sp.Fori(0, NH) as h:
                sp.wait_ge(wt_ready, h + 1)
                col = lambda w, n: g.dram[w].rearrange("d (i x c) -> d x i c", x=NH, c=128)[:, bass.ds(h, 1), :, :]
                sp.dma_start(stage_w[:, 0:3, :].unsqueeze(1), col("Wk", 3)).then_inc(staged, 16)
                sp.dma_start(stage_w[:, 3:4, :].unsqueeze(1), col("Wq", 1)).then_inc(staged, 16)
                sp.dma_start(stage_w[:, 4:7, :].unsqueeze(1), col("Wv", 3)).then_inc(staged, 16)
                sp.dma_start(stage_w[:, 7:8, :].unsqueeze(1), col("Wg", 1)).then_inc(staged, 16)
                sp.dma_start(stage_w[:, 8, :], g.dram["Wo"][bass.ds(h * 128, 128), :]).then_inc(staged, 16)
                tap = lambda w: g.dram[w].rearrange("(i x c) k -> x i (c k)", x=NH, c=128)
                for i in range(3):
                    sp.dma_start(stage_c[:, i, :, :], tap("conv_k")[bass.ds(h, 1), i, :].rearrange("a n -> (a n)").partition_broadcast(128)).then_inc(staged, 16)
                    sp.dma_start(stage_c[:, 4 + i, :, :], tap("conv_v")[bass.ds(h, 1), i, :].rearrange("a n -> (a n)").partition_broadcast(128)).then_inc(staged, 16)
                sp.dma_start(stage_c[:, 3, :, :], tap("conv_q")[bass.ds(h, 1), 0, :].rearrange("a n -> (a n)").partition_broadcast(128)).then_inc(staged, 16)

        @block.gpsimd
        def _(pool):
            def prep(h):
                pool.wait_ge(g_ex, h * 4 + 4)

            def s_sq(N, k, par, now):
                pool.wait_ge(silu[0], done(N))
                pool.wait_ge(silu[1], done(N))
                pool.wait_ge(ss_mm, done(N - 1))
                qv = kq[par][:, :, 3, :].rearrange("p (b c) t -> p b c t", c=NCC)
                nc.gpsimd.tensor_tensor(sqq[:, :, :, :].rearrange("p c b t -> p b c t"), qv, qv, ALU.mult)
                nc.gpsimd.tensor_tensor(sq[:, :, :, :], kq[par][:, :, 0:3, :], kq[par][:, :, 0:3, :], ALU.mult).then_inc(sq_ev, 1)

            def s_es4(N, k, par, now):
                pool.wait_ge(es_ev, done(N))
                pool.wait_ge(ap_ev, done(N - 1))
                nc.gpsimd.tensor_tensor(es4[:, :, :, :], es[par][:, :, :].unsqueeze(2).broadcast_to([R, U, 4, TC]),
                                        g.mask4[:, :].rearrange("p (i t) -> p i t", i=4).unsqueeze(1).broadcast_to([R, U, 4, TC]), ALU.mult).then_inc(es4_ev, 1)

            def s_kqg(N, k, par, now):
                pool.wait_ge(o_mm[1], done(N - 2))
                kv = kq[par][:, :, :, :].rearrange("p (b c) i t -> p b c i t", c=NCC)
                ov = kqg[par][:, :, :, :].rearrange("p (b c) i t -> p b c i t", c=NCC)
                for cc in range(NCC):
                    d = gdec[:, :, bass.ds(k * SPAN + cc * TC, TC)].unsqueeze(2).broadcast_to([128, B, 4, TC])
                    last = nc.gpsimd.tensor_tensor(ov[:, :, cc], kv[:, :, cc], d, ALU.mult)
                last.then_inc(kqg_ev, 1)

            def s_rk(N, k, par, now):
                pool.wait_ge(ss_ev, done(N))
                pool.wait_ge(vr_ev, done(N - 2))
                nc.gpsimd.tensor_tensor(rk[par][:, :], ss[:, :], g.half[0:R, :], ALU.pow).then_inc(rk_ev, 1)

            def s_fo(N, k, par, now, cc):
                pool.wait_ge(mo_ev[cc], done(N))
                pool.wait_ge(osb_ev[cc], done(N - 1))
                nc.gpsimd.tensor_tensor(fo[:, cc:cc + 1], mo[:, cc:cc + 1], q2[par][:, cc:cc + 1], ALU.add).then_inc(fs_ev[cc], 1)
                pool.wait_ge(fs_ev[cc], done(N))
                nc.gpsimd.tensor_tensor(fo[:, cc:cc + 1], fo[:, cc:cc + 1], g.minus_half[:, 0:1], ALU.pow).then_inc(fo_ev[cc], 1)

            def s_ix(N, k, par, now, n):
                pool.wait_ge(x_ev[LEVELS - 1] if n == 0 else xn_ev, done(N))
                pool.wait_ge(r_ev[1], done(N - 1)) if n == 0 else pool.wait_ge(r_ev[0], done(N))
                nc.gpsimd.tensor_tensor(ix[:, :, :], g.ident[0:R, 0:R].unsqueeze(1).broadcast_to([R, U, R]), X[:, :, :], ALU.subtract).then_inc(ix_ev[n], 1)

            program(pool, ORDER, {"sq": s_sq, "rk": s_rk, "fo": s_fo, "es4": s_es4, "kqg": s_kqg, "ix": s_ix}, prep)

        @block.scalar
        def _(act):
            def prep(h):
                for i in range(4):
                    act.wait_ge(e_mm, h * 4 + i + 1)
                    nc.scalar.activation(edec[:, i, :].rearrange("p (a n) -> p a n", a=2), G2[0:R, :, :], ACT.Exp).then_inc(e_ex, 1)
                    act.wait_ge(g_mm, h * 4 + i + 1)
                    nc.scalar.activation(gdec[:, i, :].rearrange("p (a n) -> p a n", a=2), L2[:, :, :], ACT.Exp).then_inc(g_ex, 1)

            def s_silu(N, k, par, now, q):
                act.wait_ge(proj[q], done(N))
                src = PP[q % 2][:, :].rearrange("p (a u t) -> p a u t", a=2, t=TC)
                if q == 0:
                    act.wait_ge(kqg_ev, done(N - 2))
                    nc.scalar.activation(kq[par][:, :, 0:2, :].rearrange("p u i t -> p i u t"), src, ACT.Silu).then_inc(silu[q], 1)
                elif q == 1:
                    nc.scalar.activation(kq[par][:, :, 2:4, :].rearrange("p u i t -> p i u t"), src, ACT.Silu).then_inc(silu[q], 1)
                elif q == 2:
                    act.wait_ge(vtr_mm, done(N - 2))
                    nc.scalar.activation(vt[par][:, :, 0:2, :].rearrange("p u i t -> p i u t"), src, ACT.Silu).then_inc(silu[q], 1)
                else:
                    nc.scalar.activation(vt[par][:, :, 2, :], src[:, 0], ACT.Silu)
                    act.wait_ge(og_ev[1], done(N - 2))
                    nc.scalar.activation(gate[par][:, :, :], src[:, 1], ACT.Silu).then_inc(silu[q], 1)

            def s_xev(N, k, par, now, l):
                act.wait_ge(x_mm[l], done(N))
                if l == LEVELS - 1:
                    act.wait_ge(ix_ev[1], done(N - 1))
                nc.scalar.activation(units(X if l == LEVELS - 1 else Xr), flat2(L2), ACT.Copy).then_inc(x_ev[l], 1)

            def s_ar(N, k, par, now):
                act.wait_ge(ap_ev, done(N))
                act.wait_ge(z_mm[LEVELS - 1], done(N - 1))
                nc.scalar.activation(ar[:, :, :], ap[par][:, :, 0:R], ACT.Copy).then_inc(ar_ev, 1)

            def s_wev(N, k, par, now, cc):
                act.wait_ge(w_mm[cc], done(N))
                nc.scalar.activation(ws[:, :, :], RB[0:R, :].rearrange("p (b n) -> p b n", b=B), ACT.Copy).then_inc(w_ev[cc], 1)

            def s_mo(N, k, par, now, cc):
                act.wait_ge(o_mm[cc], done(N))
                act.wait_ge(fo_ev[1 - cc], done(N) if cc else done(N - 1))
                nc.scalar.activation(osq[:, :], RB[:, 0:128], ACT.Square, accum_out=mo[:, cc:cc + 1]).then_inc(mo_ev[cc], 1)

            program(act, ORDER, {"silu": s_silu, "ar": s_ar, "xev": s_xev, "wev": s_wev, "mo": s_mo}, prep)

        @block.vector
        def _(dve):
            dve.wait_ge(g.rms_sem, 16)
            nc.vector.tensor_scalar(rmsw[:, :], g.rms_in[:, :], math.sqrt(128.0), None, ALU.mult).then_inc(rms_ready, 1)
            dve.wait_ge(rms_ready, 1)
            nc.vector.tensor_copy(ident_r[:, :], g.ident[0:R, 0:R]).then_inc(identr_ready, 1)
            nc.vector.memset(stage_w[:, 0, 0:1], 0.0).then_inc(wt_ready, 1)

            def prep(h):
                dve.wait_ge(staged, (h + 1) * (16 * (5 + 7)))
                dve.wait_ge(out_mm[1], done(h * KSTEPS - 1))
                nc.vector.tensor_tensor(wt[:, :, :, :], stage_w[:, 0:7, :].unsqueeze(2).broadcast_to([128, 7, TAPS, 128]),
                                        stage_c[:, :, :, :].rearrange("p a c k -> p a k c"), ALU.mult)
                nc.vector.tensor_copy(wgo[:, :, :], stage_w[:, 7:9, :]).then_inc(wt_ready, 1)
                nc.vector.memset(S[:, :, :], 0.0).then_inc(zero_ready, 1)
                nc.vector.tensor_tensor(gm[:, :, :], g.gt[:, :, bass.ds(h, 1)].broadcast_to([TC, NTOK // TC, TC]),
                                        g.upto[:, :].unsqueeze(1).broadcast_to([TC, NTOK // TC, TC]), ALU.mult).then_inc(gm_ready, 1)
                dve.wait_ge(g_ex, h * 4 + 4)

            cur = Shared()

            def prep_h(h):
                cur.h = h
                prep(h)

            def s_sc(N, k, par, now):
                dve.wait_ge(ss_mm, done(N))
                dve.wait_ge(vr_ev, done(N - 1))
                dve.wait_ge(rk_ev, done(N - 1))
                nc.vector.tensor_scalar(ss[:, :], L2[0:R, 0, 384:384 + U], 1e-6, None, ALU.add).then_inc(ss_ev, 1)
                dve.wait_ge(ss_ev, done(N))
                nc.vector.reciprocal(rinv[:, :], ss[:, :]).then_inc(rinv_ev, 1)
                nc.vector.tensor_scalar(q2[par][:, :], L2[:, 0, 392:392 + NCC], 1e-5 * 128 * 128, 1e-6 * 1e-5 * 128 * 128, ALU.mult, ALU.add).then_inc(sc_ev, 1)
                dve.wait_ge(rinv_ev, done(N))
                nc.vector.tensor_tensor(step_s[:, :].rearrange("p (b c) -> p b c", c=NCC), rinv[:, :].rearrange("p (b c) -> p b c", c=NCC),
                                        g.beta[:, bass.ds(cur.h, 1), :].rearrange("p x (b c) -> p (x b) c", b=B)[:, :, bass.ds(k * NCC, NCC)], ALU.mult).then_inc(s_ev, 1)
                dve.wait_ge(s_ev, done(N))
                nc.vector.tensor_tensor(es[par][:, :, :].rearrange("p (b c) t -> p b c t", c=NCC),
                                        edec[:, :, bass.ds(k * SPAN, SPAN)].rearrange("p b (c t) -> p b c t", c=NCC),
                                        step_s[:, :].rearrange("p (b c) -> p b c", c=NCC).unsqueeze(3).broadcast_to([R, B, NCC, TC]), ALU.mult).then_inc(es_ev, 1)

            def s_kr(N, k, par, now):
                dve.wait_ge(ktr_mm, done(N))
                dve.wait_ge(es_ev, done(N))
                dve.wait_ge(s_mm[1], done(N - 2))
                nc.vector.tensor_tensor(krow[par][:, :, :], G2[0:R, :, :].rearrange("p a (c n) -> p (a c) n", n=128),
                                        es[par][:, :, TC - 1:TC].broadcast_to([R, U, 128]), ALU.mult).then_inc(kr_ev, 1)

            def s_vr(N, k, par, now):
                dve.wait_ge(vtr_mm, done(N))
                dve.wait_ge(rk_ev, done(N))
                nc.vector.tensor_tensor(vrow[par][:, :, :], L2[0:R, :, :].rearrange("p a (c n) -> p (a c) n", n=128),
                                        rk[par][:, :].unsqueeze(2).broadcast_to([R, U, 128]), ALU.mult).then_inc(vr_ev, 1)

            def s_ap(N, k, par, now):
                dve.wait_ge(gram_mm, done(N))
                dve.wait_ge(es4_ev, done(N))
                dve.wait_ge(o_mm[1], done(N - 2))
                nc.vector.tensor_tensor(ap[par][:, :, :], G2[0:R, :, :].rearrange("p a (c n) -> p (a c) n", n=128),
                                        es4[:, :, :, :].rearrange("p u i t -> p u (i t)"), ALU.mult).then_inc(ap_ev, 1)

            def s_zev(N, k, par, now, l):
                dve.wait_ge(z_mm[l], done(N))
                mask = g.lev[:, l * R:(l + 1) * R].unsqueeze(1).unsqueeze(1).broadcast_to([R, 2, 4, R])
                nc.vector.tensor_tensor(units(Zr), flat2(L2), mask, ALU.mult).then_inc(z_ev[l], 1)

            def s_yev(N, k, par, now, l):
                dve.wait_ge(y_mm[l], done(N))
                old = g.ident[0:R, 0:R].unsqueeze(1).unsqueeze(1).broadcast_to([R, 2, 4, R]) if l == 0 else units(Yr.bitcast(F32))
                nc.vector.tensor_tensor(units(Y if l == LEVELS - 1 else Yr), flat2(G2), old, ALU.add).then_inc(y_ev[l], 1)

            def s_res(N, k, par, now, n):
                dve.wait_ge(m_mm[n], done(N))
                dve.wait_ge(ix_ev[n], done(N))
                nc.vector.tensor_tensor(units(Z), units(ix), flat2(L2), ALU.subtract).then_inc(r_ev[n], 1)

            def s_xnev(N, k, par, now):
                dve.wait_ge(xn_mm, done(N))
                nc.vector.tensor_tensor(units(X), flat2(L2), units(X), ALU.add).then_inc(xn_ev, 1)

            def s_ynev(N, k, par, now):
                dve.wait_ge(yn_mm, done(N))
                nc.vector.tensor_tensor(units(Y), flat2(G2), units(Y), ALU.add).then_inc(yn_ev, 1)

            def s_yfev(N, k, par, now):
                dve.wait_ge(yf_mm, done(N))
                nc.vector.tensor_tensor(units(yf[par]), flat2(G2), units(Y), ALU.add).then_inc(yf_ev, 1)

            def s_rhs(N, k, par, now, cc):
                dve.wait_ge(ks_mm[cc], done(N))
                v = vrow[par][:, :, :].rearrange("p (b c) n -> p b c n", c=NCC)[:, :, cc, :]
                nc.vector.tensor_tensor(rhs[:, :, :], v, RA[0:R, :].rearrange("p (b n) -> p b n", b=B), ALU.subtract).then_inc(rhs_ev[cc], 1)

            def s_sup(N, k, par, now, cc):
                dve.wait_ge(s_mm[cc], done(N))
                dve.wait_ge(o_mm[cc], done(N))
                for b in range(B):
                    last = nc.vector.scalar_tensor_tensor(S[:, b, :], S[:, b, :], gdec[:, b, bass.ds(k * SPAN + cc * TC + TC - 1, 1)],
                                                          RA[:, b * 128:(b + 1) * 128], ALU.mult, ALU.add)
                last.then_inc(sup_ev[cc], 1)

            def s_osb(N, k, par, now, cc):
                dve.wait_ge(fo_ev[cc], done(N))
                nc.vector.tensor_scalar(osb[:, cc, :], RB[:, 0:128], fo[:, cc:cc + 1], None, ALU.mult).then_inc(osb_ev[cc], 1)

            def s_og(N, k, par, now, cc):
                dve.wait_ge(ot_mm[cc], done(N))
                gv = gate[par][:, :, :].rearrange("p (b c) t -> p b c t", c=NCC)[:, :, cc, :]
                nc.vector.scalar_tensor_tensor(og[:, cc, :].rearrange("p (b t) -> p b t", b=B), side.rearrange("p (b t) -> p b t", b=B),
                                               rmsw[:, :], gv, ALU.mult, ALU.mult).then_inc(og_ev[cc], 1)

            def s_acc(N, k, par, now, cc):
                dve.wait_ge(out_mm[cc], done(N))
                x = g.xT[:, :, bass.ds(k * SPAN + cc * TC, TC)]
                nc.vector.tensor_tensor(x, side.rearrange("p (b t) -> p b t", b=B), x, ALU.add).then_inc(acc_ev[cc], 1)

            program(dve, ORDER, {"sc": s_sc, "kr": s_kr, "vr": s_vr, "ap": s_ap, "zev": s_zev, "yev": s_yev, "res": s_res,
                                 "xnev": s_xnev, "ynev": s_ynev, "yfev": s_yfev, "rhs": s_rhs, "sup": s_sup, "osb": s_osb, "og": s_og, "acc": s_acc}, prep_h)

        @block.tensor
        def _(pe):
            mm = nc.tensor.matmul
            pe.wait_ge(identr_ready, 1)

            def prep(h):
                pe.wait_ge(gm_ready, h + 1)
                pe.wait_ge(acc_ev[1], done(h * KSTEPS - 1))
                pe.wait_ge(yf_ev, done(h * KSTEPS - 1))
                for i in range(4):
                    pe.wait_ge(e_ex, h * 4 + i) if i else None
                    for a in range(2):
                        last = mm(G2[0:R, a, :], g.after[:, :], gm[:, bass.ds(32 * i + 16 * a, 16), :], start=True, stop=True)
                    last.then_inc(e_mm, 1)
                    pe.wait_ge(g_ex, h * 4 + i) if i else None
                    for a in range(2):
                        last = mm(L2[:, a, :], g.ones[0:TC, :], gm[:, bass.ds(32 * i + 16 * a, 16), :], start=True, stop=True)
                    last.then_inc(g_mm, 1)
                pe.wait_ge(wt_ready, h + 2)
                pe.wait_ge(zero_ready, h + 1)
                pe.wait_ge(e_ex, h * 4 + 4)
                pe.wait_ge(g_ex, h * 4 + 4)

            def s_pt(N, k, par, now, q, a):
                if a == 0:
                    pe.wait_ge(silu[(q + 2) % 4], done(N - 1) if q < 2 else done(N))
                tile = 2 * q + a
                out = PP[q % 2][:, a * 256:(a + 1) * 256].rearrange("p (b t) -> p b t", b=B)
                if tile < 7:
                    for tap in range(TAPS):
                        last = mm(out, wt[:, tile, tap, :], g.xn[:, :, bass.ds(k * SPAN + tap, SPAN)], start=tap == 0, stop=tap == TAPS - 1)
                else:
                    last = mm(out, wgo[:, 0, :], g.xn[:, :, bass.ds(k * SPAN + PAD, SPAN)], start=True, stop=True)
                if a:
                    last.then_inc(proj[q], 1)

            def s_ktr(N, k, par, now):
                pe.wait_ge(silu[1], done(N))
                pe.wait_ge(yf_ev, done(N - 1))
                for u in range(U):
                    last = nc.tensor.transpose(slot(G2, u, 128), kq[par][:, u, 0:3, :].rearrange("p i t -> p (i t)"), g.ident[:, :])
                last.then_inc(ktr_mm, 1)

            def s_ss(N, k, par, now):
                pe.wait_ge(sq_ev, done(N))
                pe.wait_ge(r_ev[1], done(N - 1))
                if "R" in now:
                    pe.wait_ge(acc_ev[1], done(N - 2))
                for u in range(U):
                    mm(L2[0:R, 0, 384 + u:385 + u], sq[:, u, 0:3, :].rearrange("p i t -> p (i t)"), g.ones[:, 0:1], start=True, stop=True)
                for cc in range(NCC):
                    last = mm(L2[:, 0, 392 + cc:393 + cc], sqq[:, cc, :, :].rearrange("p b t -> p (b t)"), g.ones[:, 0:1], start=True, stop=True)
                last.then_inc(ss_mm, 1)

            def s_vtr(N, k, par, now):
                pe.wait_ge(silu[3], done(N))
                pe.wait_ge(sc_ev, done(N))
                for u in range(U):
                    last = nc.tensor.transpose(slot(L2, u, 128), vt[par][:, u, :, :].rearrange("p i t -> p (i t)"), g.ident[:, :])
                last.then_inc(vtr_mm, 1)

            def s_gram(N, k, par, now):
                pe.wait_ge(kr_ev, done(N))
                for u in range(U):
                    v = kq[par][:, u, :, :].rearrange("p i t -> p (i t)")
                    last = mm(slot(G2, u, 128), v[:, 0:R], v, start=True, stop=True)
                last.then_inc(gram_mm, 1)

            def s_z(N, k, par, now, l):
                pe.wait_ge(ar_ev if l == 0 else x_ev[l - 1], done(N))
                if l == 0:
                    pe.wait_ge(vr_ev, done(N))
                for u in range(U):
                    last = mm(slot(L2, u, R), ar[:, u, :], ident_r[:, :] if l == 0 else Xr[:, u, :], start=True, stop=True)
                last.then_inc(z_mm[l], 1)

            def s_x(N, k, par, now, l):
                pe.wait_ge(z_ev[l], done(N))
                if l:
                    pe.wait_ge(y_ev[l - 1], done(N))
                if "R" in now and l < 4:
                    pe.wait_ge((og_ev[0], acc_ev[0], og_ev[1], acc_ev[1])[l], done(N - 1))
                for u in range(U):
                    mm(slot(L2, u, R), ident_r[:, :], ident_r[:, :] if l == 0 else Xr[:, u, :], start=True, stop=False)
                    last = mm(slot(L2, u, R), ident_r[:, :] if l == 0 else Yr[:, u, :], Zr[:, u, :], start=False, stop=True)
                last.then_inc(x_mm[l], 1)

            def s_y(N, k, par, now, l):
                for u in range(U):
                    last = mm(slot(G2, u, R), Zr[:, u, :], ident_r[:, :] if l == 0 else Yr[:, u, :], start=True, stop=True)
                last.then_inc(y_mm[l], 1)

            def s_m(N, k, par, now, n):
                pe.wait_ge(x_ev[LEVELS - 1] if n == 0 else xn_ev, done(N))
                for u in range(U):
                    last = mm(slot(L2, u, R), ap[par][:, u, 0:R], X[:, u, :], start=True, stop=True)
                last.then_inc(m_mm[n], 1)

            def s_xn(N, k, par, now):
                pe.wait_ge(r_ev[0], done(N))
                pe.wait_ge(y_ev[LEVELS - 1], done(N))
                for u in range(U):
                    last = mm(slot(L2, u, R), Y[:, u, :], Z[:, u, :], start=True, stop=True)
                last.then_inc(xn_mm, 1)

            def s_yn(N, k, par, now):
                for u in range(U):
                    last = mm(slot(G2, u, R), Z[:, u, :], Y[:, u, :], start=True, stop=True)
                last.then_inc(yn_mm, 1)

            def s_yf(N, k, par, now):
                pe.wait_ge(r_ev[1], done(N))
                pe.wait_ge(yn_ev, done(N))
                for u in range(U):
                    last = mm(slot(G2, u, R), Z[:, u, :], Y[:, u, :], start=True, stop=True)
                last.then_inc(yf_mm, 1)

            def s_ks(N, k, par, now, cc):
                pe.wait_ge(kqg_ev, done(N))
                pe.wait_ge(sup_ev[1 - cc], done(N) if cc else done(N - 1))
                for b in range(B):
                    u = b * NCC + cc
                    last = mm(RA[0:R, b * 128:(b + 1) * 128], kqg[par][:, u, 0:3, :].rearrange("p i t -> p (i t)"), S[:, b, :], start=True, stop=True)
                last.then_inc(ks_mm[cc], 1)

            def s_w(N, k, par, now, cc):
                pe.wait_ge(rhs_ev[cc], done(N))
                pe.wait_ge(yf_ev, done(N))
                pe.wait_ge(osb_ev[1 - cc], done(N) if cc else done(N - 1))
                for b in range(B):
                    last = mm(RB[0:R, b * 128:(b + 1) * 128], yf[par][:, b * NCC + cc, :], rhs[:, b, :], start=True, stop=True)
                last.then_inc(w_mm[cc], 1)

            def s_so(N, k, par, now, cc):
                pe.wait_ge(w_ev[cc], done(N))
                for b in range(B):
                    last = mm(RA[:, b * 128:(b + 1) * 128], krow[par][:, b * NCC + cc, :], ws[:, b, :], start=True, stop=True)
                last.then_inc(s_mm[cc], 1)
                for b in range(B):
                    u = b * NCC + cc
                    o = RB[b * TC:(b + 1) * TC, 0:128]
                    mm(o, kqg[par][:, u, 3, :], S[:, b, :], start=True, stop=False)
                    last = mm(o, ap[par][:, u, R:R + TC], ws[:, b, :], start=False, stop=True)
                last.then_inc(o_mm[cc], 1)

            def s_ot(N, k, par, now, cc):
                pe.wait_ge(osb_ev[cc], done(N))
                if "I" in now:
                    pe.wait_ge(x_ev[1] if cc else vr_ev, done(N + 1))
                elif cc:
                    pe.wait_ge(acc_ev[0], done(N))
                nc.tensor.transpose(side, osb[:, cc, :], g.ident[:, :]).then_inc(ot_mm[cc], 1)

            def s_out(N, k, par, now, cc):
                pe.wait_ge(og_ev[cc], done(N))
                if "I" in now:
                    pe.wait_ge(x_ev[2 if cc else 0], done(N + 1))
                mm(side, wgo[:, 1, :], og[:, cc, :], start=True, stop=True).then_inc(out_mm[cc], 1)

            program(pe, ORDER, {"pt": s_pt, "ktr": s_ktr, "ss": s_ss, "vtr": s_vtr, "gram": s_gram, "z": s_z, "x": s_x, "y": s_y, "m": s_m,
                                "xn": s_xn, "yn": s_yn, "yf": s_yf, "ks": s_ks, "w": s_w, "so": s_so, "ot": s_ot, "out": s_out}, prep)


def mixture(nc, g, tag):
    NE = E_N + 1
    with ExitStack() as ctx:
        new_sem = semaphores(nc, ctx)
        sb = lambda n, s, dt=F32: ctx.enter_context(nc.sbuf_tensor(tag + n, s, dt))
        pb = lambda n, s: ctx.enter_context(nc.psum_tensor(tag + n, s, F32))
        sem = lambda n: new_sem(tag + n)
        w1, w2 = sb("w1", [128, NE, 128]), sb("w2", [128, NE, 128])
        b1, b2 = sb("b1", [128, NE]), sb("b2", [NE, 128])
        rw, rb = sb("rw", [128, NE]), sb("rb", [NE, 1])
        self32 = sb("sel32", [96, E_N * 128])
        sel = sb("sel", [96, E_N, 128], BF16)
        lt = sb("lt", [NE, TILE])
        lg = sb("lg", [128, 4, NE])
        mx = sb("mx", [128, 4])
        den = sb("den", [128, 4])
        p20 = sb("p20", [128, 4, 20])
        m20 = sb("m20", [128, 4, 20])
        top = sb("top", [128, 4, 8])
        held = sb("held", [128, 2])
        cw = sb("cw", [128, 4, NE])
        cwt = [sb(f"cwt{i}", [NE, TILE]) for i in range(2)]
        rest = sb("rest", [NE, 2, TILE])
        midw = sb("midw", [NE, TILE], BF16)
        parts = [sb(f"parts{i}", [96, TILE], BF16) for i in range(2)]
        hr, hs = sb("hr", [128, 2, TILE]), sb("hs", [128, 2, TILE])
        ph, pc, py = ([pb(f"{n}{i}", [128, TILE]) for i in range(2)] for n in ("ph", "pc", "py"))
        pl, pt = pb("pl", [128, TILE]), pb("pt", [128, TILE])
        evs = []

        def ev(n):
            evs.append(sem(n))
            return evs[-1]

        hc_mm, relu, hs_ev, y_mm = ([ev(f"{n}{e}") for e in range(NE)] for n in ("hc_mm", "relu", "scaled", "y_mm"))
        lt_mm, lt_ev, tr_mm, mx_ev, sub_ev, exp_ev, den_ev, rden_ev, p_ev, top_ev, topf_ev, m_ev, cw_ev, ct_mm, ct_ev = (
            ev(n) for n in ("lt_mm", "lt_ready", "tr_mm", "max_ready", "sub_ready", "exp_ready", "den_ready", "rden_ready", "p_ready",
                            "top_ready", "top3_ready", "match_ready", "cw_ready", "ct_mm", "cwt_ready"))
        hi_ev, r1_ev, mid_ev, r2_ev, parts_ev, acc_ev = (ev(n) for n in ("hi_ready", "r1_ready", "mid_ready", "r2_ready", "parts_ready", "acc_ready"))
        loaded, zeroed, const = sem("loaded"), sem("zeroed"), sem("const")
        with nc.Block() as b0:
            @b0.gpsimd
            def _(pool):
                for s in evs:
                    pool.sem_inc(s, CREDIT)
        block = ctx.enter_context(nc.Block())
        d = g.dram
        loads = [(w1[:, 0:E_N, :], d["eW1"].rearrange("e d h -> d e h")), (w1[:, E_N, :], d["sW1"]),
                 (w2[:, 0:E_N, :], d["eW2"].rearrange("e d h -> d e h")), (w2[:, E_N, :], d["sW2"]),
                 (b1[:, 0:E_N], d["eb1"].rearrange("e h -> h e")), (b1[:, E_N:NE], d["sb1"].unsqueeze(1)),
                 (b2[0:E_N, :], d["eb2"]), (b2[E_N:NE, :], d["sb2"].unsqueeze(0)),
                 (rw[:, 0:E_N], d["router_W"]), (rb[0:E_N, :], d["router_b"].unsqueeze(1)), (self32[:, :], d["c_sel"])]
        NPAIR = NT // 2

        def tiles(eng, step, lead):
            lead(0, 0, 0)
            with eng.Fori(0, NPAIR - 1) as j:
                step(j * 2, j, 0, j * 2 + 1, j)
                step(j * 2 + 1, j, 1, j * 2 + 2, j + 1)
            step(NT - 2, NPAIR - 1, 0, NT - 1, NPAIR - 1)
            step(NT - 1, NPAIR - 1, 1, None, None)

        def xn(j, par):
            return g.xn[:, bass.ds(j, 1), PAD + TILE * par:PAD + TILE * (par + 1)]

        @block.sync
        def _(sp):
            sp.wait_ge(zeroed, 1)
            for dst, src in loads:
                sp.dma_start(dst, src, allow_slow_non_contiguous=True).then_inc(loaded, 16)

        @block.tensor
        def _(pe):
            mm = nc.tensor.matmul
            pe.wait_ge(loaded, 16 * len(loads))
            pe.wait_ge(const, 1)

            def r_lt(n, j, par):
                pe.wait_ge(ct_ev, done(n - 1))
                pe.wait_ge(r1_ev, done(n - 1))
                mm(pl[0:NE, :], rw[:, :], xn(j, par), start=True, stop=True).then_inc(lt_mm, 1)

            def r_tr(n):
                pe.wait_ge(lt_ev, done(n))
                pe.wait_ge(sub_ev, done(n - 1))
                for a in range(4):
                    last = mm(pt[:, a * NE:(a + 1) * NE], lt[:, a * 128:(a + 1) * 128], g.ident[0:NE, 0:NE], start=True, stop=True)
                last.then_inc(tr_mm, 1)

            def r_ct(n):
                pe.wait_ge(cw_ev, done(n))
                for a in range(4):
                    last = nc.tensor.transpose(pl[0:NE, a * 128:(a + 1) * 128], cw[:, a, :], g.ident[:, :])
                last.then_inc(ct_mm, 1)

            def lead(n, j, par):
                r_lt(n, j, par)
                r_tr(n)
                r_ct(n)

            def step(n, j, par, n1, j1):
                def hidden(e):
                    if e < NE:
                        pe.wait_ge(relu[e - 2], done(n) if e >= 2 else done(n - 1))
                        pe.wait_ge(hs_ev[e - 2], done(n) if e >= 2 else done(n - 1))
                        last = mm(ph[e % 2][:, :], w1[:, e, :], xn(j, par), start=True, stop=True)
                        if e < E_N:
                            last = mm(pc[e % 2][:, :], sel[:, e, :], parts[par][:, :], start=True, stop=True)
                        last.then_inc(hc_mm[e], 1)
                pe.wait_ge(parts_ev, done(n))
                hidden(0)
                pe.wait_ge(acc_ev, done(n - 2))
                mm(py[par][:, :], b2[:, :], cwt[par][:, :], start=True, stop=False)
                for e in range(NE):
                    hidden(e + 1)
                    pe.wait_ge(hs_ev[e], done(n))
                    mm(py[par][:, :], w2[:, e, :], hs[:, e % 2, :], start=False, stop=e == NE - 1).then_inc(y_mm[e], 1)
                    if n1 is not None:
                        if e == 1:
                            r_lt(n1, j1, 1 - par)
                        if e == 3:
                            r_tr(n1)
                        if e == 10:
                            r_ct(n1)

            tiles(pe, step, lead)

        @block.scalar
        def _(act):
            act.wait_ge(loaded, 16 * len(loads))

            def r_lt(n):
                act.wait_ge(lt_mm, done(n))
                act.wait_ge(tr_mm, done(n - 1))
                nc.scalar.activation(lt[:, :], pl[0:NE, :], ACT.Identity, bias=rb[:, :]).then_inc(lt_ev, 1)

            def r_exp(n):
                act.wait_ge(sub_ev, done(n))
                nc.scalar.activation(lg[:, :, 0:E_N], lg[:, :, 0:E_N], ACT.Exp).then_inc(exp_ev, 1)

            def lead(n, j, par):
                r_lt(n)
                r_exp(n)

            def step(n, j, par, n1, j1):
                for e in range(NE):
                    act.wait_ge(hc_mm[e], done(n))
                    act.wait_ge(hs_ev[e - 2], done(n) if e >= 2 else done(n - 1))
                    nc.scalar.activation(hr[:, e % 2, :], ph[e % 2][:, :], ACT.Relu, bias=b1[:, e:e + 1]).then_inc(relu[e], 1)
                    if n1 is not None:
                        if e == 2:
                            r_lt(n1)
                        if e == 5:
                            r_exp(n1)

            tiles(act, step, lead)

        @block.vector
        def _(dve):
            nc.vector.memset(parts[0][:, :], 0.0)
            nc.vector.memset(parts[1][:, :], 0.0)
            nc.vector.memset(p20[:, :, :], -1.0)
            nc.vector.memset(rw[:, :], 0.0)
            nc.vector.memset(rb[:, :], 0.0)
            nc.vector.memset(cw[:, :, :], 1.0).then_inc(zeroed, 1)
            dve.wait_ge(zeroed, 1)
            dve.wait_ge(loaded, 16 * len(loads))
            nc.vector.tensor_copy(sel[:, :, :].rearrange("p e n -> p (e n)"), self32[:, :]).then_inc(const, 1)

            def r_sub(n):
                dve.wait_ge(tr_mm, done(n))
                v = pt[:, 0:4 * NE].rearrange("p (a e) -> p a e", e=NE)[:, :, 0:E_N]
                nc.vector.tensor_reduce(mx[:, :], v, AX.X, ALU.max).then_inc(mx_ev, 1)
                dve.wait_ge(mx_ev, done(n))
                nc.vector.tensor_tensor(lg[:, :, 0:E_N], v, mx[:, :].unsqueeze(2).broadcast_to([128, 4, E_N]), ALU.subtract).then_inc(sub_ev, 1)

            def r_top(n):
                dve.wait_ge(exp_ev, done(n))
                nc.vector.tensor_reduce(den[:, :], lg[:, :, 0:E_N], AX.X, ALU.add).then_inc(den_ev, 1)
                dve.wait_ge(den_ev, done(n))
                nc.vector.reciprocal(den[:, :], den[:, :]).then_inc(rden_ev, 1)
                dve.wait_ge(rden_ev, done(n))
                nc.vector.tensor_tensor(p20[:, :, 0:E_N], lg[:, :, 0:E_N], den[:, :].unsqueeze(2).broadcast_to([128, 4, E_N]), ALU.mult).then_inc(p_ev, 1)
                dve.wait_ge(p_ev, done(n))
                nc.vector.memset(held[:, 0:1], 0.0)
                for a in range(4):
                    last = nc.vector.max(top[:, a, :], p20[:, a, :])
                last.then_inc(top_ev, 1)
                dve.wait_ge(top_ev, done(n))
                nc.vector.memset(top[:, :, TOPK:8], -1.0).then_inc(topf_ev, 1)
                dve.wait_ge(topf_ev, done(n))
                nc.vector.memset(held[:, 1:2], 0.0)
                for a in range(4):
                    last = nc.vector.match_replace(m20[:, a, :], top[:, a, :], p20[:, a, :], -2.0)
                last.then_inc(m_ev, 1)
                dve.wait_ge(m_ev, done(n))
                dve.wait_ge(ct_mm, done(n - 1))
                nc.vector.scalar_tensor_tensor(cw[:, :, 0:E_N], m20[:, :, 0:E_N], -1.5, p20[:, :, 0:E_N], ALU.is_lt, ALU.mult).then_inc(cw_ev, 1)

            def r_parts(n, par):
                dve.wait_ge(ct_mm, done(n))
                dve.wait_ge(y_mm[NE - 1], done(n - 2))
                hi, mid, lo = (parts[par][32 * i:32 * i + NE, :] for i in range(3))
                nc.vector.tensor_copy(cwt[par][:, :], pl[0:NE, :]).then_inc(ct_ev, 1)
                nc.vector.tensor_copy(hi, pl[0:NE, :]).then_inc(hi_ev, 1)
                dve.wait_ge(hi_ev, done(n))
                nc.vector.tensor_tensor(rest[:, 0, :], pl[0:NE, :], hi, ALU.subtract).then_inc(r1_ev, 1)
                dve.wait_ge(r1_ev, done(n))
                nc.vector.tensor_copy(midw[:, :], rest[:, 0, :]).then_inc(mid_ev, 1)
                dve.wait_ge(mid_ev, done(n))
                nc.vector.tensor_copy(mid, midw[:, :])
                nc.vector.tensor_tensor(rest[:, 1, :], rest[:, 0, :], midw[:, :], ALU.subtract).then_inc(r2_ev, 1)
                dve.wait_ge(r2_ev, done(n))
                nc.vector.tensor_copy(lo, rest[:, 1, :]).then_inc(parts_ev, 1)

            def lead(n, j, par):
                r_sub(n)
                r_top(n)
                r_parts(n, par)

            def step(n, j, par, n1, j1):
                for e in range(NE):
                    dve.wait_ge(relu[e], done(n))
                    dve.wait_ge(y_mm[e - 2], done(n) if e >= 2 else done(n - 1))
                    if e < E_N:
                        nc.vector.tensor_tensor(hs[:, e % 2, :], pc[e % 2][:, :], hr[:, e % 2, :], ALU.mult).then_inc(hs_ev[e], 1)
                    else:
                        nc.vector.tensor_copy(hs[:, e % 2, :], hr[:, e % 2, :]).then_inc(hs_ev[e], 1)
                    if n1 is not None:
                        if e == 4:
                            r_sub(n1)
                        if e == 6:
                            r_top(n1)
                        if e == 11:
                            r_parts(n1, 1 - par)
                dve.wait_ge(y_mm[NE - 1], done(n))
                x = g.xT[:, bass.ds(j, 1), TILE * par:TILE * (par + 1)]
                nc.vector.tensor_tensor(x, py[par][:, :].unsqueeze(1), x, ALU.add).then_inc(acc_ev, 1)

            tiles(dve, step, lead)


def decay_attention(nc, g):
    NG = NTOK // 128
    LV = 5
    with ExitStack() as ctx:
        new_sem = semaphores(nc, ctx)
        sb = lambda n, s, dt=F32: ctx.enter_context(nc.sbuf_tensor("b_" + n, s, dt))
        pb = lambda n, s: ctx.enter_context(nc.psum_tensor("b_" + n, s, F32))
        sem = lambda n: new_sem("b_" + n)
        w = sb("w", [128, 6, 128])
        bw = sb("bw", [128, 1])
        masks = sb("masks", [128, LV + 1, 128])
        bmask = sb("bmask", [128, 128])
        F = sb("F", [128, NTOK])
        rF = sb("rF", [128, NTOK])
        kB = sb("kB", [128, NTOK])
        V = sb("V", [128, NG, 128])
        P = sb("P", [128, NG, 2, 128])
        kBr = sb("kBr", [128, NG, 128])
        z1 = sb("z1", [128, 2, TILE])
        wz = sb("wz", [128, 2, TILE])
        tmp4 = sb("tmp4", [128, 4, TILE])
        S = sb("S", [128, 2, B, 128])
        uS = sb("uS", [128, 2, B, 128])
        oT = sb("oT", [128, 2, B, 128])
        bank = [pb(f"bank{i}", [128, TILE]) for i in range(8)]
        loaded = sem("loaded")
        d = g.dram
        loads = [(w[:, i, :], d["b_" + n]) for i, n in enumerate(("Wx", "Ww", "Wk", "Wv", "Wr", "Wo"))] + [
            (bw[:, :], d["b_bw"].unsqueeze(1)), (masks[:, :, :].rearrange("p a b -> p (a b)"), d["c_bmasks"]), (bmask[:, :], d["c_bdiag"])]
        mm = nc.tensor.matmul
        zx, zx_ev, z_mm, k_mm, r_mm, w_ev, a_ev, k_ev, r_ev, v_mm, v_ev = (sem(n) for n in ("zx", "zx_ready", "z_mm", "k_mm", "r_mm", "w_ready", "a_ready", "k_ready", "r_ready", "v_mm", "v_ready"))
        with nc.Block() as block:
            @block.sync
            def _(sp):
                for dst, src in loads:
                    sp.dma_start(dst, src).then_inc(loaded, 16)

            @block.tensor
            def _(pe):
                pe.wait_ge(loaded, 16 * len(loads))
                for i in range(NT):
                    x = g.xn[:, i // 2, PAD + TILE * (i % 2):PAD + TILE * (i % 2 + 1)]
                    if i:
                        pe.wait_ge(zx_ev, i)
                    mm(bank[0][:, :], w[:, 0, :], x, start=True, stop=True).then_inc(zx, 1)
                    if i:
                        pe.wait_ge(k_ev, i)
                    mm(bank[1][:, :], w[:, 2, :], x, start=True, stop=True).then_inc(k_mm, 1)
                    if i:
                        pe.wait_ge(r_ev, i)
                    mm(bank[2][:, :], w[:, 4, :], x, start=True, stop=True).then_inc(r_mm, 1)
                    if i >= 2:
                        pe.wait_ge(v_ev, i - 1)
                    for a in range(4):
                        last = mm(bank[4 + i % 2][:, a * 128:(a + 1) * 128], x[:, a * 128:(a + 1) * 128], w[:, 3, :], start=True, stop=True)
                    last.then_inc(v_mm, 1)
                    pe.wait_ge(zx_ev, i + 1)
                    if i:
                        pe.wait_ge(w_ev, i)
                    mm(bank[3][:, :], w[:, 1, :], z1[:, i % 2, :], start=True, stop=True).then_inc(z_mm, 1)

            @block.scalar
            def _(act):
                act.wait_ge(loaded, 16 * len(loads))
                for i in range(NT):
                    act.wait_ge(zx, i + 1)
                    nc.scalar.activation(z1[:, i % 2, :], bank[0][:, :], ACT.Copy).then_inc(zx_ev, 1)
                    act.wait_ge(r_mm, i + 1)
                    nc.scalar.activation(rF[:, TILE * i:TILE * (i + 1)], bank[2][:, :], ACT.Sigmoid).then_inc(r_ev, 1)
                    act.wait_ge(z_mm, i + 1)
                    if i >= 2:
                        act.wait_ge(a_ev, i - 1)
                    nc.scalar.activation(wz[:, i % 2, :], bank[3][:, :], ACT.Sigmoid, bias=bw[:, :]).then_inc(w_ev, 1)

            @block.vector
            def _(dve):
                for i in range(NT):
                    dve.wait_ge(k_mm, i + 1)
                    nc.vector.tensor_copy(kB[:, TILE * i:TILE * (i + 1)], bank[1][:, :]).then_inc(k_ev, 1)
                    dve.wait_ge(v_mm, i + 1)
                    nc.vector.tensor_copy(V[:, 4 * i:4 * i + 4, :], bank[4 + i % 2][:, :].rearrange("p (a n) -> p a n", a=4)).then_inc(v_ev, 1)
                    dve.wait_ge(w_ev, i + 1)
                    nc.vector.tensor_scalar(F[:, TILE * i:TILE * (i + 1)], wz[:, i % 2, :], -1.0, 1.0, ALU.mult, ALU.add).then_inc(a_ev, 1)

        p_mm, p_ev, up_ev, t_ev, add_ev = sem("p_mm"), sem("p_ready"), sem("up_ready"), sem("f_read"), sem("added")
        NBK = NG // 2
        with nc.Block() as block:
            @block.tensor
            def _(pe):
                n = 0
                for l in range(LV + 1):
                    for q in range(NBK):
                        if l:
                            pe.wait_ge(up_ev, (l - 1) * B + q // (NBK // B) + 1)
                        if n >= 8:
                            pe.wait_ge(p_ev, n - 7)
                        h = q % 2
                        for a in range(4):
                            t0 = (4 * (q // 2) + a) * 128
                            last = mm(bank[n % 8][:, a * 128:(a + 1) * 128], kB[64 * h:64 * h + 64, t0:t0 + 128], rF[64 * h:64 * h + 64, t0:t0 + 128], start=True, stop=True)
                        last.then_inc(p_mm, 1)
                        n += 1

            @block.gpsimd
            def _(pool):
                pool.wait_ge(loaded, 16 * len(loads))
                for n in range(NBK * (LV + 1)):
                    l, q = divmod(n, NBK)
                    if l:
                        pool.wait_ge(p_ev, n + 1)
                        dst = P[:, 4 * (q // 2):4 * (q // 2) + 4, q % 2, :]
                        nc.gpsimd.tensor_tensor(dst, dst, tmp4[:, n % 4, :].rearrange("p (a t) -> p a t", a=4), ALU.add).then_inc(add_ev, 1)
                        pool.wait_ge(add_ev, n + 1 - NBK)

            @block.vector
            def _(dve):
                n = 0
                ups = 0
                for l in range(LV + 1):
                    for q in range(NBK):
                        dve.wait_ge(p_mm, n + 1)
                        src = bank[n % 8][:, :].rearrange("p (x t) -> p x t", t=128)
                        mask = masks[:, l, :].unsqueeze(1).broadcast_to([128, 4, 128])
                        if l == 0:
                            dst = P[:, 4 * (q // 2):4 * (q // 2) + 4, q % 2, :]
                        else:
                            dst = tmp4[:, n % 4, :].rearrange("p (x t) -> p x t", t=128)
                            if n - NBK >= 4:
                                dve.wait_ge(add_ev, n - NBK - 3)
                        nc.vector.tensor_tensor(dst, src, mask, ALU.mult).then_inc(p_ev, 1)
                        n += 1
                        if n % (NBK // B) == 0 and l <= LV:
                            b = q // (NBK // B)
                            s0, s1 = b * T, (b + 1) * T
                            if l == 0:
                                nc.vector.tensor_tensor(rF[:, s0:s1], rF[:, s0:s1], F[:, s0:s1], ALU.mult).then_inc(up_ev, 1)
                                continue
                            hs = 1 << (l - 1)
                            v = lambda t: t[:, s0:s1].rearrange("p (n two h) -> p n two h", two=2, h=hs)
                            fv, rv, kv = v(F), v(rF), v(kB)
                            sh = [128, T // (2 * hs), hs]
                            mid, end = fv[:, :, 0, hs - 1:hs].broadcast_to(sh), fv[:, :, 1, hs - 1:hs].broadcast_to(sh)
                            nc.vector.tensor_tensor(kv[:, :, 0, :], kv[:, :, 0, :], end, ALU.mult)
                            nc.vector.tensor_tensor(rv[:, :, 1, :], rv[:, :, 1, :], mid, ALU.mult).then_inc(t_ev, 1)
                            ups += 1
                            dve.wait_ge(t_ev, ups)
                            nc.vector.tensor_tensor(fv[:, :, 1, :], fv[:, :, 1, :], mid, ALU.mult).then_inc(up_ev, 1)
                            dve.wait_ge(up_ev, l * B + b + 1)

        kt_mm, kt_ev, u_mm, u_ev, s_ev, i_mm, a_mm, o_ev, o2_ev, y_mm, y_ev, z_ev = (sem(n) for n in ("kt_mm", "kt_ready", "u_mm", "u_ready", "s_ready", "i_mm", "a_mm", "o_ready", "o2_ready", "y_mm", "y_ready", "s_zero"))
        NGB = NG // B
        with nc.Block() as block:
            @block.tensor
            def _(pe):
                for q in range(NG // 4):
                    if q >= 2:
                        pe.wait_ge(kt_ev, q - 1)
                    for a in range(4):
                        last = nc.tensor.transpose(bank[q % 2][:, a * 128:(a + 1) * 128], kB[:, (4 * q + a) * 128:(4 * q + a + 1) * 128], g.ident[:, :])
                    last.then_inc(kt_mm, 1)
                pe.wait_ge(kt_ev, NG // 4)
                pe.wait_ge(z_ev, 1)

                def update(n):
                    gr, c = divmod(n, 4)
                    if n >= 2:
                        pe.wait_ge(u_ev, n - 1)
                    for b in range(B):
                        i = b * NGB + gr
                        last = mm(bank[2 + n % 2][:, b * 128:(b + 1) * 128], kBr[32 * c:32 * c + 32, i, :], V[32 * c:32 * c + 32, i, :], start=True, stop=True)
                    last.then_inc(u_mm, 1)

                update(0)
                for gr in range(NGB):
                    if gr >= 2:
                        pe.wait_ge(o_ev, gr - 1)
                    for b in range(B):
                        i = b * NGB + gr
                        for h in range(2):
                            last = mm(bank[4 + gr % 2][64 * h:64 * h + 64, b * 128:(b + 1) * 128], V[:, i, 64 * h:64 * h + 64], P[:, i, h, :], start=True, stop=True)
                    last.then_inc(a_mm, 1)
                    for c in range(4):
                        n = 4 * gr + c
                        if n + 1 < 4 * NGB:
                            update(n + 1)
                        if n:
                            pe.wait_ge(s_ev, n)
                        if c == 0 and gr:
                            pe.wait_ge(o2_ev, gr)
                        for b in range(B):
                            last = mm(bank[6][:, b * 128 + 32 * c:b * 128 + 32 * c + 32], S[:, n % 2, b, :], rF[:, b * T + 32 * n:b * T + 32 * n + 32], start=True, stop=True)
                        last.then_inc(i_mm, 1)
                    pe.wait_ge(o2_ev, gr + 1)
                    if gr:
                        pe.wait_ge(y_ev, gr)
                    mm(bank[7][:, :], w[:, 5, :], oT[:, gr % 2, :, :].rearrange("p b t -> p (b t)"), start=True, stop=True).then_inc(y_mm, 1)

            @block.scalar
            def _(act):
                for q in range(NG // 4):
                    act.wait_ge(kt_mm, q + 1)
                    nc.scalar.activation(kBr[:, 4 * q:4 * q + 4, :], bank[q % 2][:, :].rearrange("p (a n) -> p a n", a=4), ACT.Copy).then_inc(kt_ev, 1)
                for gr in range(NGB):
                    act.wait_ge(a_mm, gr + 1)
                    if gr >= 2:
                        act.wait_ge(y_mm, gr - 1)
                    nc.scalar.activation(oT[:, gr % 2, :, :].rearrange("p b t -> p (b t)"), bank[4 + gr % 2][:, :], ACT.Copy).then_inc(o_ev, 1)

            @block.vector
            def _(dve):
                nc.vector.memset(S[:, 0, :, :], 0.0).then_inc(z_ev, 1)
                dve.wait_ge(z_ev, 1)
                for n in range(4 * NGB):
                    if n + 1 < 4 * NGB:
                        dve.wait_ge(u_mm, n + 1)
                        nc.vector.tensor_tensor(uS[:, n % 2, :, :], bank[2 + n % 2][:, :].rearrange("p (b e) -> p b e", b=B),
                                                bmask[:, :].unsqueeze(1).broadcast_to([128, B, 128]), ALU.mult).then_inc(u_ev, 1)
                        dve.wait_ge(u_ev, n + 1)
                        if n:
                            dve.wait_ge(s_ev, n)
                            dve.wait_ge(i_mm, n)
                        for b in range(B):
                            end = b * T + 32 * n + 31
                            last = nc.vector.scalar_tensor_tensor(S[:, (n + 1) % 2, b, :], S[:, n % 2, b, :], F[:, end:end + 1], uS[:, n % 2, b, :], ALU.mult, ALU.add)
                        last.then_inc(s_ev, 1)
                    if n % 4 == 3:
                        gr = n // 4
                        dve.wait_ge(i_mm, n + 1)
                        dve.wait_ge(o_ev, gr + 1)
                        o = oT[:, gr % 2, :, :].rearrange("p b t -> p (b t)")
                        nc.vector.tensor_tensor(o, bank[6][:, :], o, ALU.add).then_inc(o2_ev, 1)
                        dve.wait_ge(y_mm, gr + 1)
                        x = g.xT[:, :, gr * 128:(gr + 1) * 128]
                        nc.vector.tensor_tensor(x, bank[7][:, :].rearrange("p (b t) -> p b t", b=B), x, ALU.add).then_inc(y_ev, 1)



INS = [("x", "L0_attn_a_x")] + [(n, "L0_attn_a_" + n) for n in ("Wq", "Wk", "Wv", "Wb", "Wa", "A_log", "dt_bias", "conv_q", "conv_k", "conv_v", "Wg", "rms_weight", "Wo")] + [
    ("b_" + n, "L0_attn_b_" + n) for n in ("ln_g", "ln_b", "Wx", "Ww", "bw", "Wk", "Wv", "Wr", "Wo")] + [
    (n, "L0_ffn_" + n) for n in ("router_W", "router_b", "sW1", "sb1", "sW2", "sb2", "eW1", "eb1", "eW2", "eb2")]


def build(nc, dram, phases="abcd"):
    with ExitStack() as ctx:
        sb = lambda n, s, dt=F32: ctx.enter_context(nc.sbuf_tensor(n, s, dt))
        g = Shared()
        g.dram = dram
        g.xT = sb("xT", [128, B, T])
        g.xn = sb("xn", [128, B, PAD + T])
        g.ident = sb("ident", [128, 128])
        g.mean = sb("mean", [128, 128])
        g.ones = sb("ones", [128, 128])
        g.half = sb("half", [128, U])
        g.minus_half = sb("minus_half", [128, 1])
        zeroed = ctx.enter_context(nc.semaphore("zeroed"))
        g.rms_sem = ctx.enter_context(nc.semaphore("rms_in"))
        with ExitStack() as a:
            sa = lambda n, s: a.enter_context(nc.sbuf_tensor(n, s, F32))
            g.mask4 = sa("mask4", [R, 128])
            g.lev = sa("lev", [R, LEVELS * R])
            g.after = sa("after", [TC, R])
            g.upto = sa("upto", [TC, TC])
            g.beta = sa("beta", [R, NH, NTOK // TC])
            g.gt = sa("gt", [TC, NTOK // TC, NH])
            g.rms_in = sa("rms_w", [128, 1])
            g.const_loads = [("c_ident", g.ident[:, :]), ("c_mean", g.mean[:, :]), ("c_mask4", g.mask4[:, :]), ("c_lev", g.lev[:, :]),
                             ("c_after", g.after[:, :]), ("c_upto", g.upto[:, :])]
            load_rows(nc, g)
            with nc.Block() as b:
                @b.vector
                def _(dve):
                    nc.vector.memset(g.xn[:, :, 0:PAD], 0.0)
                    nc.vector.memset(g.half[:, :], 0.5)
                    nc.vector.memset(g.minus_half[:, :], -0.5)
                    nc.vector.memset(g.ones[:, :], 1.0).then_inc(zeroed, 1)
                    dve.wait_ge(zeroed, 1)

                @b.sync
                def _(sp):
                    sp.dma_start(g.rms_in[:, :], dram["rms_weight"].unsqueeze(1)).then_inc(g.rms_sem, 16)
                    sp.wait_ge(g.rms_sem, 16)
            layernorm(nc, g, "ln0", lambda i: g.xT[:, i // 2, TILE * (i % 2):TILE * (i % 2 + 1)])
            decay_gates(nc, g)
            delta_attention(nc, g)
        x_tile = lambda i: g.xT[:, i // 2, TILE * (i % 2):TILE * (i % 2 + 1)]
        n_tile = lambda i: g.xn[:, i // 2, PAD + TILE * (i % 2):PAD + TILE * (i % 2 + 1)]
        layernorm(nc, g, "ln1", x_tile)
        mixture(nc, g, "f1")
        layernorm(nc, g, "ln2", x_tile)
        with ExitStack() as a:
            gain = a.enter_context(nc.sbuf_tensor("ln_gain", [128, 2], F32))
            gain_in = a.enter_context(nc.semaphore("ln_gain_in"))
            with nc.Block() as b:
                @b.sync
                def _(sp):
                    sp.dma_start(gain[:, 0:1], dram["b_ln_g"].unsqueeze(1)).then_inc(gain_in, 16)
                    sp.dma_start(gain[:, 1:2], dram["b_ln_b"].unsqueeze(1)).then_inc(gain_in, 16)
                    sp.wait_ge(gain_in, 32)
            layernorm(nc, g, "ln3", n_tile, (gain[:, 0:1], gain[:, 1:2]))
            decay_attention(nc, g)
        layernorm(nc, g, "ln4", x_tile)
        mixture(nc, g, "f2")
        store_rows(nc, g)


def kernel(**inputs):
    import concourse.bacc as _bacc
    from concourse.bass_utils import run_bass_kernel_spmd as _run

    nc = _bacc.Bacc("TRN2", target_bir_lowering=False, num_devices=1)
    arrays, dram = {}, {}
    named = [(s, np.ascontiguousarray(inputs[n])) for s, n in INS] + list(constants().items())
    for name, a in named:
        arrays[f"in_{name}_dram"] = a
        dram[name] = nc.dram_tensor(f"in_{name}_dram", a.shape, mybir.dt.from_np(a.dtype), kind="ExternalInput").ap()
    dram["out"] = nc.dram_tensor("out_0_dram", (B, T, D), F32, kind="ExternalOutput").ap()
    build(nc, dram)
    r = _run(nc, [arrays], core_ids=[0])
    return r.results[0]["out_0_dram"]
```

```python
import math
from contextlib import ExitStack

import numpy as np
import concourse.bass as bass
from concourse import mybir

F32 = mybir.dt.float32
BF16 = mybir.dt.bfloat16
F16 = mybir.dt.float16
F32R = mybir.dt.float32r
ALU = mybir.AluOpType
ACT = mybir.ActivationFunctionType
AX = mybir.AxisListType

B, T, D = 4, 1024, 128
NTOK = B * T
NH, NHH, TAPS = 8, 3, 4
TC = 32
R = NHH * TC
NCC = 2
SPAN = NCC * TC
U = B * NCC
KSTEPS = T // SPAN
PAD = TAPS - 1
LEVELS = 6
HU = U // 2
CREDIT = 2
TILE = 512
NT = NTOK // TILE
E_N, TOPK = 15, 3


class Shared:

    dram = h = None


def done(n):
    return n + 1 + CREDIT


def done_half(n, hf):
    return 2 * n + hf + 1 + CREDIT


def constants():
    i, t = np.divmod(np.arange(R), TC)
    tau = NHH * t + i
    later = tau[None, :] > tau[:, None]
    tri = np.arange(TC)[None, :] >= t[:, None]
    mask4 = np.concatenate([later, tri], axis=1).astype(np.float32)
    lev = []
    for l in range(LEVELS):
        s, joined = (NHH << (l - 1), NHH << l) if l else (1, NHH)
        same = (tau[:, None] // joined) == (tau[None, :] // joined)
        lev.append(-(same & (tau[:, None] // s > tau[None, :] // s)).astype(np.float32))
    lev.append(lev[0].T)
    j = np.arange(TC)
    after_m = (j[:, None] > t[None, :]).astype(np.float32)
    upto = (j[:, None] <= j[None, :]).astype(np.float32)
    c = {
        "c_ident": np.eye(128, dtype=np.float32),
        "c_mean": np.full((128, 128), 1.0 / D, np.float32),
        "c_mask4": mask4,
        "c_lev": np.concatenate(lev, axis=1),
        "c_after": after_m,
        "c_upto": upto,
    }
    sel = np.zeros((96, E_N, 128), np.float32)
    for part in range(3):
        for e in range(E_N):
            sel[32 * part + e, e] = 1
    c["c_sel"] = sel.reshape(96, -1)
    a = np.arange(128)
    bm = [np.eye(128, dtype=np.float32)]
    for l in range(5):
        s = 1 << l
        same = (a[:, None] // (2 * s)) == (a[None, :] // (2 * s))
        bm.append((same & (a[:, None] // s < a[None, :] // s)).astype(np.float32))
    c["c_bmasks"] = np.stack(bm, 1).reshape(128, -1)
    c["c_bdiag"] = (a[:, None] // 64 == a[None, :] // 64).astype(np.float32)
    return c


def semaphores(nc, ctx):
    held = []

    def sem(name):
        held.append(nc.alloc_semaphore(name))
        return held[-1]

    def end():
        nc.clear_and_free_semaphores(held)
        nc.all_engine_barrier()

    ctx.callback(end)
    return sem


def load_rows(nc, g):
    with ExitStack() as ctx:
        new_sem = semaphores(nc, ctx)
        xin = ctx.enter_context(nc.sbuf_tensor("xin", [128, NTOK // 128, D], F32))
        ps = [ctx.enter_context(nc.psum_tensor(f"ld{i}", [128, TILE], F32)) for i in range(4)]
        loaded, cst, turned, kept = (new_sem(n) for n in ("ld_x", "ld_cst", "ld_turned", "ld_kept"))
        block = ctx.enter_context(nc.Block())
        src = g.dram["x"].rearrange("b t d -> (b t) d").rearrange("(j p) d -> p j d", p=128)

        @block.sync
        def _(sp):
            n = 0
            for name, dst in g.const_loads:
                sp.dma_start(dst, g.dram[name]).then_inc(cst, 16)
                n += 16
            sp.wait_ge(cst, n)
            for q in range(4):
                sp.dma_start(xin[:, 8 * q:8 * q + 8, :], src[:, 8 * q:8 * q + 8, :]).then_inc(loaded, 16)
                sp.wait_ge(loaded, 16 * (q + 1))

        @block.tensor
        def _(pe):
            pe.wait_ge(cst, 16 * len(g.const_loads))
            for i in range(NT):
                pe.wait_ge(loaded, 16 * (i // 2 + 1))
                if i >= 4:
                    pe.wait_ge(kept, i - 3)
                for a in range(4):
                    last = nc.tensor.transpose(ps[i % 4][:, 128 * a:128 * a + 128], xin[:, 4 * i + a, :], g.ident[:, :])
                last.then_inc(turned, 1)

        @block.scalar
        def _(act):
            for i in range(NT):
                act.wait_ge(turned, i + 1)
                nc.scalar.activation(g.xT[:, i // 2, TILE * (i % 2):TILE * (i % 2 + 1)], ps[i % 4][:, :], ACT.Copy).then_inc(kept, 1)


def store_rows(nc, g):
    with ExitStack() as ctx:
        new_sem = semaphores(nc, ctx)
        xo = ctx.enter_context(nc.sbuf_tensor("xout", [128, NTOK // 128, D], F32))
        ps = [ctx.enter_context(nc.psum_tensor(f"st{i}", [128, TILE], F32)) for i in range(4)]
        turned, kept, stored = (new_sem(n) for n in ("st_turned", "st_kept", "st_stored"))
        block = ctx.enter_context(nc.Block())
        dst = g.dram["out"].rearrange("b t d -> (b t) d").rearrange("(j p) d -> p j d", p=128)

        @block.tensor
        def _(pe):
            for i in range(NT):
                if i >= 4:
                    pe.wait_ge(kept, i - 3)
                for a in range(4):
                    o = TILE * (i % 2) + 128 * a
                    last = nc.tensor.transpose(ps[i % 4][:, 128 * a:128 * a + 128], g.xT[:, i // 2, o:o + 128], g.ident[:, :])
                last.then_inc(turned, 1)

        @block.scalar
        def _(act):
            for i in range(NT):
                act.wait_ge(turned, i + 1)
                nc.scalar.activation(xo[:, 4 * i:4 * i + 4, :], ps[i % 4][:, :].rearrange("p (a d) -> p a d", a=4), ACT.Copy).then_inc(kept, 1)

        @block.sync
        def _(sp):
            for q in range(4):
                sp.wait_ge(kept, 2 * q + 2)
                sp.dma_start(dst[:, 8 * q:8 * q + 8, :], xo[:, 8 * q:8 * q + 8, :]).then_inc(stored, 16)
            sp.wait_ge(stored, 64)


def layernorm(nc, g, tag, src, affine=None):
    with ExitStack() as ctx:
        new_sem = semaphores(nc, ctx)
        sb = lambda n, s: ctx.enter_context(nc.sbuf_tensor(tag + n, s, F32))
        mean = [ctx.enter_context(nc.psum_tensor(f"{tag}mean{i}", [128, TILE], F32)) for i in range(2)]
        var = [ctx.enter_context(nc.psum_tensor(f"{tag}var{i}", [128, TILE], F32)) for i in range(2)]
        xc = sb("xc", [128, 2, TILE])
        sq = sb("sq", [128, 2, TILE])
        rs = sb("rs", [128, 2, TILE])
        sem = lambda n: new_sem(tag + n)
        meaned, centred, squared, varied, rooted, scaled, normed = (sem(n) for n in ("meaned", "centred", "squared", "varied", "rooted", "scaled", "normed"))
        eps = ctx.enter_context(nc.sbuf_tensor(tag + "eps", [128, 1], F32))
        eps_ready = sem("eps_ready")
        block = ctx.enter_context(nc.Block())

        @block.tensor
        def _(pe):
            def mean_of(i):
                if i >= 2:
                    pe.wait_ge(centred, i - 1)
                nc.tensor.matmul(mean[i % 2][:, :], g.mean[:, :], src(i), start=True, stop=True).then_inc(meaned, 1)
            mean_of(0)
            for i in range(NT):
                if i + 1 < NT:
                    mean_of(i + 1)
                pe.wait_ge(squared, i + 1)
                if i >= 2:
                    pe.wait_ge(rooted, i - 1)
                nc.tensor.matmul(var[i % 2][:, :], g.mean[:, :], sq[:, i % 2, :], start=True, stop=True).then_inc(varied, 1)

        @block.scalar
        def _(act):
            act.wait_ge(eps_ready, 1)

            def square(i):
                act.wait_ge(centred, i + 1)
                if i >= 2:
                    act.wait_ge(varied, i - 1)
                nc.scalar.activation(sq[:, i % 2, :], xc[:, i % 2, :], ACT.Square).then_inc(squared, 1)
            square(0)
            for i in range(NT):
                if i + 1 < NT:
                    square(i + 1)
                act.wait_ge(varied, i + 1)
                if i >= 2:
                    act.wait_ge(normed, i - 1)
                nc.scalar.activation(rs[:, i % 2, :], var[i % 2][:, :], ACT.Sqrt, bias=eps[:, :]).then_inc(rooted, 1)

        @block.vector
        def _(dve):
            def centre(i):
                dve.wait_ge(meaned, i + 1)
                if i >= 2:
                    dve.wait_ge(squared, i - 1)
                    dve.wait_ge(normed, i - 1)
                nc.vector.tensor_tensor(xc[:, i % 2, :], src(i), mean[i % 2][:, :], ALU.subtract).then_inc(centred, 1)
            nc.vector.memset(eps[:, :], 1e-5).then_inc(eps_ready, 1)
            centre(0)
            for i in range(NT):
                if i + 1 < NT:
                    centre(i + 1)
                dve.wait_ge(rooted, i + 1)
                nc.vector.reciprocal(rs[:, i % 2, :], rs[:, i % 2, :]).then_inc(scaled, 1)
                dve.wait_ge(scaled, i + 1)
                dst = g.xn[:, i // 2, PAD + TILE * (i % 2):PAD + TILE * (i % 2 + 1)]
                if affine is None:
                    nc.vector.tensor_tensor(dst, xc[:, i % 2, :], rs[:, i % 2, :], ALU.mult).then_inc(normed, 1)
                else:
                    nc.vector.tensor_tensor(rs[:, i % 2, :], xc[:, i % 2, :], rs[:, i % 2, :], ALU.mult).then_inc(normed, 1)
                    dve.wait_ge(normed, i + 1)
                    nc.vector.tensor_scalar(dst, rs[:, i % 2, :], affine[0], affine[1], ALU.mult, ALU.add)


def decay_gates(nc, g):
    with ExitStack() as ctx:
        new_sem = semaphores(nc, ctx)
        sb = lambda n, s: ctx.enter_context(nc.sbuf_tensor(n, s, F32))
        wba = sb("wba", [128, 2, 32])
        bg = sb("bg", [32, 2, NTOK])
        turned = sb("bg_turned", [32, 2, NTOK])
        small = sb("small", [32, 3, NH])
        z, m, e, s, s2, p = (sb("sp_" + n, [32, NTOK // TC, NH]) for n in ("z", "m", "e", "s", "s2", "p"))
        ps = [[ctx.enter_context(nc.psum_tensor(f"bg{i}{j}", [32, TILE], F32)) for j in range(2)] for i in range(2)]
        sem = new_sem
        w_in, w_zero, mm, kept, chain, ex, al = (sem(n) for n in ("bg_w", "bg_zero", "bg_mm", "bg_kept", "bg_chain", "bg_exp", "bg_alog"))
        block = ctx.enter_context(nc.Block())

        @block.sync
        def _(sp):
            sp.wait_ge(w_zero, 1)
            sp.dma_start(wba[:, 0, 0:NHH * NH], g.dram["Wb"]).then_inc(w_in, 16)
            sp.dma_start(wba[:, 1, 0:NH], g.dram["Wa"]).then_inc(w_in, 16)
            sp.dma_start(small[:, 0, :], g.dram["dt_bias"].partition_broadcast(32)).then_inc(w_in, 16)
            sp.dma_start(small[:, 1, :], g.dram["A_log"].partition_broadcast(32)).then_inc(w_in, 16)

        @block.tensor
        def _(pe):
            pe.wait_ge(w_in, 64)
            for i in range(NT):
                if i >= 2:
                    pe.wait_ge(kept, i - 1)
                rhs = g.xn[:, i // 2, PAD + TILE * (i % 2):PAD + TILE * (i % 2 + 1)]
                for j in range(2):
                    last = nc.tensor.matmul(ps[j][i % 2][:, :], wba[:, j, :], rhs, start=True, stop=True)
                last.then_inc(mm, 1)

        @block.scalar
        def _(act):
            for i in range(NT):
                act.wait_ge(mm, i + 1)
                nc.scalar.activation(bg[:, 0, TILE * i:TILE * (i + 1)], ps[0][i % 2][:, :], ACT.Sigmoid)
                nc.scalar.activation(bg[:, 1, TILE * i:TILE * (i + 1)], ps[1][i % 2][:, :], ACT.Copy).then_inc(kept, 1)
            act.wait_ge(w_in, 64)
            nc.scalar.activation(small[:, 2, :], small[:, 1, :], ACT.Exp).then_inc(al, 1)
            act.wait_ge(chain, 3)
            nc.scalar.activation(e[:, :, :], e[:, :, :], ACT.Exp).then_inc(ex, 1)

        @block.vector
        def _(dve):
            nc.vector.memset(wba[:, :, :], 0.0).then_inc(w_zero, 1)
            n = [0]

            def link(ins):
                n[0] += 1
                ins.then_inc(chain, 1)
                dve.wait_ge(chain, n[0])

            dve.wait_ge(kept, NT)
            nc.vector.transpose(turned[:, 0, :], bg[:, 0, :])
            link(nc.vector.transpose(turned[:, 1, :], bg[:, 1, :]))
            dve.wait_ge(w_in, 64)
            a = turned[:, 1, :].rearrange("t (k r) -> t k r", r=32)[:, :, 0:NH]
            bias = small[:, 0, :].unsqueeze(1).broadcast_to([32, NTOK // TC, NH])
            link(nc.vector.tensor_tensor(z[:, :, :], a, bias, ALU.add))
            link(nc.vector.scalar_tensor_tensor(e[:, :, :], z[:, :, :], -1.0, z[:, :, :], ALU.mult, ALU.min))
            for i in range(NHH):
                bt = turned[:, 0, :].rearrange("t (k r) -> t r k", r=32)[:, NH * i:NH * (i + 1), :]
                nc.vector.tensor_scalar(g.beta[TC * i:TC * (i + 1), :, :], bt, 2.0, None, ALU.mult)
            link(nc.vector.tensor_scalar(m[:, :, :], z[:, :, :], 0.0, None, ALU.max))
            dve.wait_ge(ex, 1)
            link(nc.vector.tensor_scalar(s[:, :, :], e[:, :, :], 2.0, None, ALU.add))
            link(nc.vector.reciprocal(s[:, :, :], s[:, :, :]))
            link(nc.vector.tensor_tensor(s[:, :, :], s[:, :, :], e[:, :, :], ALU.mult))
            link(nc.vector.tensor_tensor(s2[:, :, :], s[:, :, :], s[:, :, :], ALU.mult))
            link(nc.vector.tensor_scalar(p[:, :, :], s2[:, :, :], 2.0 / 17, 2.0 / 15, ALU.mult, ALU.add))
            for c in (13, 11, 9, 7, 5, 3, 1):
                link(nc.vector.tensor_tensor(p[:, :, :], p[:, :, :], s2[:, :, :], ALU.mult))
                link(nc.vector.tensor_scalar(p[:, :, :], p[:, :, :], 2.0 / c, None, ALU.add))
            link(nc.vector.tensor_tensor(p[:, :, :], p[:, :, :], s[:, :, :], ALU.mult))
            link(nc.vector.tensor_tensor(p[:, :, :], p[:, :, :], m[:, :, :], ALU.add))
            dve.wait_ge(al, 1)
            ea = small[:, 2, :].unsqueeze(1).broadcast_to([32, NTOK // TC, NH])
            nc.vector.scalar_tensor_tensor(g.gt[:, :, :], p[:, :, :], -1.0, ea, ALU.mult, ALU.mult)


def delta_attention(nc, g):
    with ExitStack() as ctx:
        new_sem = semaphores(nc, ctx)
        sb = lambda n, s, dt=F32: ctx.enter_context(nc.sbuf_tensor(n, s, dt))
        stage_w = sb("stage_w", [128, 9, 128])
        stage_c = sb("stage_c", [128, 7, 128, TAPS])
        wt = sb("wt", [128, 7, TAPS, 128])
        wgo = sb("wgo", [128, 2, 128])
        rmsw = sb("rmsw", [128, 1])
        edec = sb("edec", [R, B, T])
        gdec = sb("gdec", [128, B, T])
        kqs = sb("kqs", [128, 4, U, 4, TC])
        kq = [kqs[:, i] for i in range(2)]
        vt = [sb(f"vt{i}", [128, U, NHH, TC]) for i in range(2)]
        gate = [sb(f"gate{i}", [128, U, TC]) for i in range(2)]
        kqg = [kqs[:, 2 + i] for i in range(2)]
        gm = kqs[0:TC].rearrange("p a u i t -> p (a u i) t")
        ksq = sb("ksq", [R, U, 128])
        ksum = sb("ksum", [R, U])
        sqq = sb("sqq", [128, NCC, B, TC])
        ss = sb("ss", [R, U])
        rk = [sb(f"rk{i}", [R, U]) for i in range(2)]
        rinv = sb("rinv", [R, U])
        step_s = sb("step_s", [R, U])
        q2 = [sb(f"q2{i}", [128, NCC]) for i in range(2)]
        es = [sb(f"es{i}", [R, U, TC]) for i in range(2)]
        es4 = sb("es4", [R, U, 4, TC])
        krow = [sb(f"krow{i}", [R, U, 128]) for i in range(2)]
        vrow = [sb(f"vrow{i}", [R, U, 128]) for i in range(2)]
        ap = [sb(f"ap{i}", [R, U, 128]) for i in range(2)]
        ix = sb("ix", [R, U, R])
        ar = sb("ar", [R, U, R], F16)
        al = sb("al", [R, U, R], F16)
        Xr = sb("Xr", [R, U, R], F16)
        Yr = sb("Yr", [R, U, R], F16)
        Zr = sb("Zr", [R, U, R], F16)
        ident_r = sb("ident_r", [R, R], F16)
        ident_h = sb("ident_h", [R, HU, R], F16)
        yf = [sb(f"yf{i}", [R, U, R]) for i in range(2)]
        S = sb("S", [128, B, 128])
        rhs = sb("rhs", [R, B, 128])
        ws = sb("ws", [R, B, 128])
        mo = sb("mo", [128, NCC])
        fo = sb("fo", [128, NCC])
        osq = sb("osq", [128, 128])
        osb = sb("osb", [128, NCC, 128])
        og = sb("og", [128, NCC, 128])

        PP = [ctx.enter_context(nc.psum_tensor(f"PP{i}", [128, TILE], F32)) for i in range(2)]
        G2 = ctx.enter_context(nc.psum_tensor("G2", [128, 2, TILE], F32))
        L2 = ctx.enter_context(nc.psum_tensor("L2", [128, 2, TILE], F32))
        RA = ctx.enter_context(nc.psum_tensor("RA", [128, TILE], F32))
        RB = ctx.enter_context(nc.psum_tensor("RB", [128, TILE], F32))
        side = L2[:, 1, 384:512]

        QS = 5
        evs = []

        def ev(name):
            s = new_sem(name)
            evs.append(s)
            return s

        proj = [ev(f"proj_mm{q}") for q in range(4)]
        silu = [ev(f"silu{q}") for q in range(4)]
        rk_ev, ss_ev, sq_ev, qs_mm, q2_ev, rinv_ev, s_ev, es_ev, es4_ev = (ev(n) for n in ("rk_ready", "ss_ready", "sq_ready", "qs_mm", "q2_ready", "rinv_ready", "step_s_ready", "es_ready", "es4_ready"))
        ktr_mm, vtr_mm, gram_mm, kr_ev, vr_ev, ap_ev, ar_ev, al_ev = (
            [ev(f"{n}{hf}") for hf in range(2)] for n in ("ktr_mm", "vtr_mm", "gram_mm", "krow_ready", "vrow_ready", "ap_ready", "ar_ready", "al_ready"))
        kqg_ev = ev("kqg_ready")
        n_ev = ev("n_ready")
        ksum_ev = ev("ksum_ready")
        z_mm, z_ev, x_mm, x_ev, y_mm, y_ev = ([ev(f"{n}{l}") for l in range(LEVELS)] for n in ("z_mm", "z_ready", "x_mm", "x_ready", "y_mm", "y_ready"))
        m_mm, ix_ev, r_ev, yf_mm, yf_ev = ([ev(f"{n}{hf}") for hf in range(2)] for n in ("m_mm", "ix_ready", "resid_ready", "yf_mm", "yf_ready"))
        ks_mm, rhs_ev, w_mm, w_ev, s_mm, o_mm, sup_ev, mo_ev, fs_ev, fo_ev, osb_ev, ot_mm, og_ev, out_mm, acc_ev = (
            [ev(f"{n}{c}") for c in range(NCC)] for n in ("ks_mm", "rhs_ready", "w_mm", "w_ready", "snew_mm", "o_mm", "state_ready", "osum_ready", "osum_eps_ready", "oscale_ready", "o_ready", "ot_mm", "og_ready", "out_mm", "acc_ready"))
        staged, wt_ready, gm_ready, zero_ready, rms_ready, identr_ready = (new_sem(n) for n in ("staged", "wt_ready", "gm_ready", "state_zeroed", "rms_ready", "identr_ready"))
        e_mm, g_mm, e_ex, g_ex = (new_sem(n) for n in ("e_mm", "g_mm", "e_exp", "g_exp"))

        with nc.Block() as b0:
            @b0.gpsimd
            def _(pool):
                for s in evs:
                    pool.sem_inc(s, CREDIT)

        NDMA = 7
        block = ctx.enter_context(nc.Block())
        LAST = KSTEPS - 1

        def weave(order, segs, base, k, par, now):
            shift = {"P": 1, "I": 0, "R": -1}
            for part, name, *args in order:
                if part in now and name in segs:
                    d = shift[part]
                    segs[name](base + k + d, k + d, (par + d) % 2, now, *args)

        def program(eng, order, segs, prep):
            with eng.Fori(0, NH) as h:
                prep(h)
                base = h * KSTEPS
                weave(order, segs, base, -1, 1, "P")
                weave(order, segs, base, 0, 0, "PI")
                with eng.Fori(0, (KSTEPS - 2) // 2) as j:
                    weave(order, segs, base, j * 2 + 1, 1, "PIR")
                    weave(order, segs, base, j * 2 + 2, 0, "PIR")
                weave(order, segs, base, LAST, LAST % 2, "IR")
                weave(order, segs, base, LAST + 1, (LAST + 1) % 2, "R")

        both = lambda name, *args: [("I", name, *args, hf) for hf in range(2)]
        ORDER = [
            ("R", "ks", 0), *both("gram"), *both("ap"), ("R", "rhs", 0), *both("vtr"), *both("ar"), *both("n"), ("R", "w", 0), ("R", "wev", 0),
            *both("vr"), ("P", "pt", 0, 0, 0),
            *both("z", 0), *both("zev", 0), ("R", "so", 0), ("R", "sup", 0), ("R", "mo", 0), ("R", "fo", 0), *both("al"), ("I", "kqg"), ("P", "pt", 0, 0, 1),
            *both("x", 0), *both("xev", 0), *both("y", 0), *both("yev", 0), ("P", "pt", 0, 1, 0), ("R", "osb", 0), ("R", "ks", 1), ("R", "rhs", 1),
            ("R", "ot", 0), *both("z", 1), *both("zev", 1), ("R", "og", 0), ("P", "pt", 0, 1, 1), ("P", "silu", 0), ("R", "w", 1), ("R", "wev", 1),
            *both("x", 1), *both("xev", 1), *both("y", 1), *both("yev", 1), ("P", "pt", 1, 0, 0),
            ("R", "out", 0), *both("z", 2), *both("zev", 2), ("R", "acc", 0), ("R", "so", 1), ("R", "sup", 1), ("R", "mo", 1), ("R", "fo", 1),
            *both("x", 2), *both("xev", 2), *both("y", 2), *both("yev", 2), ("P", "pt", 1, 0, 1), ("P", "pt", 1, 1, 0), ("R", "osb", 1),
            ("R", "ot", 1), *both("z", 3), *both("zev", 3), ("R", "og", 1), ("P", "pt", 1, 1, 1), ("P", "silu", 1), ("P", "sq"),
            *both("x", 3), *both("xev", 3), *both("y", 3), *both("yev", 3), ("P", "pt", 2, 0, 0), ("P", "pt", 2, 0, 1),
            ("R", "out", 1), *both("z", 4), *both("zev", 4), ("R", "acc", 1), ("P", "pt", 2, 1, 0),
            *both("x", 4), *both("xev", 4), *both("y", 4), *both("yev", 4), ("P", "pt", 2, 1, 1), ("P", "silu", 2),
            ("P", "qs"), *both("z", 5), *both("zev", 5), ("P", "q2"), ("P", "pt", 3, 0, 0), ("P", "pt", 3, 0, 1), ("P", "pt", 3, 1, 0), ("P", "silu", 3), ("P", "ktr", 0), ("P", "ksum", 0),
            *both("x", 5), *both("xev", 5), *both("ix"), *both("y", 5), *both("yev", 5), ("P", "ktr", 1), ("P", "ksum", 1),
            *both("m"), *both("res"), ("P", "sc"), *both("yf"), *both("yfev"), ("P", "es4", 0), ("P", "es4", 1), ("P", "rk"), ("P", "kr", 0), ("P", "kr", 1),
        ]

        def bank(ps, hf, n=R):
            return ps[0:R, hf, 0:HU * n].rearrange("p (c n) -> p c n", n=n)

        def half(t, hf):
            return t[:, hf * HU:(hf + 1) * HU]

        def slot(ps, u, n):
            return ps[0:R, u // HU, (u % HU) * n:(u % HU + 1) * n]

        def kslot(u):
            return PP[u // HU][0:R, (u % HU) * 128:(u % HU + 1) * 128]

        def units_of(hf):
            return range(hf * HU, (hf + 1) * HU)

        @block.sync
        def _(sp):
            with sp.Fori(0, NH) as h:
                sp.wait_ge(wt_ready, h + 1)
                col = lambda w, n: g.dram[w].rearrange("d (i x c) -> d x i c", x=NH, c=128)[:, bass.ds(h, 1), :, :]
                sp.dma_start(stage_w[:, 0:3, :].unsqueeze(1), col("Wk", 3)).then_inc(staged, 16)
                sp.dma_start(stage_w[:, 3:4, :].unsqueeze(1), col("Wq", 1)).then_inc(staged, 16)
                sp.dma_start(stage_w[:, 4:7, :].unsqueeze(1), col("Wv", 3)).then_inc(staged, 16)
                sp.dma_start(stage_w[:, 7:8, :].unsqueeze(1), col("Wg", 1)).then_inc(staged, 16)
                sp.dma_start(stage_w[:, 8, :], g.dram["Wo"][bass.ds(h * 128, 128), :]).then_inc(staged, 16)
                tap = lambda w: g.dram[w].rearrange("(i x c) k -> x i (c k)", x=NH, c=128)
                for i in range(3):
                    sp.dma_start(stage_c[:, i, :, :], tap("conv_k")[bass.ds(h, 1), i, :].rearrange("a n -> (a n)").partition_broadcast(128)).then_inc(staged, 16)
                    sp.dma_start(stage_c[:, 4 + i, :, :], tap("conv_v")[bass.ds(h, 1), i, :].rearrange("a n -> (a n)").partition_broadcast(128)).then_inc(staged, 16)
                sp.dma_start(stage_c[:, 3, :, :], tap("conv_q")[bass.ds(h, 1), 0, :].rearrange("a n -> (a n)").partition_broadcast(128)).then_inc(staged, 16)

        @block.gpsimd
        def _(pool):
            def prep(h):
                pool.wait_ge(g_ex, h * 4 + 4)

            def s_sq(N, k, par, now):
                pool.wait_ge(silu[1], done(N))
                pool.wait_ge(qs_mm, done(N - 1))
                qv = kq[par][:, :, 3, :].rearrange("p (b c) t -> p b c t", c=NCC)
                nc.gpsimd.tensor_tensor(sqq[:, :, :, :].rearrange("p c b t -> p b c t"), qv, qv, ALU.mult).then_inc(sq_ev, 1)

            def s_es4(N, k, par, now, hf):
                pool.wait_ge(es_ev, done(N))
                pool.wait_ge(ap_ev[hf], done(N - 1))
                nc.gpsimd.tensor_tensor(half(es4, hf), half(es[par], hf).unsqueeze(2).broadcast_to([R, HU, 4, TC]),
                                        g.mask4[:, :].rearrange("p (i t) -> p i t", i=4).unsqueeze(1).broadcast_to([R, HU, 4, TC]), ALU.mult).then_inc(es4_ev, 1)

            def s_kqg(N, k, par, now):
                pool.wait_ge(o_mm[1], done(N - 2))
                kv = kq[par][:, :, :, :].rearrange("p (b c) i t -> p b c i t", c=NCC)
                ov = kqg[par][:, :, :, :].rearrange("p (b c) i t -> p b c i t", c=NCC)
                for cc in range(NCC):
                    d = gdec[:, :, bass.ds(k * SPAN + cc * TC, TC)].unsqueeze(2).broadcast_to([128, B, 4, TC])
                    last = nc.gpsimd.tensor_tensor(ov[:, :, cc], kv[:, :, cc], d, ALU.mult)
                last.then_inc(kqg_ev, 1)

            def s_rk(N, k, par, now):
                pool.wait_ge(ss_ev, done(N))
                pool.wait_ge(vr_ev[1], done(N - 2))
                nc.gpsimd.tensor_tensor(rk[par][:, :], ss[:, :], g.half[0:R, :], ALU.pow).then_inc(rk_ev, 1)

            def s_fo(N, k, par, now, cc):
                pool.wait_ge(mo_ev[cc], done(N))
                pool.wait_ge(osb_ev[cc], done(N - 1))
                nc.gpsimd.tensor_tensor(fo[:, cc:cc + 1], mo[:, cc:cc + 1], q2[par][:, cc:cc + 1], ALU.add).then_inc(fs_ev[cc], 1)
                pool.wait_ge(fs_ev[cc], done(N))
                nc.gpsimd.tensor_tensor(fo[:, cc:cc + 1], fo[:, cc:cc + 1], g.minus_half[:, 0:1], ALU.pow).then_inc(fo_ev[cc], 1)

            def s_al(N, k, par, now, hf):
                pool.wait_ge(ar_ev[hf], done(N))
                pool.wait_ge(m_mm[hf], done(N - 1))
                nc.gpsimd.tensor_tensor(half(al, hf), half(ap[par], hf)[:, :, 0:R], half(ar, hf), ALU.subtract).then_inc(al_ev[hf], 1)

            def s_n(N, k, par, now, hf):
                pool.wait_ge(ar_ev[hf], done(N))
                pool.wait_ge(yf_ev[hf], done(N - 1))
                nc.gpsimd.tensor_tensor(half(Yr, hf), half(ar, hf), g.lev[:, LEVELS * R:].unsqueeze(1).broadcast_to([R, HU, R]), ALU.mult).then_inc(n_ev, 1)

            def s_ix(N, k, par, now, hf):
                pool.wait_ge(x_ev[LEVELS - 1], done_half(N, hf))
                pool.wait_ge(r_ev[hf], done(N - 1))
                nc.gpsimd.tensor_tensor(half(ix, hf), g.ident[0:R, 0:R].unsqueeze(1).broadcast_to([R, HU, R]), half(Xr, hf), ALU.subtract).then_inc(ix_ev[hf], 1)

            program(pool, ORDER, {"n": s_n, "sq": s_sq, "rk": s_rk, "fo": s_fo, "es4": s_es4, "al": s_al, "kqg": s_kqg, "ix": s_ix}, prep)

        @block.scalar
        def _(act):
            def prep(h):
                for i in range(4):
                    act.wait_ge(e_mm, h * 4 + i + 1)
                    nc.scalar.activation(edec[:, i, :].rearrange("p (a n) -> p a n", a=2), G2[0:R, :, :], ACT.Exp).then_inc(e_ex, 1)
                    act.wait_ge(g_mm, h * 4 + i + 1)
                    nc.scalar.activation(gdec[:, i, :].rearrange("p (a n) -> p a n", a=2), L2[:, :, :], ACT.Exp).then_inc(g_ex, 1)

            def s_silu(N, k, par, now, q):
                act.wait_ge(proj[q], done(N))
                src = PP[q % 2][:, :].rearrange("p (a u t) -> p a u t", a=2, t=TC)
                if q == 0:
                    act.wait_ge(kqg_ev, done(N - 2))
                    nc.scalar.activation(kq[par][:, :, 0:2, :].rearrange("p u i t -> p i u t"), src, ACT.Silu).then_inc(silu[q], 1)
                elif q == 1:
                    nc.scalar.activation(kq[par][:, :, 2:4, :].rearrange("p u i t -> p i u t"), src, ACT.Silu).then_inc(silu[q], 1)
                elif q == 2:
                    act.wait_ge(vtr_mm[1], done(N - 2))
                    nc.scalar.activation(vt[par][:, :, 0:2, :].rearrange("p u i t -> p i u t"), src, ACT.Silu).then_inc(silu[q], 1)
                else:
                    nc.scalar.activation(vt[par][:, :, 2, :], src[:, 0], ACT.Silu)
                    act.wait_ge(og_ev[1], done(N - 2))
                    nc.scalar.activation(gate[par][:, :, :], src[:, 1], ACT.Silu).then_inc(silu[q], 1)

            def s_xev(N, k, par, now, l, hf):
                act.wait_ge(x_mm[l], done_half(N, hf))
                if l == 0:
                    act.wait_ge(ix_ev[hf], done(N - 1))
                nc.scalar.activation(half(Xr, hf), bank(L2, hf), ACT.Copy).then_inc(x_ev[l], 1)

            def s_ar(N, k, par, now, hf):
                act.wait_ge(ap_ev[hf], done(N))
                act.wait_ge(m_mm[hf], done(N - 1))
                act.wait_ge(al_ev[hf], done(N - 1))
                nc.scalar.activation(half(ar, hf), half(ap[par], hf)[:, :, 0:R], ACT.Copy).then_inc(ar_ev[hf], 1)

            def s_ksum(N, k, par, now, hf):
                act.wait_ge(ktr_mm[hf], done(N))
                act.wait_ge(ss_ev, done(N - 1))
                for u in units_of(hf):
                    last = nc.scalar.activation(ksq[:, u, :], kslot(u), ACT.Square, accum_out=ksum[:, u:u + 1])
                last.then_inc(ksum_ev, 1)

            def s_wev(N, k, par, now, cc):
                act.wait_ge(w_mm[cc], done(N))
                nc.scalar.activation(ws[:, :, :], RB[0:R, :].rearrange("p (b n) -> p b n", b=B), ACT.Copy).then_inc(w_ev[cc], 1)

            def s_mo(N, k, par, now, cc):
                act.wait_ge(o_mm[cc], done(N))
                act.wait_ge(fo_ev[1 - cc], done(N) if cc else done(N - 1))
                nc.scalar.activation(osq[:, :], RB[:, 0:128], ACT.Square, accum_out=mo[:, cc:cc + 1]).then_inc(mo_ev[cc], 1)

            program(act, ORDER, {"ksum": s_ksum, "silu": s_silu, "ar": s_ar, "xev": s_xev, "wev": s_wev, "mo": s_mo}, prep)

        @block.vector
        def _(dve):
            dve.wait_ge(g.rms_sem, 16)
            nc.vector.tensor_scalar(rmsw[:, :], g.rms_in[:, :], math.sqrt(128.0), None, ALU.mult).then_inc(rms_ready, 1)
            dve.wait_ge(rms_ready, 1)
            nc.vector.tensor_copy(ident_r[:, :], g.ident[0:R, 0:R])
            nc.vector.tensor_copy(ident_h[:, :, :], g.ident[0:R, 0:R].unsqueeze(1).broadcast_to([R, HU, R])).then_inc(identr_ready, 1)
            nc.vector.memset(stage_w[:, 0, 0:1], 0.0).then_inc(wt_ready, 1)

            def prep(h):
                dve.wait_ge(staged, (h + 1) * (16 * (5 + 7)))
                dve.wait_ge(out_mm[1], done(h * KSTEPS - 1))
                nc.vector.tensor_tensor(wt[:, :, :, :], stage_w[:, 0:7, :].unsqueeze(2).broadcast_to([128, 7, TAPS, 128]),
                                        stage_c[:, :, :, :].rearrange("p a c k -> p a k c"), ALU.mult)
                nc.vector.tensor_copy(wgo[:, :, :], stage_w[:, 7:9, :]).then_inc(wt_ready, 1)
                nc.vector.memset(S[:, :, :], 0.0).then_inc(zero_ready, 1)
                nc.vector.tensor_tensor(gm[:, :, :], g.gt[:, :, bass.ds(h, 1)].broadcast_to([TC, NTOK // TC, TC]),
                                        g.upto[:, :].unsqueeze(1).broadcast_to([TC, NTOK // TC, TC]), ALU.mult).then_inc(gm_ready, 1)
                dve.wait_ge(g_ex, h * 4 + 4)

            cur = Shared()

            def prep_h(h):
                cur.h = h
                prep(h)

            def s_q2(N, k, par, now):
                dve.wait_ge(qs_mm, done(N))
                dve.wait_ge(fs_ev[1], done(N - 2))
                nc.vector.tensor_scalar(q2[par][:, :], L2[:, 1, 384:384 + NCC], 1e-5 * 128 * 128, 1e-6 * 1e-5 * 128 * 128, ALU.mult, ALU.add).then_inc(q2_ev, 1)

            def s_sc(N, k, par, now):
                dve.wait_ge(ksum_ev, done_half(N, 1))
                dve.wait_ge(rk_ev, done(N - 1))
                nc.vector.tensor_scalar(ss[:, :], ksum[:, :], 1e-6, None, ALU.add).then_inc(ss_ev, 1)
                dve.wait_ge(ss_ev, done(N))
                nc.vector.reciprocal(rinv[:, :], ss[:, :]).then_inc(rinv_ev, 1)
                dve.wait_ge(rinv_ev, done(N))
                nc.vector.tensor_tensor(step_s[:, :].rearrange("p (b c) -> p b c", c=NCC), rinv[:, :].rearrange("p (b c) -> p b c", c=NCC),
                                        g.beta[:, bass.ds(cur.h, 1), :].rearrange("p x (b c) -> p (x b) c", b=B)[:, :, bass.ds(k * NCC, NCC)], ALU.mult).then_inc(s_ev, 1)
                dve.wait_ge(s_ev, done(N))
                nc.vector.tensor_tensor(es[par][:, :, :].rearrange("p (b c) t -> p b c t", c=NCC),
                                        edec[:, :, bass.ds(k * SPAN, SPAN)].rearrange("p b (c t) -> p b c t", c=NCC),
                                        step_s[:, :].rearrange("p (b c) -> p b c", c=NCC).unsqueeze(3).broadcast_to([R, B, NCC, TC]), ALU.mult).then_inc(es_ev, 1)

            def s_kr(N, k, par, now, hf):
                dve.wait_ge(ktr_mm[hf], done(N))
                dve.wait_ge(es_ev, done(N))
                dve.wait_ge(s_mm[1], done(N - 2))
                nc.vector.tensor_tensor(half(krow[par], hf), PP[hf][0:R, :].rearrange("p (c n) -> p c n", n=128), half(es[par], hf)[:, :, TC - 1:TC].broadcast_to([R, HU, 128]), ALU.mult).then_inc(kr_ev[hf], 1)

            def s_vr(N, k, par, now, hf):
                dve.wait_ge(vtr_mm[hf], done(N))
                dve.wait_ge(rk_ev, done(N))
                nc.vector.tensor_tensor(half(vrow[par], hf), bank(L2, hf, 128), half(rk[par], hf).unsqueeze(2).broadcast_to([R, HU, 128]), ALU.mult).then_inc(vr_ev[hf], 1)

            def s_ap(N, k, par, now, hf):
                dve.wait_ge(gram_mm[hf], done(N))
                dve.wait_ge(es4_ev, done_half(N, hf))
                dve.wait_ge(o_mm[1], done(N - 2))
                nc.vector.tensor_tensor(half(ap[par], hf), bank(G2, hf, 128), half(es4, hf).rearrange("p u i t -> p u (i t)"), ALU.mult).then_inc(ap_ev[hf], 1)

            def s_zev(N, k, par, now, l, hf):
                dve.wait_ge(z_mm[l], done_half(N, hf))
                mask = g.lev[:, l * R:(l + 1) * R].unsqueeze(1).broadcast_to([R, HU, R])
                nc.vector.tensor_tensor(half(Zr, hf), bank(L2, hf), mask, ALU.mult).then_inc(z_ev[l], 1)

            def s_yev(N, k, par, now, l, hf):
                dve.wait_ge(y_mm[l], done_half(N, hf))
                old = g.ident[0:R, 0:R].unsqueeze(1).broadcast_to([R, HU, R]) if l == 0 else half(Yr, hf)
                nc.vector.tensor_tensor(half(Yr, hf), bank(G2, hf), old, ALU.add).then_inc(y_ev[l], 1)

            def s_res(N, k, par, now, hf):
                dve.wait_ge(m_mm[hf], done(N))
                dve.wait_ge(ix_ev[hf], done(N))
                nc.vector.tensor_tensor(half(Zr, hf), half(ix, hf), bank(L2, hf), ALU.subtract).then_inc(r_ev[hf], 1)

            def s_yfev(N, k, par, now, hf):
                dve.wait_ge(yf_mm[hf], done(N))
                nc.vector.tensor_tensor(half(yf[par], hf), bank(G2, hf), half(Yr, hf), ALU.add).then_inc(yf_ev[hf], 1)

            def s_rhs(N, k, par, now, cc):
                dve.wait_ge(ks_mm[cc], done(N))
                v = vrow[par][:, :, :].rearrange("p (b c) n -> p b c n", c=NCC)[:, :, cc, :]
                nc.vector.tensor_tensor(rhs[:, :, :], v, RA[0:R, :].rearrange("p (b n) -> p b n", b=B), ALU.subtract).then_inc(rhs_ev[cc], 1)

            def s_sup(N, k, par, now, cc):
                dve.wait_ge(s_mm[cc], done(N))
                dve.wait_ge(o_mm[cc], done(N))
                for b in range(B):
                    last = nc.vector.scalar_tensor_tensor(S[:, b, :], S[:, b, :], gdec[:, b, bass.ds(k * SPAN + cc * TC + TC - 1, 1)],
                                                          RA[:, b * 128:(b + 1) * 128], ALU.mult, ALU.add)
                last.then_inc(sup_ev[cc], 1)

            def s_osb(N, k, par, now, cc):
                dve.wait_ge(fo_ev[cc], done(N))
                nc.vector.tensor_scalar(osb[:, cc, :], RB[:, 0:128], fo[:, cc:cc + 1], None, ALU.mult).then_inc(osb_ev[cc], 1)

            def s_og(N, k, par, now, cc):
                dve.wait_ge(ot_mm[cc], done(N))
                gv = gate[par][:, :, :].rearrange("p (b c) t -> p b c t", c=NCC)[:, :, cc, :]
                nc.vector.scalar_tensor_tensor(og[:, cc, :].rearrange("p (b t) -> p b t", b=B), side.rearrange("p (b t) -> p b t", b=B),
                                               rmsw[:, :], gv, ALU.mult, ALU.mult).then_inc(og_ev[cc], 1)

            def s_acc(N, k, par, now, cc):
                dve.wait_ge(out_mm[cc], done(N))
                x = g.xT[:, :, bass.ds(k * SPAN + cc * TC, TC)]
                nc.vector.tensor_tensor(x, side.rearrange("p (b t) -> p b t", b=B), x, ALU.add).then_inc(acc_ev[cc], 1)

            program(dve, ORDER, {"q2": s_q2, "sc": s_sc, "kr": s_kr, "vr": s_vr, "ap": s_ap, "zev": s_zev, "yev": s_yev, "res": s_res,
                                 "yfev": s_yfev, "rhs": s_rhs, "sup": s_sup, "osb": s_osb, "og": s_og, "acc": s_acc}, prep_h)

        @block.tensor
        def _(pe):
            mm = nc.tensor.matmul
            pe.wait_ge(identr_ready, 1)

            def prep(h):
                pe.wait_ge(gm_ready, h + 1)
                pe.wait_ge(acc_ev[1], done(h * KSTEPS - 1))
                pe.wait_ge(yf_ev[1], done(h * KSTEPS - 1))
                for i in range(4):
                    pe.wait_ge(e_ex, h * 4 + i) if i else None
                    for a in range(2):
                        last = mm(G2[0:R, a, :], g.after[:, :], gm[:, bass.ds(32 * i + 16 * a, 16), :], start=True, stop=True)
                    last.then_inc(e_mm, 1)
                    pe.wait_ge(g_ex, h * 4 + i) if i else None
                    for a in range(2):
                        last = mm(L2[:, a, :], g.ones[0:TC, :], gm[:, bass.ds(32 * i + 16 * a, 16), :], start=True, stop=True)
                    last.then_inc(g_mm, 1)
                pe.wait_ge(wt_ready, h + 2)
                pe.wait_ge(zero_ready, h + 1)
                pe.wait_ge(e_ex, h * 4 + 4)
                pe.wait_ge(g_ex, h * 4 + 4)

            def s_pt(N, k, par, now, q, a, part):
                if part or a:
                    pass
                elif q < 2:
                    pe.wait_ge(kr_ev[q], done(N - 1))
                else:
                    pe.wait_ge(silu[q - 2], done(N))
                tile = 2 * q + a
                out = PP[q % 2][:, a * 256:(a + 1) * 256].rearrange("p (b t) -> p b t", b=B)
                if tile < 7:
                    for tap in range(part * TAPS // 2, (part + 1) * TAPS // 2):
                        last = mm(out, wt[:, tile, tap, :], g.xn[:, :, bass.ds(k * SPAN + tap, SPAN)], start=tap == 0, stop=tap == TAPS - 1)
                else:
                    last = mm(out, wgo[:, 0, :], g.xn[:, :, bass.ds(k * SPAN + PAD, SPAN)], start=True, stop=True)
                if tile == 7 or (a and part):
                    last.then_inc(proj[q], 1)

            def s_ktr(N, k, par, now, hf):
                pe.wait_ge(silu[1], done(N))
                pe.wait_ge(silu[2 + hf], done(N))
                for u in units_of(hf):
                    last = nc.tensor.transpose(kslot(u), kq[par][:, u, 0:3, :].rearrange("p i t -> p (i t)"), g.ident[:, :])
                last.then_inc(ktr_mm[hf], 1)

            def s_qs(N, k, par, now):
                pe.wait_ge(sq_ev, done(N))
                if "I" in now:
                    pe.wait_ge(x_ev[QS - 1], done_half(N - 1, 1))
                for cc in range(NCC):
                    last = mm(L2[:, 1, 384 + cc:385 + cc], sqq[:, cc, :, :].rearrange("p b t -> p (b t)"), g.ones[:, 0:1], start=True, stop=True)
                last.then_inc(qs_mm, 1)

            def s_vtr(N, k, par, now, hf):
                pe.wait_ge(silu[3], done(N))
                pe.wait_ge(q2_ev, done(N))
                pe.wait_ge(r_ev[hf], done(N - 1))
                for u in units_of(hf):
                    last = nc.tensor.transpose(slot(L2, u, 128), vt[par][:, u, :, :].rearrange("p i t -> p (i t)"), g.ident[:, :])
                last.then_inc(vtr_mm[hf], 1)

            def s_gram(N, k, par, now, hf):
                pe.wait_ge(yf_ev[hf], done(N - 1))
                for u in units_of(hf):
                    v = kq[par][:, u, :, :].rearrange("p i t -> p (i t)")
                    last = mm(slot(G2, u, 128), v[:, 0:R], v, start=True, stop=True)
                last.then_inc(gram_mm[hf], 1)

            def s_z(N, k, par, now, l, hf):
                if l:
                    pe.wait_ge(x_ev[l - 1], done_half(N, hf))
                else:
                    pe.wait_ge(ar_ev[hf], done(N))
                    pe.wait_ge(vr_ev[hf], done(N))
                for u in units_of(hf):
                    last = mm(slot(L2, u, R), ar[:, u, :], ident_r[:, :] if l == 0 else Xr[:, u, :], start=True, stop=True)
                last.then_inc(z_mm[l], 1)

            def s_x(N, k, par, now, l, hf):
                pe.wait_ge(z_ev[l], done_half(N, hf))
                if l:
                    pe.wait_ge(y_ev[l - 1], done_half(N, hf))
                if "R" in now and 0 < l < 5 and hf == 1:
                    pe.wait_ge((og_ev[0], acc_ev[0], og_ev[1], acc_ev[1])[l - 1], done(N - 1))
                if "P" in now and l == QS and hf == 1:
                    pe.wait_ge(q2_ev, done(N + 1))
                mm(bank(L2, hf), ident_r[:, :], ident_h[:, :, :] if l == 0 else half(Xr, hf), start=True, stop=False)
                if l == 0:
                    pe.wait_ge(n_ev, done_half(N, hf))
                    mm(bank(L2, hf), ident_r[:, :], half(Zr, hf), start=False, stop=False)
                for u in units_of(hf):
                    last = mm(slot(L2, u, R), Yr[:, u, :], Zr[:, u, :], start=False, stop=u % HU == HU - 1)
                last.then_inc(x_mm[l], 1)

            def s_y(N, k, par, now, l, hf):
                if l == 0:
                    mm(bank(G2, hf), ident_r[:, :], half(Yr, hf), start=True, stop=False)
                for u in units_of(hf):
                    last = mm(slot(G2, u, R), Zr[:, u, :], Yr[:, u, :], start=l > 0, stop=l > 0 or u % HU == HU - 1)
                last.then_inc(y_mm[l], 1)

            def s_m(N, k, par, now, hf):
                pe.wait_ge(x_ev[LEVELS - 1], done_half(N, hf))
                pe.wait_ge(al_ev[hf], done(N))
                for u in units_of(hf):
                    mm(slot(L2, u, R), ar[:, u, :], Xr[:, u, :], start=True, stop=False)
                    last = mm(slot(L2, u, R), al[:, u, :], Xr[:, u, :], start=False, stop=True)
                last.then_inc(m_mm[hf], 1)

            def s_yf(N, k, par, now, hf):
                pe.wait_ge(r_ev[hf], done(N))
                pe.wait_ge(y_ev[LEVELS - 1], done_half(N, hf))
                for u in units_of(hf):
                    last = mm(slot(G2, u, R), Zr[:, u, :], Yr[:, u, :], start=True, stop=True)
                last.then_inc(yf_mm[hf], 1)

            def s_ks(N, k, par, now, cc):
                pe.wait_ge(kqg_ev, done(N))
                pe.wait_ge(sup_ev[1 - cc], done(N) if cc else done(N - 1))
                for b in range(B):
                    u = b * NCC + cc
                    last = mm(RA[0:R, b * 128:(b + 1) * 128], kqg[par][:, u, 0:3, :].rearrange("p i t -> p (i t)"), S[:, b, :], start=True, stop=True)
                last.then_inc(ks_mm[cc], 1)

            def s_w(N, k, par, now, cc):
                pe.wait_ge(rhs_ev[cc], done(N))
                pe.wait_ge(yf_ev[1], done(N))
                pe.wait_ge(osb_ev[1 - cc], done(N) if cc else done(N - 1))
                for b in range(B):
                    last = mm(RB[0:R, b * 128:(b + 1) * 128], yf[par][:, b * NCC + cc, :], rhs[:, b, :], start=True, stop=True)
                last.then_inc(w_mm[cc], 1)

            def s_so(N, k, par, now, cc):
                pe.wait_ge(w_ev[cc], done(N))
                for b in range(B):
                    last = mm(RA[:, b * 128:(b + 1) * 128], krow[par][:, b * NCC + cc, :], ws[:, b, :], start=True, stop=True)
                last.then_inc(s_mm[cc], 1)
                for b in range(B):
                    u = b * NCC + cc
                    o = RB[b * TC:(b + 1) * TC, 0:128]
                    mm(o, kqg[par][:, u, 3, :], S[:, b, :], start=True, stop=False)
                    last = mm(o, ap[par][:, u, R:R + TC], ws[:, b, :], start=False, stop=True)
                last.then_inc(o_mm[cc], 1)

            def s_ot(N, k, par, now, cc):
                pe.wait_ge(osb_ev[cc], done(N))
                if "I" in now:
                    pe.wait_ge(x_ev[2 if cc else 0], done_half(N + 1, 1))
                elif cc:
                    pe.wait_ge(acc_ev[0], done(N))
                nc.tensor.transpose(side, osb[:, cc, :], g.ident[:, :]).then_inc(ot_mm[cc], 1)

            def s_out(N, k, par, now, cc):
                pe.wait_ge(og_ev[cc], done(N))
                if "I" in now:
                    pe.wait_ge(x_ev[3 if cc else 1], done_half(N + 1, 1))
                mm(side, wgo[:, 1, :], og[:, cc, :], start=True, stop=True).then_inc(out_mm[cc], 1)

            program(pe, ORDER, {"pt": s_pt, "ktr": s_ktr, "qs": s_qs, "vtr": s_vtr, "gram": s_gram, "z": s_z, "x": s_x, "y": s_y, "m": s_m,
                                "yf": s_yf, "ks": s_ks, "w": s_w, "so": s_so, "ot": s_ot, "out": s_out}, prep)


def mixture(nc, g, tag):
    NE = E_N + 1
    with ExitStack() as ctx:
        new_sem = semaphores(nc, ctx)
        sb = lambda n, s, dt=F32: ctx.enter_context(nc.sbuf_tensor(tag + n, s, dt))
        pb = lambda n, s: ctx.enter_context(nc.psum_tensor(tag + n, s, F32))
        sem = lambda n: new_sem(tag + n)
        w1, w2 = sb("w1", [128, NE, 128]), sb("w2", [128, NE, 128])
        b1, b2 = sb("b1", [128, NE]), sb("b2", [NE, 128])
        rw, rb = sb("rw", [128, NE]), sb("rb", [NE, 1])
        self32 = sb("sel32", [96, E_N * 128])
        sel = sb("sel", [96, E_N, 128], BF16)
        lt = sb("lt", [NE, TILE])
        lg = sb("lg", [128, 4, NE])
        mx = sb("mx", [128, 4])
        den = sb("den", [128, 4])
        p20 = sb("p20", [128, 4, 20])
        m20 = sb("m20", [128, 4, 20])
        top = sb("top", [128, 4, 8])
        held = sb("held", [128, 2])
        cw = sb("cw", [128, 4, NE])
        cwt = [sb(f"cwt{i}", [NE, TILE]) for i in range(2)]
        rest = sb("rest", [NE, 2, TILE])
        midw = sb("midw", [NE, TILE], BF16)
        parts = [sb(f"parts{i}", [96, TILE], BF16) for i in range(2)]
        hr, hs = sb("hr", [128, 2, TILE]), sb("hs", [128, 2, TILE])
        ph, pc, py = ([pb(f"{n}{i}", [128, TILE]) for i in range(2)] for n in ("ph", "pc", "py"))
        pl, pt = pb("pl", [128, TILE]), pb("pt", [128, TILE])
        evs = []

        def ev(n):
            evs.append(sem(n))
            return evs[-1]

        hc_mm, relu, hs_ev, y_mm = ([ev(f"{n}{e}") for e in range(NE)] for n in ("hc_mm", "relu", "scaled", "y_mm"))
        lt_mm, lt_ev, tr_mm, mx_ev, sub_ev, exp_ev, den_ev, rden_ev, p_ev, top_ev, topf_ev, m_ev, cw_ev, ct_mm, ct_ev = (
            ev(n) for n in ("lt_mm", "lt_ready", "tr_mm", "max_ready", "sub_ready", "exp_ready", "den_ready", "rden_ready", "p_ready",
                            "top_ready", "top3_ready", "match_ready", "cw_ready", "ct_mm", "cwt_ready"))
        hi_ev, r1_ev, mid_ev, r2_ev, parts_ev, acc_ev = (ev(n) for n in ("hi_ready", "r1_ready", "mid_ready", "r2_ready", "parts_ready", "acc_ready"))
        loaded, zeroed, const = sem("loaded"), sem("zeroed"), sem("const")
        with nc.Block() as b0:
            @b0.gpsimd
            def _(pool):
                for s in evs:
                    pool.sem_inc(s, CREDIT)
        block = ctx.enter_context(nc.Block())
        d = g.dram
        loads = [(w1[:, 0:E_N, :], d["eW1"].rearrange("e d h -> d e h")), (w1[:, E_N, :], d["sW1"]),
                 (w2[:, 0:E_N, :], d["eW2"].rearrange("e d h -> d e h")), (w2[:, E_N, :], d["sW2"]),
                 (b1[:, 0:E_N], d["eb1"].rearrange("e h -> h e")), (b1[:, E_N:NE], d["sb1"].unsqueeze(1)),
                 (b2[0:E_N, :], d["eb2"]), (b2[E_N:NE, :], d["sb2"].unsqueeze(0)),
                 (rw[:, 0:E_N], d["router_W"]), (rb[0:E_N, :], d["router_b"].unsqueeze(1)), (self32[:, :], d["c_sel"])]
        NPAIR = NT // 2

        def tiles(eng, step, lead):
            lead(0, 0, 0)
            with eng.Fori(0, NPAIR - 1) as j:
                step(j * 2, j, 0, j * 2 + 1, j)
                step(j * 2 + 1, j, 1, j * 2 + 2, j + 1)
            step(NT - 2, NPAIR - 1, 0, NT - 1, NPAIR - 1)
            step(NT - 1, NPAIR - 1, 1, None, None)

        def xn(j, par):
            return g.xn[:, bass.ds(j, 1), PAD + TILE * par:PAD + TILE * (par + 1)]

        @block.sync
        def _(sp):
            sp.wait_ge(zeroed, 1)
            for dst, src in loads:
                sp.dma_start(dst, src, allow_slow_non_contiguous=True).then_inc(loaded, 16)

        @block.tensor
        def _(pe):
            mm = nc.tensor.matmul
            pe.wait_ge(loaded, 16 * len(loads))
            pe.wait_ge(const, 1)

            def r_lt(n, j, par):
                pe.wait_ge(ct_ev, done(n - 1))
                pe.wait_ge(r1_ev, done(n - 1))
                mm(pl[0:NE, :], rw[:, :], xn(j, par), start=True, stop=True).then_inc(lt_mm, 1)

            def r_tr(n):
                pe.wait_ge(lt_ev, done(n))
                pe.wait_ge(sub_ev, done(n - 1))
                for a in range(4):
                    last = mm(pt[:, a * NE:(a + 1) * NE], lt[:, a * 128:(a + 1) * 128], g.ident[0:NE, 0:NE], start=True, stop=True)
                last.then_inc(tr_mm, 1)

            def r_ct(n):
                pe.wait_ge(cw_ev, done(n))
                for a in range(4):
                    last = nc.tensor.transpose(pl[0:NE, a * 128:(a + 1) * 128], cw[:, a, :], g.ident[:, :])
                last.then_inc(ct_mm, 1)

            def lead(n, j, par):
                r_lt(n, j, par)
                r_tr(n)
                r_ct(n)

            def step(n, j, par, n1, j1):
                def hidden(e):
                    if e < NE:
                        pe.wait_ge(relu[e - 2], done(n) if e >= 2 else done(n - 1))
                        pe.wait_ge(hs_ev[e - 2], done(n) if e >= 2 else done(n - 1))
                        last = mm(ph[e % 2][:, :], w1[:, e, :], xn(j, par), start=True, stop=True)
                        if e < E_N:
                            last = mm(pc[e % 2][:, :], sel[:, e, :], parts[par][:, :], start=True, stop=True)
                        last.then_inc(hc_mm[e], 1)
                pe.wait_ge(parts_ev, done(n))
                hidden(0)
                pe.wait_ge(acc_ev, done(n - 2))
                mm(py[par][:, :], b2[:, :], cwt[par][:, :], start=True, stop=False)
                for e in range(NE):
                    hidden(e + 1)
                    pe.wait_ge(hs_ev[e], done(n))
                    mm(py[par][:, :], w2[:, e, :], hs[:, e % 2, :], start=False, stop=e == NE - 1).then_inc(y_mm[e], 1)
                    if n1 is not None:
                        if e == 1:
                            r_lt(n1, j1, 1 - par)
                        if e == 3:
                            r_tr(n1)
                        if e == 10:
                            r_ct(n1)

            tiles(pe, step, lead)

        @block.scalar
        def _(act):
            act.wait_ge(loaded, 16 * len(loads))

            def r_lt(n):
                act.wait_ge(lt_mm, done(n))
                act.wait_ge(tr_mm, done(n - 1))
                nc.scalar.activation(lt[:, :], pl[0:NE, :], ACT.Identity, bias=rb[:, :]).then_inc(lt_ev, 1)

            def r_exp(n):
                act.wait_ge(sub_ev, done(n))
                nc.scalar.activation(lg[:, :, 0:E_N], lg[:, :, 0:E_N], ACT.Exp).then_inc(exp_ev, 1)

            def lead(n, j, par):
                r_lt(n)
                r_exp(n)

            def step(n, j, par, n1, j1):
                for e in range(NE):
                    act.wait_ge(hc_mm[e], done(n))
                    act.wait_ge(hs_ev[e - 2], done(n) if e >= 2 else done(n - 1))
                    nc.scalar.activation(hr[:, e % 2, :], ph[e % 2][:, :], ACT.Relu, bias=b1[:, e:e + 1]).then_inc(relu[e], 1)
                    if n1 is not None:
                        if e == 2:
                            r_lt(n1)
                        if e == 5:
                            r_exp(n1)

            tiles(act, step, lead)

        @block.vector
        def _(dve):
            nc.vector.memset(parts[0][:, :], 0.0)
            nc.vector.memset(parts[1][:, :], 0.0)
            nc.vector.memset(p20[:, :, :], -1.0)
            nc.vector.memset(rw[:, :], 0.0)
            nc.vector.memset(rb[:, :], 0.0)
            nc.vector.memset(cw[:, :, :], 1.0).then_inc(zeroed, 1)
            dve.wait_ge(zeroed, 1)
            dve.wait_ge(loaded, 16 * len(loads))
            nc.vector.tensor_copy(sel[:, :, :].rearrange("p e n -> p (e n)"), self32[:, :]).then_inc(const, 1)

            def r_sub(n):
                dve.wait_ge(tr_mm, done(n))
                v = pt[:, 0:4 * NE].rearrange("p (a e) -> p a e", e=NE)[:, :, 0:E_N]
                nc.vector.tensor_reduce(mx[:, :], v, AX.X, ALU.max).then_inc(mx_ev, 1)
                dve.wait_ge(mx_ev, done(n))
                nc.vector.tensor_tensor(lg[:, :, 0:E_N], v, mx[:, :].unsqueeze(2).broadcast_to([128, 4, E_N]), ALU.subtract).then_inc(sub_ev, 1)

            def r_top(n):
                dve.wait_ge(exp_ev, done(n))
                nc.vector.tensor_reduce(den[:, :], lg[:, :, 0:E_N], AX.X, ALU.add).then_inc(den_ev, 1)
                dve.wait_ge(den_ev, done(n))
                nc.vector.reciprocal(den[:, :], den[:, :]).then_inc(rden_ev, 1)
                dve.wait_ge(rden_ev, done(n))
                nc.vector.tensor_tensor(p20[:, :, 0:E_N], lg[:, :, 0:E_N], den[:, :].unsqueeze(2).broadcast_to([128, 4, E_N]), ALU.mult).then_inc(p_ev, 1)
                dve.wait_ge(p_ev, done(n))
                nc.vector.memset(held[:, 0:1], 0.0)
                for a in range(4):
                    last = nc.vector.max(top[:, a, :], p20[:, a, :])
                last.then_inc(top_ev, 1)
                dve.wait_ge(top_ev, done(n))
                nc.vector.memset(top[:, :, TOPK:8], -1.0).then_inc(topf_ev, 1)
                dve.wait_ge(topf_ev, done(n))
                nc.vector.memset(held[:, 1:2], 0.0)
                for a in range(4):
                    last = nc.vector.match_replace(m20[:, a, :], top[:, a, :], p20[:, a, :], -2.0)
                last.then_inc(m_ev, 1)
                dve.wait_ge(m_ev, done(n))
                dve.wait_ge(ct_mm, done(n - 1))
                nc.vector.scalar_tensor_tensor(cw[:, :, 0:E_N], m20[:, :, 0:E_N], -1.5, p20[:, :, 0:E_N], ALU.is_lt, ALU.mult).then_inc(cw_ev, 1)

            def r_parts(n, par):
                dve.wait_ge(ct_mm, done(n))
                dve.wait_ge(y_mm[NE - 1], done(n - 2))
                hi, mid, lo = (parts[par][32 * i:32 * i + NE, :] for i in range(3))
                nc.vector.tensor_copy(cwt[par][:, :], pl[0:NE, :]).then_inc(ct_ev, 1)
                nc.vector.tensor_copy(hi, pl[0:NE, :]).then_inc(hi_ev, 1)
                dve.wait_ge(hi_ev, done(n))
                nc.vector.tensor_tensor(rest[:, 0, :], pl[0:NE, :], hi, ALU.subtract).then_inc(r1_ev, 1)
                dve.wait_ge(r1_ev, done(n))
                nc.vector.tensor_copy(midw[:, :], rest[:, 0, :]).then_inc(mid_ev, 1)
                dve.wait_ge(mid_ev, done(n))
                nc.vector.tensor_copy(mid, midw[:, :])
                nc.vector.tensor_tensor(rest[:, 1, :], rest[:, 0, :], midw[:, :], ALU.subtract).then_inc(r2_ev, 1)
                dve.wait_ge(r2_ev, done(n))
                nc.vector.tensor_copy(lo, rest[:, 1, :]).then_inc(parts_ev, 1)

            def lead(n, j, par):
                r_sub(n)
                r_top(n)
                r_parts(n, par)

            def step(n, j, par, n1, j1):
                for e in range(NE):
                    dve.wait_ge(relu[e], done(n))
                    dve.wait_ge(y_mm[e - 2], done(n) if e >= 2 else done(n - 1))
                    if e < E_N:
                        nc.vector.tensor_tensor(hs[:, e % 2, :], pc[e % 2][:, :], hr[:, e % 2, :], ALU.mult).then_inc(hs_ev[e], 1)
                    else:
                        nc.vector.tensor_copy(hs[:, e % 2, :], hr[:, e % 2, :]).then_inc(hs_ev[e], 1)
                    if n1 is not None:
                        if e == 4:
                            r_sub(n1)
                        if e == 6:
                            r_top(n1)
                        if e == 11:
                            r_parts(n1, 1 - par)
                dve.wait_ge(y_mm[NE - 1], done(n))
                x = g.xT[:, bass.ds(j, 1), TILE * par:TILE * (par + 1)]
                nc.vector.tensor_tensor(x, py[par][:, :].unsqueeze(1), x, ALU.add).then_inc(acc_ev, 1)

            tiles(dve, step, lead)


def decay_attention(nc, g):
    NG = NTOK // 128
    LV = 5
    with ExitStack() as ctx:
        new_sem = semaphores(nc, ctx)
        sb = lambda n, s, dt=F32: ctx.enter_context(nc.sbuf_tensor("b_" + n, s, dt))
        pb = lambda n, s: ctx.enter_context(nc.psum_tensor("b_" + n, s, F32))
        sem = lambda n: new_sem("b_" + n)
        w = sb("w", [128, 6, 128])
        bw = sb("bw", [128, 1])
        masks = sb("masks", [128, LV + 1, 128])
        bmask = sb("bmask", [128, 128])
        F = sb("F", [128, NTOK])
        rF = sb("rF", [128, NTOK])
        kB = sb("kB", [128, NTOK])
        V = sb("V", [128, NG, 128])
        P = sb("P", [128, NG, 2, 128])
        kBr = sb("kBr", [128, NG, 128])
        z1 = sb("z1", [128, 2, TILE])
        wz = sb("wz", [128, 2, TILE])
        tmp4 = sb("tmp4", [128, 4, TILE])
        S = sb("S", [128, 2, B, 128])
        uS = sb("uS", [128, 2, B, 128])
        oT = sb("oT", [128, 2, B, 128])
        bank = [pb(f"bank{i}", [128, TILE]) for i in range(8)]
        loaded = sem("loaded")
        d = g.dram
        loads = [(w[:, i, :], d["b_" + n]) for i, n in enumerate(("Wx", "Ww", "Wk", "Wv", "Wr", "Wo"))] + [
            (bw[:, :], d["b_bw"].unsqueeze(1)), (masks[:, :, :].rearrange("p a b -> p (a b)"), d["c_bmasks"]), (bmask[:, :], d["c_bdiag"])]
        mm = nc.tensor.matmul
        zx, zx_ev, z_mm, k_mm, r_mm, w_ev, a_ev, k_ev, r_ev, v_mm, v_ev = (sem(n) for n in ("zx", "zx_ready", "z_mm", "k_mm", "r_mm", "w_ready", "a_ready", "k_ready", "r_ready", "v_mm", "v_ready"))
        with nc.Block() as block:
            @block.sync
            def _(sp):
                for dst, src in loads:
                    sp.dma_start(dst, src).then_inc(loaded, 16)

            @block.tensor
            def _(pe):
                pe.wait_ge(loaded, 16 * len(loads))
                for i in range(NT):
                    x = g.xn[:, i // 2, PAD + TILE * (i % 2):PAD + TILE * (i % 2 + 1)]
                    if i:
                        pe.wait_ge(zx_ev, i)
                    mm(bank[0][:, :], w[:, 0, :], x, start=True, stop=True).then_inc(zx, 1)
                    if i:
                        pe.wait_ge(k_ev, i)
                    mm(bank[1][:, :], w[:, 2, :], x, start=True, stop=True).then_inc(k_mm, 1)
                    if i:
                        pe.wait_ge(r_ev, i)
                    mm(bank[2][:, :], w[:, 4, :], x, start=True, stop=True).then_inc(r_mm, 1)
                    if i >= 2:
                        pe.wait_ge(v_ev, i - 1)
                    for a in range(4):
                        last = mm(bank[4 + i % 2][:, a * 128:(a + 1) * 128], x[:, a * 128:(a + 1) * 128], w[:, 3, :], start=True, stop=True)
                    last.then_inc(v_mm, 1)
                    pe.wait_ge(zx_ev, i + 1)
                    if i:
                        pe.wait_ge(w_ev, i)
                    mm(bank[3][:, :], w[:, 1, :], z1[:, i % 2, :], start=True, stop=True).then_inc(z_mm, 1)

            @block.scalar
            def _(act):
                act.wait_ge(loaded, 16 * len(loads))
                for i in range(NT):
                    act.wait_ge(zx, i + 1)
                    nc.scalar.activation(z1[:, i % 2, :], bank[0][:, :], ACT.Copy).then_inc(zx_ev, 1)
                    act.wait_ge(r_mm, i + 1)
                    nc.scalar.activation(rF[:, TILE * i:TILE * (i + 1)], bank[2][:, :], ACT.Sigmoid).then_inc(r_ev, 1)
                    act.wait_ge(z_mm, i + 1)
                    if i >= 2:
                        act.wait_ge(a_ev, i - 1)
                    nc.scalar.activation(wz[:, i % 2, :], bank[3][:, :], ACT.Sigmoid, bias=bw[:, :]).then_inc(w_ev, 1)

            @block.vector
            def _(dve):
                for i in range(NT):
                    dve.wait_ge(k_mm, i + 1)
                    nc.vector.tensor_copy(kB[:, TILE * i:TILE * (i + 1)], bank[1][:, :]).then_inc(k_ev, 1)
                    dve.wait_ge(v_mm, i + 1)
                    nc.vector.tensor_copy(V[:, 4 * i:4 * i + 4, :], bank[4 + i % 2][:, :].rearrange("p (a n) -> p a n", a=4)).then_inc(v_ev, 1)
                    dve.wait_ge(w_ev, i + 1)
                    nc.vector.tensor_scalar(F[:, TILE * i:TILE * (i + 1)], wz[:, i % 2, :], -1.0, 1.0, ALU.mult, ALU.add).then_inc(a_ev, 1)

        p_mm, p_ev, up_ev, t_ev, add_ev = sem("p_mm"), sem("p_ready"), sem("up_ready"), sem("f_read"), sem("added")
        NBK = NG // 2
        with nc.Block() as block:
            @block.tensor
            def _(pe):
                n = 0
                for l in range(LV + 1):
                    for q in range(NBK):
                        if l:
                            pe.wait_ge(up_ev, (l - 1) * B + q // (NBK // B) + 1)
                        if n >= 8:
                            pe.wait_ge(p_ev, n - 7)
                        h = q % 2
                        for a in range(4):
                            t0 = (4 * (q // 2) + a) * 128
                            last = mm(bank[n % 8][:, a * 128:(a + 1) * 128], kB[64 * h:64 * h + 64, t0:t0 + 128], rF[64 * h:64 * h + 64, t0:t0 + 128], start=True, stop=True)
                        last.then_inc(p_mm, 1)
                        n += 1

            @block.gpsimd
            def _(pool):
                pool.wait_ge(loaded, 16 * len(loads))
                for n in range(NBK * (LV + 1)):
                    l, q = divmod(n, NBK)
                    if l:
                        pool.wait_ge(p_ev, n + 1)
                        dst = P[:, 4 * (q // 2):4 * (q // 2) + 4, q % 2, :]
                        nc.gpsimd.tensor_tensor(dst, dst, tmp4[:, n % 4, :].rearrange("p (a t) -> p a t", a=4), ALU.add).then_inc(add_ev, 1)
                        pool.wait_ge(add_ev, n + 1 - NBK)

            @block.vector
            def _(dve):
                n = 0
                ups = 0
                for l in range(LV + 1):
                    for q in range(NBK):
                        dve.wait_ge(p_mm, n + 1)
                        src = bank[n % 8][:, :].rearrange("p (x t) -> p x t", t=128)
                        mask = masks[:, l, :].unsqueeze(1).broadcast_to([128, 4, 128])
                        if l == 0:
                            dst = P[:, 4 * (q // 2):4 * (q // 2) + 4, q % 2, :]
                        else:
                            dst = tmp4[:, n % 4, :].rearrange("p (x t) -> p x t", t=128)
                            if n - NBK >= 4:
                                dve.wait_ge(add_ev, n - NBK - 3)
                        nc.vector.tensor_tensor(dst, src, mask, ALU.mult).then_inc(p_ev, 1)
                        n += 1
                        if n % (NBK // B) == 0 and l <= LV:
                            b = q // (NBK // B)
                            s0, s1 = b * T, (b + 1) * T
                            if l == 0:
                                nc.vector.tensor_tensor(rF[:, s0:s1], rF[:, s0:s1], F[:, s0:s1], ALU.mult).then_inc(up_ev, 1)
                                continue
                            hs = 1 << (l - 1)
                            v = lambda t: t[:, s0:s1].rearrange("p (n two h) -> p n two h", two=2, h=hs)
                            fv, rv, kv = v(F), v(rF), v(kB)
                            sh = [128, T // (2 * hs), hs]
                            mid, end = fv[:, :, 0, hs - 1:hs].broadcast_to(sh), fv[:, :, 1, hs - 1:hs].broadcast_to(sh)
                            nc.vector.tensor_tensor(kv[:, :, 0, :], kv[:, :, 0, :], end, ALU.mult)
                            nc.vector.tensor_tensor(rv[:, :, 1, :], rv[:, :, 1, :], mid, ALU.mult).then_inc(t_ev, 1)
                            ups += 1
                            dve.wait_ge(t_ev, ups)
                            nc.vector.tensor_tensor(fv[:, :, 1, :], fv[:, :, 1, :], mid, ALU.mult).then_inc(up_ev, 1)
                            dve.wait_ge(up_ev, l * B + b + 1)

        kt_mm, kt_ev, u_mm, u_ev, s_ev, i_mm, a_mm, o_ev, o2_ev, y_mm, y_ev, z_ev = (sem(n) for n in ("kt_mm", "kt_ready", "u_mm", "u_ready", "s_ready", "i_mm", "a_mm", "o_ready", "o2_ready", "y_mm", "y_ready", "s_zero"))
        NGB = NG // B
        with nc.Block() as block:
            @block.tensor
            def _(pe):
                for q in range(NG // 4):
                    if q >= 2:
                        pe.wait_ge(kt_ev, q - 1)
                    for a in range(4):
                        last = nc.tensor.transpose(bank[q % 2][:, a * 128:(a + 1) * 128], kB[:, (4 * q + a) * 128:(4 * q + a + 1) * 128], g.ident[:, :])
                    last.then_inc(kt_mm, 1)
                pe.wait_ge(kt_ev, NG // 4)
                pe.wait_ge(z_ev, 1)

                def update(n):
                    gr, c = divmod(n, 4)
                    if n >= 2:
                        pe.wait_ge(u_ev, n - 1)
                    for b in range(B):
                        i = b * NGB + gr
                        last = mm(bank[2 + n % 2][:, b * 128:(b + 1) * 128], kBr[32 * c:32 * c + 32, i, :], V[32 * c:32 * c + 32, i, :], start=True, stop=True)
                    last.then_inc(u_mm, 1)

                update(0)
                for gr in range(NGB):
                    if gr >= 2:
                        pe.wait_ge(o_ev, gr - 1)
                    for b in range(B):
                        i = b * NGB + gr
                        for h in range(2):
                            last = mm(bank[4 + gr % 2][64 * h:64 * h + 64, b * 128:(b + 1) * 128], V[:, i, 64 * h:64 * h + 64], P[:, i, h, :], start=True, stop=True)
                    last.then_inc(a_mm, 1)
                    for c in range(4):
                        n = 4 * gr + c
                        if n + 1 < 4 * NGB:
                            update(n + 1)
                        if n:
                            pe.wait_ge(s_ev, n)
                        if c == 0 and gr:
                            pe.wait_ge(o2_ev, gr)
                        for b in range(B):
                            last = mm(bank[6][:, b * 128 + 32 * c:b * 128 + 32 * c + 32], S[:, n % 2, b, :], rF[:, b * T + 32 * n:b * T + 32 * n + 32], start=True, stop=True)
                        last.then_inc(i_mm, 1)
                    pe.wait_ge(o2_ev, gr + 1)
                    if gr:
                        pe.wait_ge(y_ev, gr)
                    mm(bank[7][:, :], w[:, 5, :], oT[:, gr % 2, :, :].rearrange("p b t -> p (b t)"), start=True, stop=True).then_inc(y_mm, 1)

            @block.scalar
            def _(act):
                for q in range(NG // 4):
                    act.wait_ge(kt_mm, q + 1)
                    nc.scalar.activation(kBr[:, 4 * q:4 * q + 4, :], bank[q % 2][:, :].rearrange("p (a n) -> p a n", a=4), ACT.Copy).then_inc(kt_ev, 1)
                for gr in range(NGB):
                    act.wait_ge(a_mm, gr + 1)
                    if gr >= 2:
                        act.wait_ge(y_mm, gr - 1)
                    nc.scalar.activation(oT[:, gr % 2, :, :].rearrange("p b t -> p (b t)"), bank[4 + gr % 2][:, :], ACT.Copy).then_inc(o_ev, 1)

            @block.vector
            def _(dve):
                nc.vector.memset(S[:, 0, :, :], 0.0).then_inc(z_ev, 1)
                dve.wait_ge(z_ev, 1)
                for n in range(4 * NGB):
                    if n + 1 < 4 * NGB:
                        dve.wait_ge(u_mm, n + 1)
                        nc.vector.tensor_tensor(uS[:, n % 2, :, :], bank[2 + n % 2][:, :].rearrange("p (b e) -> p b e", b=B),
                                                bmask[:, :].unsqueeze(1).broadcast_to([128, B, 128]), ALU.mult).then_inc(u_ev, 1)
                        dve.wait_ge(u_ev, n + 1)
                        if n:
                            dve.wait_ge(s_ev, n)
                            dve.wait_ge(i_mm, n)
                        for b in range(B):
                            end = b * T + 32 * n + 31
                            last = nc.vector.scalar_tensor_tensor(S[:, (n + 1) % 2, b, :], S[:, n % 2, b, :], F[:, end:end + 1], uS[:, n % 2, b, :], ALU.mult, ALU.add)
                        last.then_inc(s_ev, 1)
                    if n % 4 == 3:
                        gr = n // 4
                        dve.wait_ge(i_mm, n + 1)
                        dve.wait_ge(o_ev, gr + 1)
                        o = oT[:, gr % 2, :, :].rearrange("p b t -> p (b t)")
                        nc.vector.tensor_tensor(o, bank[6][:, :], o, ALU.add).then_inc(o2_ev, 1)
                        dve.wait_ge(y_mm, gr + 1)
                        x = g.xT[:, :, gr * 128:(gr + 1) * 128]
                        nc.vector.tensor_tensor(x, bank[7][:, :].rearrange("p (b t) -> p b t", b=B), x, ALU.add).then_inc(y_ev, 1)



INS = [("x", "L0_attn_a_x")] + [(n, "L0_attn_a_" + n) for n in ("Wq", "Wk", "Wv", "Wb", "Wa", "A_log", "dt_bias", "conv_q", "conv_k", "conv_v", "Wg", "rms_weight", "Wo")] + [
    ("b_" + n, "L0_attn_b_" + n) for n in ("ln_g", "ln_b", "Wx", "Ww", "bw", "Wk", "Wv", "Wr", "Wo")] + [
    (n, "L0_ffn_" + n) for n in ("router_W", "router_b", "sW1", "sb1", "sW2", "sb2", "eW1", "eb1", "eW2", "eb2")]


def build(nc, dram, phases="abcd"):
    with ExitStack() as ctx:
        sb = lambda n, s, dt=F32: ctx.enter_context(nc.sbuf_tensor(n, s, dt))
        g = Shared()
        g.dram = dram
        g.xT = sb("xT", [128, B, T])
        g.xn = sb("xn", [128, B, PAD + T])
        g.ident = sb("ident", [128, 128])
        g.mean = sb("mean", [128, 128])
        g.ones = sb("ones", [128, 128])
        g.half = sb("half", [128, U])
        g.minus_half = sb("minus_half", [128, 1])
        zeroed = ctx.enter_context(nc.semaphore("zeroed"))
        g.rms_sem = ctx.enter_context(nc.semaphore("rms_in"))
        with ExitStack() as a:
            sa = lambda n, s: a.enter_context(nc.sbuf_tensor(n, s, F32))
            g.mask4 = sa("mask4", [R, 128])
            g.lev = sa("lev", [R, (LEVELS + 1) * R])
            g.after = sa("after", [TC, R])
            g.upto = sa("upto", [TC, TC])
            g.beta = sa("beta", [R, NH, NTOK // TC])
            g.gt = sa("gt", [TC, NTOK // TC, NH])
            g.rms_in = sa("rms_w", [128, 1])
            g.const_loads = [("c_ident", g.ident[:, :]), ("c_mean", g.mean[:, :]), ("c_mask4", g.mask4[:, :]), ("c_lev", g.lev[:, :]),
                             ("c_after", g.after[:, :]), ("c_upto", g.upto[:, :])]
            load_rows(nc, g)
            with nc.Block() as b:
                @b.vector
                def _(dve):
                    nc.vector.memset(g.xn[:, :, 0:PAD], 0.0)
                    nc.vector.memset(g.half[:, :], 0.5)
                    nc.vector.memset(g.minus_half[:, :], -0.5)
                    nc.vector.memset(g.ones[:, :], 1.0).then_inc(zeroed, 1)
                    dve.wait_ge(zeroed, 1)

                @b.sync
                def _(sp):
                    sp.dma_start(g.rms_in[:, :], dram["rms_weight"].unsqueeze(1)).then_inc(g.rms_sem, 16)
                    sp.wait_ge(g.rms_sem, 16)
            layernorm(nc, g, "ln0", lambda i: g.xT[:, i // 2, TILE * (i % 2):TILE * (i % 2 + 1)])
            decay_gates(nc, g)
            delta_attention(nc, g)
        x_tile = lambda i: g.xT[:, i // 2, TILE * (i % 2):TILE * (i % 2 + 1)]
        n_tile = lambda i: g.xn[:, i // 2, PAD + TILE * (i % 2):PAD + TILE * (i % 2 + 1)]
        layernorm(nc, g, "ln1", x_tile)
        mixture(nc, g, "f1")
        layernorm(nc, g, "ln2", x_tile)
        with ExitStack() as a:
            gain = a.enter_context(nc.sbuf_tensor("ln_gain", [128, 2], F32))
            gain_in = a.enter_context(nc.semaphore("ln_gain_in"))
            with nc.Block() as b:
                @b.sync
                def _(sp):
                    sp.dma_start(gain[:, 0:1], dram["b_ln_g"].unsqueeze(1)).then_inc(gain_in, 16)
                    sp.dma_start(gain[:, 1:2], dram["b_ln_b"].unsqueeze(1)).then_inc(gain_in, 16)
                    sp.wait_ge(gain_in, 32)
            layernorm(nc, g, "ln3", n_tile, (gain[:, 0:1], gain[:, 1:2]))
            decay_attention(nc, g)
        layernorm(nc, g, "ln4", x_tile)
        mixture(nc, g, "f2")
        store_rows(nc, g)


def kernel(**inputs):
    import concourse.bacc as _bacc
    from concourse.bass_utils import run_bass_kernel_spmd as _run

    nc = _bacc.Bacc("TRN2", target_bir_lowering=False, num_devices=1)
    arrays, dram = {}, {}
    named = [(s, np.ascontiguousarray(inputs[n])) for s, n in INS] + list(constants().items())
    for name, a in named:
        arrays[f"in_{name}_dram"] = a
        dram[name] = nc.dram_tensor(f"in_{name}_dram", a.shape, mybir.dt.from_np(a.dtype), kind="ExternalInput").ap()
    dram["out"] = nc.dram_tensor("out_0_dram", (B, T, D), F32, kind="ExternalOutput").ap()
    build(nc, dram)
    r = _run(nc, [arrays], core_ids=[0])
    return r.results[0]["out_0_dram"]
```

```python
import math
from contextlib import ExitStack

import numpy as np
import concourse.bass as bass
from concourse import mybir

F32 = mybir.dt.float32
BF16 = mybir.dt.bfloat16
F16 = mybir.dt.float16
F32R = mybir.dt.float32r
ALU = mybir.AluOpType
ACT = mybir.ActivationFunctionType
AX = mybir.AxisListType

B, T, D = 4, 1024, 128
NTOK = B * T
NH, NHH, TAPS = 8, 3, 4
TC = 32
R = NHH * TC
NCC = 2
SPAN = NCC * TC
U = B * NCC
KSTEPS = T // SPAN
PAD = TAPS - 1
LEVELS = 6
HU = U // 2
CREDIT = 2
TILE = 512
NT = NTOK // TILE
E_N, TOPK = 15, 3


class Shared:

    dram = head = next = None


def done(n):
    return n + 1 + CREDIT


def done_half(n, hf):
    return 2 * n + hf + 1 + CREDIT


def constants():
    i, t = np.divmod(np.arange(R), TC)
    tau = NHH * t + i
    later = tau[None, :] > tau[:, None]
    tri = np.arange(TC)[None, :] >= t[:, None]
    mask4 = np.concatenate([later, tri], axis=1).astype(np.float32)
    lev = []
    for l in range(LEVELS):
        s, joined = (NHH << (l - 1), NHH << l) if l else (1, NHH)
        same = (tau[:, None] // joined) == (tau[None, :] // joined)
        lev.append(-(same & (tau[:, None] // s > tau[None, :] // s)).astype(np.float32))
    lev.append(lev[0].T)
    j = np.arange(TC)
    after_m = (j[:, None] > t[None, :]).astype(np.float32)
    upto = (j[:, None] <= j[None, :]).astype(np.float32)
    c = {
        "c_ident": np.eye(128, dtype=np.float32),
        "c_mean": np.full((128, 128), 1.0 / D, np.float32),
        "c_mask4": mask4,
        "c_lev": np.concatenate(lev, axis=1),
        "c_after": after_m,
        "c_upto": upto,
    }
    sel = np.zeros((96, E_N, 128), np.float32)
    for part in range(3):
        for e in range(E_N):
            sel[32 * part + e, e] = 1
    c["c_sel"] = sel.reshape(96, -1)
    a = np.arange(128)
    bm = [np.eye(128, dtype=np.float32)]
    for l in range(5):
        s = 1 << l
        same = (a[:, None] // (2 * s)) == (a[None, :] // (2 * s))
        bm.append((same & (a[:, None] // s < a[None, :] // s)).astype(np.float32))
    c["c_bmasks"] = np.stack(bm, 1).reshape(128, -1)
    c["c_bdiag"] = (a[:, None] // 64 == a[None, :] // 64).astype(np.float32)
    return c


def semaphores(nc, ctx):
    held = []

    def sem(name):
        held.append(nc.alloc_semaphore(name))
        return held[-1]

    def end():
        nc.clear_and_free_semaphores(held)
        nc.all_engine_barrier()

    ctx.callback(end)
    return sem


def load_rows(nc, g):
    with ExitStack() as ctx:
        new_sem = semaphores(nc, ctx)
        xin = ctx.enter_context(nc.sbuf_tensor("xin", [128, NTOK // 128, D], F32))
        ps = [ctx.enter_context(nc.psum_tensor(f"ld{i}", [128, TILE], F32)) for i in range(4)]
        loaded, cst, turned, kept = (new_sem(n) for n in ("ld_x", "ld_cst", "ld_turned", "ld_kept"))
        block = ctx.enter_context(nc.Block())
        src = g.dram["x"].rearrange("b t d -> (b t) d").rearrange("(j p) d -> p j d", p=128)

        @block.sync
        def _(sp):
            n = 0
            for name, dst in g.const_loads:
                sp.dma_start(dst, g.dram[name]).then_inc(cst, 16)
                n += 16
            sp.wait_ge(cst, n)
            for q in range(4):
                sp.dma_start(xin[:, 8 * q:8 * q + 8, :], src[:, 8 * q:8 * q + 8, :]).then_inc(loaded, 16)
                sp.wait_ge(loaded, 16 * (q + 1))

        @block.tensor
        def _(pe):
            pe.wait_ge(cst, 16 * len(g.const_loads))
            for i in range(NT):
                pe.wait_ge(loaded, 16 * (i // 2 + 1))
                if i >= 4:
                    pe.wait_ge(kept, i - 3)
                for a in range(4):
                    last = nc.tensor.transpose(ps[i % 4][:, 128 * a:128 * a + 128], xin[:, 4 * i + a, :], g.ident[:, :])
                last.then_inc(turned, 1)

        @block.scalar
        def _(act):
            for i in range(NT):
                act.wait_ge(turned, i + 1)
                nc.scalar.activation(g.xT[:, i // 2, TILE * (i % 2):TILE * (i % 2 + 1)], ps[i % 4][:, :], ACT.Copy).then_inc(kept, 1)


def store_rows(nc, g):
    with ExitStack() as ctx:
        new_sem = semaphores(nc, ctx)
        xo = ctx.enter_context(nc.sbuf_tensor("xout", [128, NTOK // 128, D], F32))
        ps = [ctx.enter_context(nc.psum_tensor(f"st{i}", [128, TILE], F32)) for i in range(4)]
        turned, kept, stored = (new_sem(n) for n in ("st_turned", "st_kept", "st_stored"))
        block = ctx.enter_context(nc.Block())
        dst = g.dram["out"].rearrange("b t d -> (b t) d").rearrange("(j p) d -> p j d", p=128)

        @block.tensor
        def _(pe):
            for i in range(NT):
                if i >= 4:
                    pe.wait_ge(kept, i - 3)
                for a in range(4):
                    o = TILE * (i % 2) + 128 * a
                    last = nc.tensor.transpose(ps[i % 4][:, 128 * a:128 * a + 128], g.xT[:, i // 2, o:o + 128], g.ident[:, :])
                last.then_inc(turned, 1)

        @block.scalar
        def _(act):
            for i in range(NT):
                act.wait_ge(turned, i + 1)
                nc.scalar.activation(xo[:, 4 * i:4 * i + 4, :], ps[i % 4][:, :].rearrange("p (a d) -> p a d", a=4), ACT.Copy).then_inc(kept, 1)

        @block.sync
        def _(sp):
            for q in range(4):
                sp.wait_ge(kept, 2 * q + 2)
                sp.dma_start(dst[:, 8 * q:8 * q + 8, :], xo[:, 8 * q:8 * q + 8, :]).then_inc(stored, 16)
            sp.wait_ge(stored, 64)


def layernorm(nc, g, tag, src, affine=None):
    with ExitStack() as ctx:
        new_sem = semaphores(nc, ctx)
        sb = lambda n, s: ctx.enter_context(nc.sbuf_tensor(tag + n, s, F32))
        mean = [ctx.enter_context(nc.psum_tensor(f"{tag}mean{i}", [128, TILE], F32)) for i in range(2)]
        var = [ctx.enter_context(nc.psum_tensor(f"{tag}var{i}", [128, TILE], F32)) for i in range(2)]
        xc = sb("xc", [128, 3, TILE])
        sq = sb("sq", [128, 2, TILE])
        rs = sb("rs", [128, 2, TILE])
        sem = lambda n: new_sem(tag + n)
        meaned, centred, squared, varied, rooted, scaled, scaled_x, normed = (sem(n) for n in ("meaned", "centred", "squared", "varied", "rooted", "scaled", "scaled_x", "normed"))
        eps = ctx.enter_context(nc.sbuf_tensor(tag + "eps", [128, 1], F32))
        eps_ready = sem("eps_ready")
        block = ctx.enter_context(nc.Block())

        @block.tensor
        def _(pe):
            def mean_of(i):
                if i >= 2:
                    pe.wait_ge(centred, i - 1)
                nc.tensor.matmul(mean[i % 2][:, :], g.mean[:, :], src(i), start=True, stop=True).then_inc(meaned, 1)
            mean_of(0)
            mean_of(1)
            for i in range(NT):
                pe.wait_ge(squared, i + 1)
                if i >= 2:
                    pe.wait_ge(rooted, i - 1)
                nc.tensor.matmul(var[i % 2][:, :], g.mean[:, :], sq[:, i % 2, :], start=True, stop=True).then_inc(varied, 1)
                if i + 2 < NT:
                    mean_of(i + 2)

        @block.scalar
        def _(act):
            act.wait_ge(eps_ready, 1)

            def square(i):
                act.wait_ge(centred, i + 1)
                if i >= 2:
                    act.wait_ge(varied, i - 1)
                nc.scalar.activation(sq[:, i % 2, :], xc[:, i % 3, :], ACT.Square).then_inc(squared, 1)
            square(0)
            square(1)
            for i in range(NT):
                act.wait_ge(varied, i + 1)
                if i >= 2:
                    act.wait_ge(normed, i - 1)
                nc.scalar.activation(rs[:, i % 2, :], var[i % 2][:, :], ACT.Sqrt, bias=eps[:, :]).then_inc(rooted, 1)
                if i + 2 < NT:
                    square(i + 2)

        @block.vector
        def _(dve):
            def centre(i):
                dve.wait_ge(meaned, i + 1)
                if i >= 3:
                    dve.wait_ge(squared, i - 2)
                    dve.wait_ge(normed, i - 2)
                nc.vector.tensor_tensor(xc[:, i % 3, :], src(i), mean[i % 2][:, :], ALU.subtract).then_inc(centred, 1)
            nc.vector.memset(eps[:, :], 1e-5).then_inc(eps_ready, 1)
            centre(0)
            centre(1)
            for i in range(NT):
                dve.wait_ge(rooted, i + 1)
                nc.vector.reciprocal(rs[:, i % 2, :], rs[:, i % 2, :]).then_inc(scaled, 1)
                if i + 2 < NT:
                    centre(i + 2)
                dve.wait_ge(scaled, i + 1)
                dst = g.xn[:, i // 2, PAD + TILE * (i % 2):PAD + TILE * (i % 2 + 1)]
                if affine is None:
                    nc.vector.tensor_tensor(dst, xc[:, i % 3, :], rs[:, i % 2, :], ALU.mult).then_inc(normed, 1)
                else:
                    nc.vector.tensor_tensor(rs[:, i % 2, :], xc[:, i % 3, :], rs[:, i % 2, :], ALU.mult).then_inc(scaled_x, 1)
                    dve.wait_ge(scaled_x, i + 1)
                    nc.vector.tensor_scalar(dst, rs[:, i % 2, :], affine[0], affine[1], ALU.mult, ALU.add).then_inc(normed, 1)


def decay_gates(nc, g):
    with ExitStack() as ctx:
        new_sem = semaphores(nc, ctx)
        sb = lambda n, s: ctx.enter_context(nc.sbuf_tensor(n, s, F32))
        wba = sb("wba", [128, 2, 32])
        bg = sb("bg", [32, 2, NTOK])
        turned = sb("bg_turned", [32, 2, NTOK])
        small = sb("small", [32, 3, NH])
        z, m, e, s, s2, p = (sb("sp_" + n, [32, NTOK // TC, NH]) for n in ("z", "m", "e", "s", "s2", "p"))
        ps = [[ctx.enter_context(nc.psum_tensor(f"bg{i}{j}", [32, TILE], F32)) for j in range(2)] for i in range(2)]
        sem = new_sem
        w_in, w_zero, mm, kept, chain, ex, al = (sem(n) for n in ("bg_w", "bg_zero", "bg_mm", "bg_kept", "bg_chain", "bg_exp", "bg_alog"))
        block = ctx.enter_context(nc.Block())

        @block.sync
        def _(sp):
            sp.wait_ge(w_zero, 1)
            sp.dma_start(wba[:, 0, 0:NHH * NH], g.dram["Wb"]).then_inc(w_in, 16)
            sp.dma_start(wba[:, 1, 0:NH], g.dram["Wa"]).then_inc(w_in, 16)
            sp.dma_start(small[:, 0, :], g.dram["dt_bias"].partition_broadcast(32)).then_inc(w_in, 16)
            sp.dma_start(small[:, 1, :], g.dram["A_log"].partition_broadcast(32)).then_inc(w_in, 16)

        @block.tensor
        def _(pe):
            pe.wait_ge(w_in, 64)
            for i in range(NT):
                if i >= 2:
                    pe.wait_ge(kept, i - 1)
                rhs = g.xn[:, i // 2, PAD + TILE * (i % 2):PAD + TILE * (i % 2 + 1)]
                for j in range(2):
                    last = nc.tensor.matmul(ps[j][i % 2][:, :], wba[:, j, :], rhs, start=True, stop=True)
                last.then_inc(mm, 1)

        @block.scalar
        def _(act):
            for i in range(NT):
                act.wait_ge(mm, i + 1)
                nc.scalar.activation(bg[:, 0, TILE * i:TILE * (i + 1)], ps[0][i % 2][:, :], ACT.Sigmoid)
                nc.scalar.activation(bg[:, 1, TILE * i:TILE * (i + 1)], ps[1][i % 2][:, :], ACT.Copy).then_inc(kept, 1)
            act.wait_ge(w_in, 64)
            nc.scalar.activation(small[:, 2, :], small[:, 1, :], ACT.Exp).then_inc(al, 1)
            act.wait_ge(chain, 3)
            nc.scalar.activation(e[:, :, :], e[:, :, :], ACT.Exp).then_inc(ex, 1)

        @block.vector
        def _(dve):
            nc.vector.memset(wba[:, :, :], 0.0).then_inc(w_zero, 1)
            nc.vector.memset(g.beta[:, NH, :], 0.0)
            nc.vector.memset(g.gt[:, :, NH:NH + 1], 0.0)
            n = [0]

            def link(ins):
                n[0] += 1
                ins.then_inc(chain, 1)
                dve.wait_ge(chain, n[0])

            dve.wait_ge(kept, NT)
            nc.vector.transpose(turned[:, 0, :], bg[:, 0, :])
            link(nc.vector.transpose(turned[:, 1, :], bg[:, 1, :]))
            dve.wait_ge(w_in, 64)
            a = turned[:, 1, :].rearrange("t (k r) -> t k r", r=32)[:, :, 0:NH]
            bias = small[:, 0, :].unsqueeze(1).broadcast_to([32, NTOK // TC, NH])
            link(nc.vector.tensor_tensor(z[:, :, :], a, bias, ALU.add))
            link(nc.vector.scalar_tensor_tensor(e[:, :, :], z[:, :, :], -1.0, z[:, :, :], ALU.mult, ALU.min))
            for i in range(NHH):
                bt = turned[:, 0, :].rearrange("t (k r) -> t r k", r=32)[:, NH * i:NH * (i + 1), :]
                nc.vector.tensor_scalar(g.beta[TC * i:TC * (i + 1), 0:NH, :], bt, 2.0, None, ALU.mult)
            link(nc.vector.tensor_scalar(m[:, :, :], z[:, :, :], 0.0, None, ALU.max))
            dve.wait_ge(ex, 1)
            link(nc.vector.tensor_scalar(s[:, :, :], e[:, :, :], 2.0, None, ALU.add))
            link(nc.vector.reciprocal(s[:, :, :], s[:, :, :]))
            link(nc.vector.tensor_tensor(s[:, :, :], s[:, :, :], e[:, :, :], ALU.mult))
            link(nc.vector.tensor_tensor(s2[:, :, :], s[:, :, :], s[:, :, :], ALU.mult))
            link(nc.vector.tensor_scalar(p[:, :, :], s2[:, :, :], 2.0 / 17, 2.0 / 15, ALU.mult, ALU.add))
            for c in (13, 11, 9, 7, 5, 3, 1):
                link(nc.vector.tensor_tensor(p[:, :, :], p[:, :, :], s2[:, :, :], ALU.mult))
                link(nc.vector.tensor_scalar(p[:, :, :], p[:, :, :], 2.0 / c, None, ALU.add))
            link(nc.vector.tensor_tensor(p[:, :, :], p[:, :, :], s[:, :, :], ALU.mult))
            link(nc.vector.tensor_tensor(p[:, :, :], p[:, :, :], m[:, :, :], ALU.add))
            dve.wait_ge(al, 1)
            ea = small[:, 2, :].unsqueeze(1).broadcast_to([32, NTOK // TC, NH])
            nc.vector.scalar_tensor_tensor(g.gt[:, :, 0:NH], p[:, :, :], -1.0, ea, ALU.mult, ALU.mult)


def delta_attention(nc, g):
    with ExitStack() as ctx:
        new_sem = semaphores(nc, ctx)
        sb = lambda n, s, dt=F32: ctx.enter_context(nc.sbuf_tensor(n, s, dt))
        stage_w = sb("stage_w", [128, 9, 128])
        stage_c = sb("stage_c", [128, 4, 128, TAPS])
        stage_v = sb("stage_v", [128, NHH, TAPS])
        wt = sb("wt", [128, 4, TAPS, 128])
        wv = sb("wv", [128, NHH, 128])
        taps_v = sb("taps_v", [128, NHH, TAPS])
        raw = [sb(f"raw{i}", [128, NHH, B, PAD + SPAN]) for i in range(2)]
        conv = sb("conv", [128, NHH, B, SPAN])
        gate_raw = sb("gate_raw", [128, U, TC])
        wgo = sb("wgo", [128, 2, 128])
        rmsw = sb("rmsw", [128, 1])
        edec = sb("edec", [R, B, T])
        gdec = sb("gdec", [128, B, T])
        kqs = sb("kqs", [128, 4, U, 4, TC])
        kq = [kqs[:, i] for i in range(2)]
        vt = [sb(f"vt{i}", [128, U, NHH, TC]) for i in range(2)]
        gate = [sb(f"gate{i}", [128, U, TC]) for i in range(2)]
        kqg = [kqs[:, 2 + i] for i in range(2)]
        gm = [sb(f"gm{i}", [TC, NTOK // TC // 4, TC]) for i in range(2)]
        ksq = sb("ksq", [R, U, 128])
        ksum = sb("ksum", [R, U])
        sqq = sb("sqq", [128, NCC, B, TC])
        ss = sb("ss", [R, U])
        rk = [sb(f"rk{i}", [R, U]) for i in range(2)]
        rinv = sb("rinv", [R, U])
        step_s = sb("step_s", [R, U])
        q2 = [sb(f"q2{i}", [128, NCC]) for i in range(2)]
        es = [sb(f"es{i}", [R, U, TC]) for i in range(2)]
        es4 = sb("es4", [R, U, 4, TC])
        krow = [sb(f"krow{i}", [R, U, 128]) for i in range(2)]
        vrow = [sb(f"vrow{i}", [R, U, 128]) for i in range(2)]
        ap = [sb(f"ap{i}", [R, U, 128]) for i in range(2)]
        ix = sb("ix", [R, U, R])
        ar = sb("ar", [R, U, R], F16)
        al = sb("al", [R, U, R], F16)
        Xr = sb("Xr", [R, U, R], F16)
        Yr = sb("Yr", [R, U, R], F16)
        Zr = sb("Zr", [R, U, R], F16)
        ident_r = sb("ident_r", [R, R], F16)
        ident_h = sb("ident_h", [R, HU, R], F16)
        yf = [sb(f"yf{i}", [R, U, R]) for i in range(2)]
        S = sb("S", [128, B, 128])
        rhs = sb("rhs", [R, B, 128])
        ws = sb("ws", [R, B, 128])
        mo = sb("mo", [128, NCC])
        fo = sb("fo", [128, NCC])
        osq = sb("osq", [128, 128])
        osb = sb("osb", [128, NCC, 128])
        og = sb("og", [128, NCC, 128])

        PP = [ctx.enter_context(nc.psum_tensor(f"PP{i}", [128, TILE], F32)) for i in range(2)]
        G2 = ctx.enter_context(nc.psum_tensor("G2", [128, 2, TILE], F32))
        L2 = ctx.enter_context(nc.psum_tensor("L2", [128, 2, TILE], F32))
        RA = ctx.enter_context(nc.psum_tensor("RA", [128, TILE], F32))
        RB = ctx.enter_context(nc.psum_tensor("RB", [128, TILE], F32))
        side = L2[:, 1, 384:512]

        evs = []

        def ev(name):
            s = new_sem(name)
            evs.append(s)
            return s

        proj = [ev(f"proj_mm{q}") for q in range(4)]
        silu = [ev(f"silu{q}") for q in range(4)]
        rk_ev, ss_ev, sq_ev, qs_mm, q2_ev, rinv_ev, s_ev, es_ev, es4_ev = (ev(n) for n in ("rk_ready", "ss_ready", "sq_ready", "qs_mm", "q2_ready", "rinv_ready", "step_s_ready", "es_ready", "es4_ready"))
        ktr_mm, vtr_mm, gram_mm, kr_ev, vr_ev, ap_ev, ar_ev, al_ev = (
            [ev(f"{n}{hf}") for hf in range(2)] for n in ("ktr_mm", "vtr_mm", "gram_mm", "krow_ready", "vrow_ready", "ap_ready", "ar_ready", "al_ready"))
        kqg_ev = ev("kqg_ready")
        conv_ev = [ev(f"conv{tap}") for tap in range(TAPS)]
        v_ev, gate_ev = ev("v_ready"), ev("gate_ready")
        n_ev = ev("n_ready")
        ksum_ev = ev("ksum_ready")
        z_mm, z_ev, x_mm, x_ev, y_mm, y_ev = ([ev(f"{n}{l}") for l in range(LEVELS)] for n in ("z_mm", "z_ready", "x_mm", "x_ready", "y_mm", "y_ready"))
        m_mm, ix_ev, r_ev, yf_mm, yf_ev = ([ev(f"{n}{hf}") for hf in range(2)] for n in ("m_mm", "ix_ready", "resid_ready", "yf_mm", "yf_ready"))
        ks_mm, rhs_ev, w_mm, w_ev, s_mm, o_mm, sup_ev, mo_ev, fs_ev, fo_ev, osb_ev, ot_mm, og_ev, out_mm, acc_ev = (
            [ev(f"{n}{c}") for c in range(NCC)] for n in ("ks_mm", "rhs_ready", "w_mm", "w_ready", "snew_mm", "o_mm", "state_ready", "osum_ready", "osum_eps_ready", "oscale_ready", "o_ready", "ot_mm", "og_ready", "out_mm", "acc_ready"))
        staged, wt_ready, stage_free, gm_ready, zero_ready, rms_ready, identr_ready = (new_sem(n) for n in ("staged", "wt_ready", "stage_free", "gm_ready", "state_zeroed", "rms_ready", "identr_ready"))
        e_mm, g_mm, e_ex, g_ex = (new_sem(n) for n in ("e_mm", "g_mm", "e_exp", "g_exp"))

        with nc.Block() as b0:
            @b0.gpsimd
            def _(pool):
                for s in evs:
                    pool.sem_inc(s, CREDIT)

        NDMA = 7
        block = ctx.enter_context(nc.Block())
        LAST = KSTEPS - 1

        cur = Shared()

        def weave(order, segs, base, k, par, now):
            shift = {"P": 1, "I": 0, "R": -1, "G": 0}
            for part, name, *args in order:
                if part in now and name in segs:
                    if part == "P" and "R" in now and "I" not in now:
                        segs[name](base + KSTEPS, 0, 0, now, *args)
                    else:
                        d = shift[part]
                        segs[name](base + k + d, k + d, (par + d) % 2, now, *args)

        def program(eng, order, segs, start):
            cur.next = 0
            weave(order, segs, 0, 0, 0, "G")
            weave(order, segs, 0, -1, 1, "P")
            with eng.Fori(0, NH) as h:
                cur.head, cur.next = h, h + 1
                start(h)
                base = h * KSTEPS
                weave(order, segs, base, 0, 0, "PI")
                with eng.Fori(0, (KSTEPS - 2) // 2) as j:
                    weave(order, segs, base, j * 2 + 1, 1, "PIR")
                    weave(order, segs, base, j * 2 + 2, 0, "PIR")
                weave(order, segs, base, LAST, LAST % 2, "IRG")
                weave(order, segs, base, LAST + 1, (LAST + 1) % 2, "RP")

        def first_stage(k):
            return isinstance(k, int) and k == 0

        both = lambda name, *args: [("I", name, *args, hf) for hf in range(2)]
        ORDER = [
            ("R", "ks", 0), *both("gram"), *both("ap"), ("R", "rhs", 0), *both("vtr"), *both("ar"), *both("n"), ("R", "w", 0), ("R", "wev", 0),
            *both("vr"), ("G", "gm", 0), ("G", "gm", 1), ("G", "em", 0), ("P", "pt", 2, 0, 0), ("P", "pt", 2, 1, 0), ("P", "silu", 2),
            *both("z", 0), *both("zev", 0), ("G", "wt"), ("R", "so", 0), ("R", "sup", 0), ("R", "mo", 0), ("R", "fo", 0), *both("al"), ("I", "kqg"), ("P", "pt", 3, 0, 0), ("P", "pt", 3, 1, 0), ("P", "silu", 3),
            *both("x", 0), *both("xev", 0), ("G", "eex", 0), *both("y", 0), *both("yev", 0), ("P", "conv", 0), ("P", "pt", 0, 0, 0), ("R", "osb", 0), ("R", "ks", 1), ("R", "rhs", 1),
            ("R", "ot", 0), *both("z", 1), *both("zev", 1), ("G", "gmm", 0), ("P", "pt", 0, 0, 1), ("R", "og", 0), ("R", "w", 1), ("R", "wev", 1),
            *both("x", 1), *both("xev", 1), ("G", "gex", 0), ("G", "gm", 2), *both("y", 1), *both("yev", 1), ("P", "conv", 1), ("P", "pt", 0, 1, 0),
            ("R", "out", 0), *both("z", 2), *both("zev", 2), ("G", "em", 1), ("R", "acc", 0), ("R", "so", 1), ("R", "sup", 1), ("R", "mo", 1), ("R", "fo", 1),
            *both("x", 2), *both("xev", 2), ("G", "eex", 1), *both("y", 2), *both("yev", 2), ("P", "conv", 2), ("P", "pt", 0, 1, 1), ("P", "silu", 0), ("R", "osb", 1),
            ("R", "ot", 1), *both("z", 3), *both("zev", 3), ("G", "gmm", 1), ("P", "pt", 1, 0, 0), ("R", "og", 1),
            *both("x", 3), *both("xev", 3), ("G", "gex", 1), ("G", "gm", 3), *both("y", 3), *both("yev", 3), ("P", "conv", 3), ("P", "pt", 1, 0, 1),
            ("R", "out", 1), *both("z", 4), *both("zev", 4), ("G", "em", 2), ("P", "pt", 1, 1, 0), ("R", "acc", 1),
            *both("x", 4), *both("xev", 4), ("G", "eex", 2), *both("y", 4), *both("yev", 4), ("P", "pt", 1, 1, 1), ("P", "silu", 1), ("P", "gate"), ("P", "sq"),
            *both("z", 5), *both("zev", 5), ("G", "gmm", 2), ("P", "ktr", 0), ("P", "ksum", 0),
            *both("x", 5), *both("xev", 5), ("G", "gex", 2), *both("ix"), *both("y", 5), *both("yev", 5), ("P", "ktr", 1), ("P", "ksum", 1),
            ("P", "qs"), *both("m"), ("G", "em", 3), ("G", "eex", 3), *both("res"), ("P", "q2"), ("P", "sc"), *both("yf"), *both("yfev"), ("P", "vsilu"), ("P", "es4", 0), ("P", "es4", 1), ("P", "rk"), ("P", "kr", 0), ("P", "kr", 1),
        ]

        def bank(ps, hf, n=R):
            return ps[0:R, hf, 0:HU * n].rearrange("p (c n) -> p c n", n=n)

        def half(t, hf):
            return t[:, hf * HU:(hf + 1) * HU]

        def slot(ps, u, n):
            return ps[0:R, u // HU, (u % HU) * n:(u % HU + 1) * n]

        def kslot(u):
            return PP[u // HU][0:R, (u % HU) * 128:(u % HU + 1) * 128]

        def units_of(hf):
            return range(hf * HU, (hf + 1) * HU)

        @block.sync
        def _(sp):
            def load(m, h):
                sp.wait_ge(stage_free, m + 1)
                col = lambda w, n: g.dram[w].rearrange("d (i x c) -> d x i c", x=NH, c=128)[:, bass.ds(h, 1), :, :]
                sp.dma_start(stage_w[:, 0:3, :].unsqueeze(1), col("Wk", 3)).then_inc(staged, 16)
                sp.dma_start(stage_w[:, 3:4, :].unsqueeze(1), col("Wq", 1)).then_inc(staged, 16)
                sp.dma_start(stage_w[:, 4:7, :].unsqueeze(1), col("Wv", 3)).then_inc(staged, 16)
                sp.dma_start(stage_w[:, 7:8, :].unsqueeze(1), col("Wg", 1)).then_inc(staged, 16)
                sp.dma_start(stage_w[:, 8, :], g.dram["Wo"][bass.ds(h * 128, 128), :]).then_inc(staged, 16)
                tap = lambda w: g.dram[w].rearrange("(i x c) k -> x i (c k)", x=NH, c=128)
                for i in range(3):
                    sp.dma_start(stage_c[:, i, :, :], tap("conv_k")[bass.ds(h, 1), i, :].rearrange("a n -> (a n)").partition_broadcast(128)).then_inc(staged, 16)
                sp.dma_start(stage_v[:, :, :].unsqueeze(1), g.dram["conv_v"].rearrange("(i x c) k -> c x i k", x=NH, c=128)[:, bass.ds(h, 1), :, :]).then_inc(staged, 16)
                sp.dma_start(stage_c[:, 3, :, :], tap("conv_q")[bass.ds(h, 1), 0, :].rearrange("a n -> (a n)").partition_broadcast(128)).then_inc(staged, 16)

            with sp.Fori(0, NH) as h:
                load(h, h)
            load(NH, 0)

        @block.gpsimd
        def _(pool):
            def start(h):
                pool.wait_ge(g_ex, h * 4 + 4)

            def s_gm(N, k, par, now, i):
                if i >= 2 or "I" in now:
                    pool.wait_ge(g_mm, cur.next * 4 + i - 1)
                v = lambda t: t.rearrange("j (b c) t -> j b c t", b=B)
                nc.gpsimd.tensor_tensor(v(gm[i % 2][:, :, :]), g.gt[:, :, :].rearrange("j (b q c) h -> j q b c h", b=B, q=4)[:, i, :, :, bass.ds(cur.next, 1)].broadcast_to([TC, B, T // TC // 4, TC]),
                                        g.upto[:, :].unsqueeze(1).unsqueeze(1).broadcast_to([TC, B, T // TC // 4, TC]), ALU.mult).then_inc(gm_ready, 1)

            def s_sq(N, k, par, now):
                pool.wait_ge(silu[1], done(N))
                pool.wait_ge(qs_mm, done(N - 1))
                qv = kq[par][:, :, 3, :].rearrange("p (b c) t -> p b c t", c=NCC)
                nc.gpsimd.tensor_tensor(sqq[:, :, :, :].rearrange("p c b t -> p b c t"), qv, qv, ALU.mult).then_inc(sq_ev, 1)

            def s_es4(N, k, par, now, hf):
                pool.wait_ge(es_ev, done(N))
                pool.wait_ge(ap_ev[hf], done(N - 1))
                nc.gpsimd.tensor_tensor(half(es4, hf), half(es[par], hf).unsqueeze(2).broadcast_to([R, HU, 4, TC]),
                                        g.mask4[:, :].rearrange("p (i t) -> p i t", i=4).unsqueeze(1).broadcast_to([R, HU, 4, TC]), ALU.mult).then_inc(es4_ev, 1)

            def s_kqg(N, k, par, now):
                pool.wait_ge(o_mm[1], done(N - 2))
                kv = kq[par][:, :, :, :].rearrange("p (b c) i t -> p b c i t", c=NCC)
                ov = kqg[par][:, :, :, :].rearrange("p (b c) i t -> p b c i t", c=NCC)
                for cc in range(NCC):
                    d = gdec[:, :, bass.ds(k * SPAN + cc * TC, TC)].unsqueeze(2).broadcast_to([128, B, 4, TC])
                    last = nc.gpsimd.tensor_tensor(ov[:, :, cc], kv[:, :, cc], d, ALU.mult)
                last.then_inc(kqg_ev, 1)

            def s_rk(N, k, par, now):
                pool.wait_ge(ss_ev, done(N))
                pool.wait_ge(vr_ev[1], done(N - 2))
                nc.gpsimd.tensor_tensor(rk[par][:, :], ss[:, :], g.half[0:R, :], ALU.pow).then_inc(rk_ev, 1)

            def s_fo(N, k, par, now, cc):
                pool.wait_ge(mo_ev[cc], done(N))
                pool.wait_ge(osb_ev[cc], done(N - 1))
                nc.gpsimd.tensor_tensor(fo[:, cc:cc + 1], mo[:, cc:cc + 1], q2[par][:, cc:cc + 1], ALU.add).then_inc(fs_ev[cc], 1)
                pool.wait_ge(fs_ev[cc], done(N))
                nc.gpsimd.tensor_tensor(fo[:, cc:cc + 1], fo[:, cc:cc + 1], g.minus_half[:, 0:1], ALU.pow).then_inc(fo_ev[cc], 1)

            def s_al(N, k, par, now, hf):
                pool.wait_ge(ar_ev[hf], done(N))
                pool.wait_ge(m_mm[hf], done(N - 1))
                nc.gpsimd.tensor_tensor(half(al, hf), half(ap[par], hf)[:, :, 0:R], half(ar, hf), ALU.subtract).then_inc(al_ev[hf], 1)

            def s_n(N, k, par, now, hf):
                pool.wait_ge(ar_ev[hf], done(N))
                pool.wait_ge(yf_ev[hf], done(N - 1))
                nc.gpsimd.tensor_tensor(half(Yr, hf), half(ar, hf), g.lev[:, LEVELS * R:].unsqueeze(1).broadcast_to([R, HU, R]), ALU.mult).then_inc(n_ev, 1)

            def s_ix(N, k, par, now, hf):
                pool.wait_ge(x_ev[LEVELS - 1], done_half(N, hf))
                pool.wait_ge(r_ev[hf], done(N - 1))
                nc.gpsimd.tensor_tensor(half(ix, hf), g.ident[0:R, 0:R].unsqueeze(1).broadcast_to([R, HU, R]), half(Xr, hf), ALU.subtract).then_inc(ix_ev[hf], 1)

            program(pool, ORDER, {"gm": s_gm, "n": s_n, "sq": s_sq, "rk": s_rk, "fo": s_fo, "es4": s_es4, "al": s_al, "kqg": s_kqg, "ix": s_ix}, start)

        @block.scalar
        def _(act):
            def exp_of(dst, src, i):
                for a in range(2):
                    last = nc.scalar.activation(dst[:, 2 * a:2 * a + 2, T // 4 * i:T // 4 * (i + 1)], src(a).rearrange("p (b t) -> p b t", b=2), ACT.Exp)
                return last

            def start(h):
                act.wait_ge(g_mm, h * 4 + 4)
                act.wait_ge(sup_ev[1], done(h * KSTEPS - 1))
                act.wait_ge(kqg_ev, done(h * KSTEPS - 1))
                exp_of(gdec, lambda a: G2[:, a, :], 3).then_inc(g_ex, 1)

            def s_eex(N, k, par, now, i):
                act.wait_ge(e_mm, cur.next * 4 + i + 1)
                if "I" in now:
                    act.wait_ge(es_ev, done(N))
                exp_of(edec, lambda a: PP[a][0:R, :], i).then_inc(e_ex, 1)

            def s_gex(N, k, par, now, i):
                act.wait_ge(g_mm, cur.next * 4 + i + 1)
                if "I" in now:
                    act.wait_ge(sup_ev[1], done(N - 2))
                    act.wait_ge(kqg_ev, done(N - 1))
                exp_of(gdec, lambda a: PP[a][:, :], i).then_inc(g_ex, 1)

            def s_silu(N, k, par, now, q):
                act.wait_ge(proj[q], done(N))
                src = PP[q % 2][:, :].rearrange("p (a u t) -> p a u t", a=2, t=TC)
                if q == 0:
                    act.wait_ge(kqg_ev, done(N - 2))
                    nc.scalar.activation(kq[par][:, :, 0:2, :].rearrange("p u i t -> p i u t"), src, ACT.Silu).then_inc(silu[q], 1)
                elif q == 1:
                    nc.scalar.activation(kq[par][:, :, 2:4, :].rearrange("p u i t -> p i u t"), src, ACT.Silu).then_inc(silu[q], 1)
                elif q == 2:
                    act.wait_ge(conv_ev[TAPS - 1], done(N - 1))
                    act.wait_ge(silu[3], done(N - 1))
                    old = g.xn[:, :, 0:PAD].unsqueeze(1).broadcast_to([128, NHH, B, PAD]) if first_stage(k) else raw[1 - par][:, :, :, SPAN:]
                    nc.scalar.activation(raw[par][:, :, :, 0:PAD], old, ACT.Copy)
                    nc.scalar.activation(raw[par][:, 0:2, :, PAD:], PP[0][:, :].rearrange("p (a b t) -> p a b t", a=2, b=B), ACT.Copy).then_inc(silu[q], 1)
                else:
                    nc.scalar.activation(raw[par][:, 2, :, PAD:], PP[1][:, 0:B * SPAN].rearrange("p (b t) -> p b t", b=B), ACT.Copy)
                    act.wait_ge(gate_ev, done(N - 1))
                    nc.scalar.activation(gate_raw[:, :, :], src[:, 1], ACT.Copy).then_inc(silu[q], 1)

            def s_gate(N, k, par, now):
                act.wait_ge(silu[3], done(N))
                act.wait_ge(og_ev[1], done(N - 2))
                nc.scalar.activation(gate[par][:, :, :], gate_raw[:, :, :], ACT.Silu).then_inc(gate_ev, 1)

            def s_vsilu(N, k, par, now):
                act.wait_ge(conv_ev[TAPS - 1], done(N))
                act.wait_ge(vtr_mm[1], done(N - 2))
                nc.scalar.activation(vt[par][:, :, :, :].rearrange("p u i t -> p i u t"), conv[:, :, :, :].rearrange("p i b (c t) -> p i (b c) t", t=TC), ACT.Silu).then_inc(v_ev, 1)

            def s_xev(N, k, par, now, l, hf):
                act.wait_ge(x_mm[l], done_half(N, hf))
                if l == 0:
                    act.wait_ge(ix_ev[hf], done(N - 1))
                nc.scalar.activation(half(Xr, hf), bank(L2, hf), ACT.Copy).then_inc(x_ev[l], 1)

            def s_ar(N, k, par, now, hf):
                act.wait_ge(ap_ev[hf], done(N))
                act.wait_ge(m_mm[hf], done(N - 1))
                act.wait_ge(al_ev[hf], done(N - 1))
                nc.scalar.activation(half(ar, hf), half(ap[par], hf)[:, :, 0:R], ACT.Copy).then_inc(ar_ev[hf], 1)

            def s_ksum(N, k, par, now, hf):
                act.wait_ge(ktr_mm[hf], done(N))
                act.wait_ge(ss_ev, done(N - 1))
                for u in units_of(hf):
                    last = nc.scalar.activation(ksq[:, u, :], kslot(u), ACT.Square, accum_out=ksum[:, u:u + 1])
                last.then_inc(ksum_ev, 1)

            def s_wev(N, k, par, now, cc):
                act.wait_ge(w_mm[cc], done(N))
                nc.scalar.activation(ws[:, :, :], RB[0:R, :].rearrange("p (b n) -> p b n", b=B), ACT.Copy).then_inc(w_ev[cc], 1)

            def s_mo(N, k, par, now, cc):
                act.wait_ge(o_mm[cc], done(N))
                act.wait_ge(fo_ev[1 - cc], done(N) if cc else done(N - 1))
                nc.scalar.activation(osq[:, :], RB[:, 0:128], ACT.Square, accum_out=mo[:, cc:cc + 1]).then_inc(mo_ev[cc], 1)

            program(act, ORDER, {"vsilu": s_vsilu, "gate": s_gate, "eex": s_eex, "gex": s_gex, "ksum": s_ksum, "silu": s_silu, "ar": s_ar, "xev": s_xev, "wev": s_wev, "mo": s_mo}, start)

        @block.vector
        def _(dve):
            dve.wait_ge(g.rms_sem, 16)
            nc.vector.tensor_scalar(rmsw[:, :], g.rms_in[:, :], math.sqrt(128.0), None, ALU.mult).then_inc(rms_ready, 1)
            dve.wait_ge(rms_ready, 1)
            nc.vector.tensor_copy(ident_r[:, :], g.ident[0:R, 0:R])
            nc.vector.tensor_copy(ident_h[:, :, :], g.ident[0:R, 0:R].unsqueeze(1).broadcast_to([R, HU, R])).then_inc(identr_ready, 1)
            nc.vector.memset(stage_w[:, 0, 0:1], 0.0).then_inc(stage_free, 1)

            def start(h):
                dve.wait_ge(out_mm[1], done(h * KSTEPS - 1))
                nc.vector.tensor_copy(wgo[:, 1, :], stage_w[:, 8, :]).then_inc(stage_free, 1)
                nc.vector.memset(S[:, :, :], 0.0).then_inc(zero_ready, 1)

            def s_wt(N, k, par, now):
                dve.wait_ge(staged, (cur.next + 1) * (16 * (5 + 3 + 2)))
                if "I" in now:
                    dve.wait_ge(proj[1], done(N))
                    dve.wait_ge(conv_ev[TAPS - 1], done(N))
                nc.vector.tensor_copy(wv[:, :, :], stage_w[:, 4:7, :])
                nc.vector.tensor_copy(taps_v[:, :, :], stage_v[:, :, :])
                nc.vector.tensor_tensor(wt[:, :, :, :], stage_w[:, 0:4, :].unsqueeze(2).broadcast_to([128, 4, TAPS, 128]),
                                        stage_c[:, :, :, :].rearrange("p a c k -> p a k c"), ALU.mult)
                nc.vector.tensor_copy(wgo[:, 0, :], stage_w[:, 7, :]).then_inc(wt_ready, 1)

            def s_q2(N, k, par, now):
                dve.wait_ge(qs_mm, done(N))
                dve.wait_ge(fs_ev[1], done(N - 2))
                nc.vector.tensor_scalar(q2[par][:, :], L2[:, 1, 384:384 + NCC], 1e-5 * 128 * 128, 1e-6 * 1e-5 * 128 * 128, ALU.mult, ALU.add).then_inc(q2_ev, 1)

            def s_sc(N, k, par, now):
                dve.wait_ge(ksum_ev, done_half(N, 1))
                dve.wait_ge(rk_ev, done(N - 1))
                nc.vector.tensor_scalar(ss[:, :], ksum[:, :], 1e-6, None, ALU.add).then_inc(ss_ev, 1)
                dve.wait_ge(ss_ev, done(N))
                nc.vector.reciprocal(rinv[:, :], ss[:, :]).then_inc(rinv_ev, 1)
                head = cur.head
                if first_stage(k):
                    head = cur.next
                    dve.wait_ge(e_ex, head * 4 + 4)
                dve.wait_ge(rinv_ev, done(N))
                nc.vector.tensor_tensor(step_s[:, :].rearrange("p (b c) -> p b c", c=NCC), rinv[:, :].rearrange("p (b c) -> p b c", c=NCC),
                                        g.beta[:, bass.ds(head, 1), :].rearrange("p x (b c) -> p (x b) c", b=B)[:, :, bass.ds(k * NCC, NCC)], ALU.mult).then_inc(s_ev, 1)
                dve.wait_ge(s_ev, done(N))
                nc.vector.tensor_tensor(es[par][:, :, :].rearrange("p (b c) t -> p b c t", c=NCC),
                                        edec[:, :, bass.ds(k * SPAN, SPAN)].rearrange("p b (c t) -> p b c t", c=NCC),
                                        step_s[:, :].rearrange("p (b c) -> p b c", c=NCC).unsqueeze(3).broadcast_to([R, B, NCC, TC]), ALU.mult).then_inc(es_ev, 1)

            def s_kr(N, k, par, now, hf):
                dve.wait_ge(ktr_mm[hf], done(N))
                dve.wait_ge(es_ev, done(N))
                dve.wait_ge(s_mm[1], done(N - 2))
                nc.vector.tensor_tensor(half(krow[par], hf), PP[hf][0:R, :].rearrange("p (c n) -> p c n", n=128), half(es[par], hf)[:, :, TC - 1:TC].broadcast_to([R, HU, 128]), ALU.mult).then_inc(kr_ev[hf], 1)

            def s_vr(N, k, par, now, hf):
                dve.wait_ge(vtr_mm[hf], done(N))
                dve.wait_ge(rk_ev, done(N))
                nc.vector.tensor_tensor(half(vrow[par], hf), bank(L2, hf, 128), half(rk[par], hf).unsqueeze(2).broadcast_to([R, HU, 128]), ALU.mult).then_inc(vr_ev[hf], 1)

            def s_ap(N, k, par, now, hf):
                dve.wait_ge(gram_mm[hf], done(N))
                dve.wait_ge(es4_ev, done_half(N, hf))
                dve.wait_ge(o_mm[1], done(N - 2))
                nc.vector.tensor_tensor(half(ap[par], hf), bank(G2, hf, 128), half(es4, hf).rearrange("p u i t -> p u (i t)"), ALU.mult).then_inc(ap_ev[hf], 1)

            def s_zev(N, k, par, now, l, hf):
                dve.wait_ge(z_mm[l], done_half(N, hf))
                mask = g.lev[:, l * R:(l + 1) * R].unsqueeze(1).broadcast_to([R, HU, R])
                nc.vector.tensor_tensor(half(Zr, hf), bank(L2, hf), mask, ALU.mult).then_inc(z_ev[l], 1)

            def s_yev(N, k, par, now, l, hf):
                dve.wait_ge(y_mm[l], done_half(N, hf))
                old = g.ident[0:R, 0:R].unsqueeze(1).broadcast_to([R, HU, R]) if l == 0 else half(Yr, hf)
                nc.vector.tensor_tensor(half(Yr, hf), bank(G2, hf), old, ALU.add).then_inc(y_ev[l], 1)

            def s_res(N, k, par, now, hf):
                dve.wait_ge(m_mm[hf], done(N))
                dve.wait_ge(ix_ev[hf], done(N))
                nc.vector.tensor_tensor(half(Zr, hf), half(ix, hf), bank(L2, hf), ALU.subtract).then_inc(r_ev[hf], 1)

            def s_yfev(N, k, par, now, hf):
                dve.wait_ge(yf_mm[hf], done(N))
                nc.vector.tensor_tensor(half(yf[par], hf), bank(G2, hf), half(Yr, hf), ALU.add).then_inc(yf_ev[hf], 1)

            def s_conv(N, k, par, now, tap):
                if tap == 0:
                    dve.wait_ge(silu[2], done(N))
                    dve.wait_ge(silu[3], done(N))
                    dve.wait_ge(v_ev, done(N - 1))
                else:
                    dve.wait_ge(conv_ev[tap - 1], done(N))
                for i in range(NHH):
                    x, w = raw[par][:, i, :, tap:tap + SPAN], taps_v[:, i, tap:tap + 1]
                    if tap == 0:
                        last = nc.vector.tensor_scalar(conv[:, i], x, w, None, ALU.mult)
                    else:
                        last = nc.vector.scalar_tensor_tensor(conv[:, i], x, w, conv[:, i], ALU.mult, ALU.add)
                last.then_inc(conv_ev[tap], 1)

            def s_rhs(N, k, par, now, cc):
                dve.wait_ge(ks_mm[cc], done(N))
                v = vrow[par][:, :, :].rearrange("p (b c) n -> p b c n", c=NCC)[:, :, cc, :]
                nc.vector.tensor_tensor(rhs[:, :, :], v, RA[0:R, :].rearrange("p (b n) -> p b n", b=B), ALU.subtract).then_inc(rhs_ev[cc], 1)

            def s_sup(N, k, par, now, cc):
                dve.wait_ge(s_mm[cc], done(N))
                dve.wait_ge(o_mm[cc], done(N))
                for b in range(B):
                    last = nc.vector.scalar_tensor_tensor(S[:, b, :], S[:, b, :], gdec[:, b, bass.ds(k * SPAN + cc * TC + TC - 1, 1)],
                                                          RA[:, b * 128:(b + 1) * 128], ALU.mult, ALU.add)
                last.then_inc(sup_ev[cc], 1)

            def s_osb(N, k, par, now, cc):
                dve.wait_ge(fo_ev[cc], done(N))
                nc.vector.tensor_scalar(osb[:, cc, :], RB[:, 0:128], fo[:, cc:cc + 1], None, ALU.mult).then_inc(osb_ev[cc], 1)

            def s_og(N, k, par, now, cc):
                dve.wait_ge(ot_mm[cc], done(N))
                dve.wait_ge(gate_ev, done(N))
                gv = gate[par][:, :, :].rearrange("p (b c) t -> p b c t", c=NCC)[:, :, cc, :]
                nc.vector.scalar_tensor_tensor(og[:, cc, :].rearrange("p (b t) -> p b t", b=B), side.rearrange("p (b t) -> p b t", b=B),
                                               rmsw[:, :], gv, ALU.mult, ALU.mult).then_inc(og_ev[cc], 1)

            def s_acc(N, k, par, now, cc):
                dve.wait_ge(out_mm[cc], done(N))
                x = g.xT[:, :, bass.ds(k * SPAN + cc * TC, TC)]
                nc.vector.tensor_tensor(x, side.rearrange("p (b t) -> p b t", b=B), x, ALU.add).then_inc(acc_ev[cc], 1)

            program(dve, ORDER, {"wt": s_wt, "conv": s_conv, "q2": s_q2, "sc": s_sc, "kr": s_kr, "vr": s_vr, "ap": s_ap, "zev": s_zev, "yev": s_yev, "res": s_res,
                                 "yfev": s_yfev, "rhs": s_rhs, "sup": s_sup, "osb": s_osb, "og": s_og, "acc": s_acc}, start)

        @block.tensor
        def _(pe):
            mm = nc.tensor.matmul
            pe.wait_ge(identr_ready, 1)

            def start(h):
                pe.wait_ge(yf_ev[1], done(h * KSTEPS - 1))
                for a in range(2):
                    last = mm(G2[:, a, :], g.ones[0:TC, :], gm[1][:, 16 * a:16 * (a + 1), :], start=True, stop=True)
                last.then_inc(g_mm, 1)
                pe.wait_ge(zero_ready, h + 1)
                pe.wait_ge(g_ex, h * 4 + 4)

            def s_em(N, k, par, now, i):
                pe.wait_ge(gm_ready, cur.next * 4 + i + 1)
                if i:
                    pe.wait_ge(g_ex, cur.next * 4 + i)
                elif "I" in now:
                    pe.wait_ge(kr_ev[0], done(N))
                    pe.wait_ge(kr_ev[1], done(N))
                for a in range(2):
                    last = mm(PP[a][0:R, :], g.after[:, :], gm[i % 2][:, 16 * a:16 * (a + 1), :], start=True, stop=True)
                last.then_inc(e_mm, 1)

            def s_gmm(N, k, par, now, i):
                pe.wait_ge(e_ex, cur.next * 4 + i + 1)
                for a in range(2):
                    last = mm(PP[a][:, :], g.ones[0:TC, :], gm[i % 2][:, 16 * a:16 * (a + 1), :], start=True, stop=True)
                last.then_inc(g_mm, 1)

            def s_pt(N, k, par, now, q, a, part):
                if first_stage(k) and (q, a, part) == (2, 0, 0):
                    pe.wait_ge(wt_ready, cur.next + 1)
                    pe.wait_ge(e_ex, cur.next * 4 + 4)
                if part or a:
                    pass
                elif q >= 2:
                    pe.wait_ge(kr_ev[q - 2], done(N - 1))
                else:
                    pe.wait_ge(silu[q + 2], done(N))
                tile = 2 * q + a
                out = PP[q % 2][:, a * 256:(a + 1) * 256].rearrange("p (b t) -> p b t", b=B)
                if tile < 4:
                    for tap in range(part * TAPS // 2, (part + 1) * TAPS // 2):
                        last = mm(out, wt[:, tile, tap, :], g.xn[:, :, bass.ds(k * SPAN + tap, SPAN)], start=tap == 0, stop=tap == TAPS - 1)
                else:
                    last = mm(out, wgo[:, 0, :] if tile == 7 else wv[:, tile - 4, :], g.xn[:, :, bass.ds(k * SPAN + PAD, SPAN)], start=True, stop=True)
                if (a and part) or (a and tile >= 4):
                    last.then_inc(proj[q], 1)

            def s_ktr(N, k, par, now, hf):
                pe.wait_ge(silu[1], done(N))
                pe.wait_ge(silu[hf], done(N))
                for u in units_of(hf):
                    last = nc.tensor.transpose(kslot(u), kq[par][:, u, 0:3, :].rearrange("p i t -> p (i t)"), g.ident[:, :])
                last.then_inc(ktr_mm[hf], 1)

            def s_qs(N, k, par, now):
                pe.wait_ge(sq_ev, done(N))
                if "I" in now:
                    pe.wait_ge(x_ev[LEVELS - 1], done_half(N - 1, 1))
                else:
                    pe.wait_ge(acc_ev[1], done(N - 1))
                for cc in range(NCC):
                    last = mm(L2[:, 1, 384 + cc:385 + cc], sqq[:, cc, :, :].rearrange("p b t -> p (b t)"), g.ones[:, 0:1], start=True, stop=True)
                last.then_inc(qs_mm, 1)

            def s_vtr(N, k, par, now, hf):
                pe.wait_ge(v_ev, done(N))
                pe.wait_ge(q2_ev, done(N))
                pe.wait_ge(r_ev[hf], done(N - 1))
                for u in units_of(hf):
                    last = nc.tensor.transpose(slot(L2, u, 128), vt[par][:, u, :, :].rearrange("p i t -> p (i t)"), g.ident[:, :])
                last.then_inc(vtr_mm[hf], 1)

            def s_gram(N, k, par, now, hf):
                pe.wait_ge(yf_ev[hf], done(N - 1))
                for u in units_of(hf):
                    v = kq[par][:, u, :, :].rearrange("p i t -> p (i t)")
                    last = mm(slot(G2, u, 128), v[:, 0:R], v, start=True, stop=True)
                last.then_inc(gram_mm[hf], 1)

            def s_z(N, k, par, now, l, hf):
                if l:
                    pe.wait_ge(x_ev[l - 1], done_half(N, hf))
                else:
                    pe.wait_ge(ar_ev[hf], done(N))
                    pe.wait_ge(vr_ev[hf], done(N))
                for u in units_of(hf):
                    last = mm(slot(L2, u, R), ar[:, u, :], ident_r[:, :] if l == 0 else Xr[:, u, :], start=True, stop=True)
                last.then_inc(z_mm[l], 1)

            def s_x(N, k, par, now, l, hf):
                pe.wait_ge(z_ev[l], done_half(N, hf))
                if l:
                    pe.wait_ge(y_ev[l - 1], done_half(N, hf))
                if "R" in now and 0 < l < 5 and hf == 1:
                    pe.wait_ge((og_ev[0], acc_ev[0], og_ev[1], acc_ev[1])[l - 1], done(N - 1))
                mm(bank(L2, hf), ident_r[:, :], ident_h[:, :, :] if l == 0 else half(Xr, hf), start=True, stop=False)
                if l == 0:
                    pe.wait_ge(n_ev, done_half(N, hf))
                    mm(bank(L2, hf), ident_r[:, :], half(Zr, hf), start=False, stop=False)
                for u in units_of(hf):
                    last = mm(slot(L2, u, R), Yr[:, u, :], Zr[:, u, :], start=False, stop=u % HU == HU - 1)
                last.then_inc(x_mm[l], 1)

            def s_y(N, k, par, now, l, hf):
                if l == 0:
                    mm(bank(G2, hf), ident_r[:, :], half(Yr, hf), start=True, stop=False)
                for u in units_of(hf):
                    last = mm(slot(G2, u, R), Zr[:, u, :], Yr[:, u, :], start=l > 0, stop=l > 0 or u % HU == HU - 1)
                last.then_inc(y_mm[l], 1)

            def s_m(N, k, par, now, hf):
                pe.wait_ge(x_ev[LEVELS - 1], done_half(N, hf))
                pe.wait_ge(al_ev[hf], done(N))
                for u in units_of(hf):
                    mm(slot(L2, u, R), ar[:, u, :], Xr[:, u, :], start=True, stop=False)
                    last = mm(slot(L2, u, R), al[:, u, :], Xr[:, u, :], start=False, stop=True)
                last.then_inc(m_mm[hf], 1)

            def s_yf(N, k, par, now, hf):
                pe.wait_ge(r_ev[hf], done(N))
                pe.wait_ge(y_ev[LEVELS - 1], done_half(N, hf))
                for u in units_of(hf):
                    last = mm(slot(G2, u, R), Zr[:, u, :], Yr[:, u, :], start=True, stop=True)
                last.then_inc(yf_mm[hf], 1)

            def s_ks(N, k, par, now, cc):
                pe.wait_ge(kqg_ev, done(N))
                pe.wait_ge(sup_ev[1 - cc], done(N) if cc else done(N - 1))
                for b in range(B):
                    u = b * NCC + cc
                    last = mm(RA[0:R, b * 128:(b + 1) * 128], kqg[par][:, u, 0:3, :].rearrange("p i t -> p (i t)"), S[:, b, :], start=True, stop=True)
                last.then_inc(ks_mm[cc], 1)

            def s_w(N, k, par, now, cc):
                pe.wait_ge(rhs_ev[cc], done(N))
                pe.wait_ge(yf_ev[1], done(N))
                pe.wait_ge(osb_ev[1 - cc], done(N) if cc else done(N - 1))
                for b in range(B):
                    last = mm(RB[0:R, b * 128:(b + 1) * 128], yf[par][:, b * NCC + cc, :], rhs[:, b, :], start=True, stop=True)
                last.then_inc(w_mm[cc], 1)

            def s_so(N, k, par, now, cc):
                pe.wait_ge(w_ev[cc], done(N))
                for b in range(B):
                    last = mm(RA[:, b * 128:(b + 1) * 128], krow[par][:, b * NCC + cc, :], ws[:, b, :], start=True, stop=True)
                last.then_inc(s_mm[cc], 1)
                for b in range(B):
                    u = b * NCC + cc
                    o = RB[b * TC:(b + 1) * TC, 0:128]
                    mm(o, kqg[par][:, u, 3, :], S[:, b, :], start=True, stop=False)
                    last = mm(o, ap[par][:, u, R:R + TC], ws[:, b, :], start=False, stop=True)
                last.then_inc(o_mm[cc], 1)

            def s_ot(N, k, par, now, cc):
                pe.wait_ge(osb_ev[cc], done(N))
                if "I" in now:
                    pe.wait_ge(x_ev[2 if cc else 0], done_half(N + 1, 1))
                elif cc:
                    pe.wait_ge(acc_ev[0], done(N))
                nc.tensor.transpose(side, osb[:, cc, :], g.ident[:, :]).then_inc(ot_mm[cc], 1)

            def s_out(N, k, par, now, cc):
                pe.wait_ge(og_ev[cc], done(N))
                if "I" in now:
                    pe.wait_ge(x_ev[3 if cc else 1], done_half(N + 1, 1))
                mm(side, wgo[:, 1, :], og[:, cc, :], start=True, stop=True).then_inc(out_mm[cc], 1)

            program(pe, ORDER, {"em": s_em, "gmm": s_gmm, "pt": s_pt, "ktr": s_ktr, "qs": s_qs, "vtr": s_vtr, "gram": s_gram, "z": s_z, "x": s_x, "y": s_y, "m": s_m,
                                "yf": s_yf, "ks": s_ks, "w": s_w, "so": s_so, "ot": s_ot, "out": s_out}, start)


def mixture(nc, g, tag):
    NE = E_N + 1
    with ExitStack() as ctx:
        new_sem = semaphores(nc, ctx)
        sb = lambda n, s, dt=F32: ctx.enter_context(nc.sbuf_tensor(tag + n, s, dt))
        pb = lambda n, s: ctx.enter_context(nc.psum_tensor(tag + n, s, F32))
        sem = lambda n: new_sem(tag + n)
        w1, w2 = sb("w1", [128, NE, 128]), sb("w2", [128, NE, 128])
        b1, b2 = sb("b1", [128, NE]), sb("b2", [NE, 128])
        rw, rb = sb("rw", [128, NE]), sb("rb", [NE, 1])
        self32 = sb("sel32", [96, E_N * 128])
        sel = sb("sel", [96, E_N, 128], BF16)
        lt = sb("lt", [NE, TILE])
        lg = sb("lg", [128, 4, NE])
        mx = sb("mx", [128, 4])
        den = sb("den", [128, 4])
        p20 = sb("p20", [128, 4, 20])
        m20 = sb("m20", [128, 4, 20])
        top = sb("top", [128, 4, 8])
        held = sb("held", [128, 2])
        cw = sb("cw", [128, 4, NE])
        cwt = [sb(f"cwt{i}", [NE, TILE]) for i in range(2)]
        rest = sb("rest", [NE, 2, TILE])
        midw = sb("midw", [NE, TILE], BF16)
        parts = [sb(f"parts{i}", [96, TILE], BF16) for i in range(2)]
        hr, hs = sb("hr", [128, 2, TILE]), sb("hs", [128, 2, TILE])
        ph, pc, py = ([pb(f"{n}{i}", [128, TILE]) for i in range(2)] for n in ("ph", "pc", "py"))
        pl, pt = pb("pl", [128, TILE]), pb("pt", [128, TILE])
        evs = []

        def ev(n):
            evs.append(sem(n))
            return evs[-1]

        hc_mm, relu, hs_ev, y_mm = ([ev(f"{n}{e}") for e in range(NE)] for n in ("hc_mm", "relu", "scaled", "y_mm"))
        lt_mm, lt_ev, tr_mm, mx_ev, sub_ev, exp_ev, den_ev, rden_ev, p_ev, top_ev, topf_ev, m_ev, cw_ev, ct_mm, ct_ev = (
            ev(n) for n in ("lt_mm", "lt_ready", "tr_mm", "max_ready", "sub_ready", "exp_ready", "den_ready", "rden_ready", "p_ready",
                            "top_ready", "top3_ready", "match_ready", "cw_ready", "ct_mm", "cwt_ready"))
        hi_ev, r1_ev, mid_ev, r2_ev, parts_ev, acc_ev = (ev(n) for n in ("hi_ready", "r1_ready", "mid_ready", "r2_ready", "parts_ready", "acc_ready"))
        loaded, zeroed, const = sem("loaded"), sem("zeroed"), sem("const")
        with nc.Block() as b0:
            @b0.gpsimd
            def _(pool):
                for s in evs:
                    pool.sem_inc(s, CREDIT)
        block = ctx.enter_context(nc.Block())
        d = g.dram
        loads = [(w1[:, 0:E_N, :], d["eW1"].rearrange("e d h -> d e h")), (w1[:, E_N, :], d["sW1"]),
                 (w2[:, 0:E_N, :], d["eW2"].rearrange("e d h -> d e h")), (w2[:, E_N, :], d["sW2"]),
                 (b1[:, 0:E_N], d["eb1"].rearrange("e h -> h e")), (b1[:, E_N:NE], d["sb1"].unsqueeze(1)),
                 (b2[0:E_N, :], d["eb2"]), (b2[E_N:NE, :], d["sb2"].unsqueeze(0)),
                 (rw[:, 0:E_N], d["router_W"]), (rb[0:E_N, :], d["router_b"].unsqueeze(1)), (self32[:, :], d["c_sel"])]
        NPAIR = NT // 2

        def tiles(eng, step, lead):
            lead(0, 0, 0)
            with eng.Fori(0, NPAIR - 1) as j:
                step(j * 2, j, 0, j * 2 + 1, j)
                step(j * 2 + 1, j, 1, j * 2 + 2, j + 1)
            step(NT - 2, NPAIR - 1, 0, NT - 1, NPAIR - 1)
            step(NT - 1, NPAIR - 1, 1, None, None)

        def xn(j, par):
            return g.xn[:, bass.ds(j, 1), PAD + TILE * par:PAD + TILE * (par + 1)]

        @block.sync
        def _(sp):
            sp.wait_ge(zeroed, 1)
            for dst, src in loads:
                sp.dma_start(dst, src, allow_slow_non_contiguous=True).then_inc(loaded, 16)

        @block.tensor
        def _(pe):
            mm = nc.tensor.matmul
            pe.wait_ge(loaded, 16 * len(loads))
            pe.wait_ge(const, 1)

            def r_lt(n, j, par):
                pe.wait_ge(ct_ev, done(n - 1))
                pe.wait_ge(r1_ev, done(n - 1))
                mm(pl[0:NE, :], rw[:, :], xn(j, par), start=True, stop=True).then_inc(lt_mm, 1)

            def r_tr(n):
                pe.wait_ge(lt_ev, done(n))
                pe.wait_ge(sub_ev, done(n - 1))
                for a in range(4):
                    last = mm(pt[:, a * NE:(a + 1) * NE], lt[:, a * 128:(a + 1) * 128], g.ident[0:NE, 0:NE], start=True, stop=True)
                last.then_inc(tr_mm, 1)

            def r_ct(n):
                pe.wait_ge(cw_ev, done(n))
                for a in range(4):
                    last = nc.tensor.transpose(pl[0:NE, a * 128:(a + 1) * 128], cw[:, a, :], g.ident[:, :])
                last.then_inc(ct_mm, 1)

            def lead(n, j, par):
                r_lt(n, j, par)
                r_tr(n)
                r_ct(n)

            def step(n, j, par, n1, j1):
                def hidden(e):
                    if e < NE:
                        pe.wait_ge(relu[e - 2], done(n) if e >= 2 else done(n - 1))
                        pe.wait_ge(hs_ev[e - 2], done(n) if e >= 2 else done(n - 1))
                        last = mm(ph[e % 2][:, :], w1[:, e, :], xn(j, par), start=True, stop=True)
                        if e < E_N:
                            last = mm(pc[e % 2][:, :], sel[:, e, :], parts[par][:, :], start=True, stop=True)
                        last.then_inc(hc_mm[e], 1)
                pe.wait_ge(parts_ev, done(n))
                hidden(0)
                pe.wait_ge(acc_ev, done(n - 2))
                mm(py[par][:, :], b2[:, :], cwt[par][:, :], start=True, stop=False)
                for e in range(NE):
                    hidden(e + 1)
                    pe.wait_ge(hs_ev[e], done(n))
                    mm(py[par][:, :], w2[:, e, :], hs[:, e % 2, :], start=False, stop=e == NE - 1).then_inc(y_mm[e], 1)
                    if n1 is not None:
                        if e == 1:
                            r_lt(n1, j1, 1 - par)
                        if e == 3:
                            r_tr(n1)
                        if e == 10:
                            r_ct(n1)

            tiles(pe, step, lead)

        @block.scalar
        def _(act):
            act.wait_ge(loaded, 16 * len(loads))

            def r_lt(n):
                act.wait_ge(lt_mm, done(n))
                act.wait_ge(tr_mm, done(n - 1))
                nc.scalar.activation(lt[:, :], pl[0:NE, :], ACT.Identity, bias=rb[:, :]).then_inc(lt_ev, 1)

            def r_exp(n):
                act.wait_ge(sub_ev, done(n))
                nc.scalar.activation(lg[:, :, 0:E_N], lg[:, :, 0:E_N], ACT.Exp).then_inc(exp_ev, 1)

            def lead(n, j, par):
                r_lt(n)
                r_exp(n)

            def step(n, j, par, n1, j1):
                for e in range(NE):
                    act.wait_ge(hc_mm[e], done(n))
                    act.wait_ge(hs_ev[e - 2], done(n) if e >= 2 else done(n - 1))
                    nc.scalar.activation(hr[:, e % 2, :], ph[e % 2][:, :], ACT.Relu, bias=b1[:, e:e + 1]).then_inc(relu[e], 1)
                    if n1 is not None:
                        if e == 2:
                            r_lt(n1)
                        if e == 5:
                            r_exp(n1)

            tiles(act, step, lead)

        @block.vector
        def _(dve):
            nc.vector.memset(parts[0][:, :], 0.0)
            nc.vector.memset(parts[1][:, :], 0.0)
            nc.vector.memset(p20[:, :, :], -1.0)
            nc.vector.memset(rw[:, :], 0.0)
            nc.vector.memset(rb[:, :], 0.0)
            nc.vector.memset(cw[:, :, :], 1.0).then_inc(zeroed, 1)
            dve.wait_ge(zeroed, 1)
            dve.wait_ge(loaded, 16 * len(loads))
            nc.vector.tensor_copy(sel[:, :, :].rearrange("p e n -> p (e n)"), self32[:, :]).then_inc(const, 1)

            def r_sub(n):
                dve.wait_ge(tr_mm, done(n))
                v = pt[:, 0:4 * NE].rearrange("p (a e) -> p a e", e=NE)[:, :, 0:E_N]
                nc.vector.tensor_reduce(mx[:, :], v, AX.X, ALU.max).then_inc(mx_ev, 1)
                dve.wait_ge(mx_ev, done(n))
                nc.vector.tensor_tensor(lg[:, :, 0:E_N], v, mx[:, :].unsqueeze(2).broadcast_to([128, 4, E_N]), ALU.subtract).then_inc(sub_ev, 1)

            def r_top(n):
                dve.wait_ge(exp_ev, done(n))
                nc.vector.tensor_reduce(den[:, :], lg[:, :, 0:E_N], AX.X, ALU.add).then_inc(den_ev, 1)
                dve.wait_ge(den_ev, done(n))
                nc.vector.reciprocal(den[:, :], den[:, :]).then_inc(rden_ev, 1)
                dve.wait_ge(rden_ev, done(n))
                nc.vector.tensor_tensor(p20[:, :, 0:E_N], lg[:, :, 0:E_N], den[:, :].unsqueeze(2).broadcast_to([128, 4, E_N]), ALU.mult).then_inc(p_ev, 1)
                dve.wait_ge(p_ev, done(n))
                nc.vector.memset(held[:, 0:1], 0.0)
                for a in range(4):
                    last = nc.vector.max(top[:, a, :], p20[:, a, :])
                last.then_inc(top_ev, 1)
                dve.wait_ge(top_ev, done(n))
                nc.vector.memset(top[:, :, TOPK:8], -1.0).then_inc(topf_ev, 1)
                dve.wait_ge(topf_ev, done(n))
                nc.vector.memset(held[:, 1:2], 0.0)
                for a in range(4):
                    last = nc.vector.match_replace(m20[:, a, :], top[:, a, :], p20[:, a, :], -2.0)
                last.then_inc(m_ev, 1)
                dve.wait_ge(m_ev, done(n))
                dve.wait_ge(ct_mm, done(n - 1))
                nc.vector.scalar_tensor_tensor(cw[:, :, 0:E_N], m20[:, :, 0:E_N], -1.5, p20[:, :, 0:E_N], ALU.is_lt, ALU.mult).then_inc(cw_ev, 1)

            def r_parts(n, par):
                dve.wait_ge(ct_mm, done(n))
                dve.wait_ge(y_mm[NE - 1], done(n - 2))
                hi, mid, lo = (parts[par][32 * i:32 * i + NE, :] for i in range(3))
                nc.vector.tensor_copy(cwt[par][:, :], pl[0:NE, :]).then_inc(ct_ev, 1)
                nc.vector.tensor_copy(hi, pl[0:NE, :]).then_inc(hi_ev, 1)
                dve.wait_ge(hi_ev, done(n))
                nc.vector.tensor_tensor(rest[:, 0, :], pl[0:NE, :], hi, ALU.subtract).then_inc(r1_ev, 1)
                dve.wait_ge(r1_ev, done(n))
                nc.vector.tensor_copy(midw[:, :], rest[:, 0, :]).then_inc(mid_ev, 1)
                dve.wait_ge(mid_ev, done(n))
                nc.vector.tensor_copy(mid, midw[:, :])
                nc.vector.tensor_tensor(rest[:, 1, :], rest[:, 0, :], midw[:, :], ALU.subtract).then_inc(r2_ev, 1)
                dve.wait_ge(r2_ev, done(n))
                nc.vector.tensor_copy(lo, rest[:, 1, :]).then_inc(parts_ev, 1)

            def lead(n, j, par):
                r_sub(n)
                r_top(n)
                r_parts(n, par)

            def step(n, j, par, n1, j1):
                for e in range(NE):
                    dve.wait_ge(relu[e], done(n))
                    dve.wait_ge(y_mm[e - 2], done(n) if e >= 2 else done(n - 1))
                    if e < E_N:
                        nc.vector.tensor_tensor(hs[:, e % 2, :], pc[e % 2][:, :], hr[:, e % 2, :], ALU.mult).then_inc(hs_ev[e], 1)
                    else:
                        nc.vector.tensor_copy(hs[:, e % 2, :], hr[:, e % 2, :]).then_inc(hs_ev[e], 1)
                    if n1 is not None:
                        if e == 4:
                            r_sub(n1)
                        if e == 6:
                            r_top(n1)
                        if e == 11:
                            r_parts(n1, 1 - par)
                dve.wait_ge(y_mm[NE - 1], done(n))
                x = g.xT[:, bass.ds(j, 1), TILE * par:TILE * (par + 1)]
                nc.vector.tensor_tensor(x, py[par][:, :].unsqueeze(1), x, ALU.add).then_inc(acc_ev, 1)

            tiles(dve, step, lead)


def decay_attention(nc, g):
    NG = NTOK // 128
    LV = 5
    with ExitStack() as ctx:
        new_sem = semaphores(nc, ctx)
        sb = lambda n, s, dt=F32: ctx.enter_context(nc.sbuf_tensor("b_" + n, s, dt))
        pb = lambda n, s: ctx.enter_context(nc.psum_tensor("b_" + n, s, F32))
        sem = lambda n: new_sem("b_" + n)
        w = sb("w", [128, 6, 128])
        bw = sb("bw", [128, 1])
        masks = sb("masks", [128, LV + 1, 128])
        bmask = sb("bmask", [128, 128])
        F = sb("F", [128, NTOK])
        rF = sb("rF", [128, NTOK])
        kB = sb("kB", [128, NTOK])
        V = sb("V", [128, NG, 128])
        P = sb("P", [128, NG, 2, 128])
        kBr = sb("kBr", [128, NG, 128])
        z1 = sb("z1", [128, 2, TILE])
        wz = sb("wz", [128, 2, TILE])
        tmp4 = sb("tmp4", [128, 4, TILE])
        S = sb("S", [128, 2, B, 128])
        uS = sb("uS", [128, 2, B, 128])
        oT = sb("oT", [128, 2, B, 128])
        bank = [pb(f"bank{i}", [128, TILE]) for i in range(8)]
        loaded = sem("loaded")
        d = g.dram
        loads = [(w[:, i, :], d["b_" + n]) for i, n in enumerate(("Wx", "Ww", "Wk", "Wv", "Wr", "Wo"))] + [
            (bw[:, :], d["b_bw"].unsqueeze(1)), (masks[:, :, :].rearrange("p a b -> p (a b)"), d["c_bmasks"]), (bmask[:, :], d["c_bdiag"])]
        mm = nc.tensor.matmul
        zx, zx_ev, z_mm, k_mm, r_mm, w_ev, a_ev, k_ev, r_ev, v_mm, v_ev = (sem(n) for n in ("zx", "zx_ready", "z_mm", "k_mm", "r_mm", "w_ready", "a_ready", "k_ready", "r_ready", "v_mm", "v_ready"))
        with nc.Block() as block:
            @block.sync
            def _(sp):
                for dst, src in loads:
                    sp.dma_start(dst, src).then_inc(loaded, 16)

            @block.tensor
            def _(pe):
                pe.wait_ge(loaded, 16 * len(loads))
                for i in range(NT):
                    x = g.xn[:, i // 2, PAD + TILE * (i % 2):PAD + TILE * (i % 2 + 1)]
                    if i:
                        pe.wait_ge(zx_ev, i)
                    mm(bank[0][:, :], w[:, 0, :], x, start=True, stop=True).then_inc(zx, 1)
                    if i:
                        pe.wait_ge(k_ev, i)
                    mm(bank[1][:, :], w[:, 2, :], x, start=True, stop=True).then_inc(k_mm, 1)
                    if i:
                        pe.wait_ge(r_ev, i)
                    mm(bank[2][:, :], w[:, 4, :], x, start=True, stop=True).then_inc(r_mm, 1)
                    if i >= 2:
                        pe.wait_ge(v_ev, i - 1)
                    for a in range(4):
                        last = mm(bank[4 + i % 2][:, a * 128:(a + 1) * 128], x[:, a * 128:(a + 1) * 128], w[:, 3, :], start=True, stop=True)
                    last.then_inc(v_mm, 1)
                    pe.wait_ge(zx_ev, i + 1)
                    if i:
                        pe.wait_ge(w_ev, i)
                    mm(bank[3][:, :], w[:, 1, :], z1[:, i % 2, :], start=True, stop=True).then_inc(z_mm, 1)

            @block.scalar
            def _(act):
                act.wait_ge(loaded, 16 * len(loads))
                for i in range(NT):
                    act.wait_ge(zx, i + 1)
                    nc.scalar.activation(z1[:, i % 2, :], bank[0][:, :], ACT.Copy).then_inc(zx_ev, 1)
                    act.wait_ge(r_mm, i + 1)
                    nc.scalar.activation(rF[:, TILE * i:TILE * (i + 1)], bank[2][:, :], ACT.Sigmoid).then_inc(r_ev, 1)
                    act.wait_ge(z_mm, i + 1)
                    if i >= 2:
                        act.wait_ge(a_ev, i - 1)
                    nc.scalar.activation(wz[:, i % 2, :], bank[3][:, :], ACT.Sigmoid, bias=bw[:, :]).then_inc(w_ev, 1)

            @block.vector
            def _(dve):
                for i in range(NT):
                    dve.wait_ge(k_mm, i + 1)
                    nc.vector.tensor_copy(kB[:, TILE * i:TILE * (i + 1)], bank[1][:, :]).then_inc(k_ev, 1)
                    dve.wait_ge(v_mm, i + 1)
                    nc.vector.tensor_copy(V[:, 4 * i:4 * i + 4, :], bank[4 + i % 2][:, :].rearrange("p (a n) -> p a n", a=4)).then_inc(v_ev, 1)
                    dve.wait_ge(w_ev, i + 1)
                    nc.vector.tensor_scalar(F[:, TILE * i:TILE * (i + 1)], wz[:, i % 2, :], -1.0, 1.0, ALU.mult, ALU.add).then_inc(a_ev, 1)

        p_mm, p_ev, up_ev, t_ev, add_ev = sem("p_mm"), sem("p_ready"), sem("up_ready"), sem("f_read"), sem("added")
        NBK = NG // 2
        with nc.Block() as block:
            @block.tensor
            def _(pe):
                n = 0
                for l in range(LV + 1):
                    for q in range(NBK):
                        if l:
                            pe.wait_ge(up_ev, (l - 1) * B + q // (NBK // B) + 1)
                        if n >= 8:
                            pe.wait_ge(p_ev, n - 7)
                        h = q % 2
                        for a in range(4):
                            t0 = (4 * (q // 2) + a) * 128
                            last = mm(bank[n % 8][:, a * 128:(a + 1) * 128], kB[64 * h:64 * h + 64, t0:t0 + 128], rF[64 * h:64 * h + 64, t0:t0 + 128], start=True, stop=True)
                        last.then_inc(p_mm, 1)
                        n += 1

            @block.gpsimd
            def _(pool):
                pool.wait_ge(loaded, 16 * len(loads))
                for n in range(NBK * (LV + 1)):
                    l, q = divmod(n, NBK)
                    if l:
                        pool.wait_ge(p_ev, n + 1)
                        dst = P[:, 4 * (q // 2):4 * (q // 2) + 4, q % 2, :]
                        nc.gpsimd.tensor_tensor(dst, dst, tmp4[:, n % 4, :].rearrange("p (a t) -> p a t", a=4), ALU.add).then_inc(add_ev, 1)
                        pool.wait_ge(add_ev, n + 1 - NBK)

            @block.vector
            def _(dve):
                n = 0
                ups = 0
                for l in range(LV + 1):
                    for q in range(NBK):
                        dve.wait_ge(p_mm, n + 1)
                        src = bank[n % 8][:, :].rearrange("p (x t) -> p x t", t=128)
                        mask = masks[:, l, :].unsqueeze(1).broadcast_to([128, 4, 128])
                        if l == 0:
                            dst = P[:, 4 * (q // 2):4 * (q // 2) + 4, q % 2, :]
                        else:
                            dst = tmp4[:, n % 4, :].rearrange("p (x t) -> p x t", t=128)
                            if n - NBK >= 4:
                                dve.wait_ge(add_ev, n - NBK - 3)
                        nc.vector.tensor_tensor(dst, src, mask, ALU.mult).then_inc(p_ev, 1)
                        n += 1
                        if n % (NBK // B) == 0 and l <= LV:
                            b = q // (NBK // B)
                            s0, s1 = b * T, (b + 1) * T
                            if l == 0:
                                nc.vector.tensor_tensor(rF[:, s0:s1], rF[:, s0:s1], F[:, s0:s1], ALU.mult).then_inc(up_ev, 1)
                                continue
                            hs = 1 << (l - 1)
                            v = lambda t: t[:, s0:s1].rearrange("p (n two h) -> p n two h", two=2, h=hs)
                            fv, rv, kv = v(F), v(rF), v(kB)
                            sh = [128, T // (2 * hs), hs]
                            mid, end = fv[:, :, 0, hs - 1:hs].broadcast_to(sh), fv[:, :, 1, hs - 1:hs].broadcast_to(sh)
                            nc.vector.tensor_tensor(kv[:, :, 0, :], kv[:, :, 0, :], end, ALU.mult)
                            nc.vector.tensor_tensor(rv[:, :, 1, :], rv[:, :, 1, :], mid, ALU.mult).then_inc(t_ev, 1)
                            ups += 1
                            dve.wait_ge(t_ev, ups)
                            nc.vector.tensor_tensor(fv[:, :, 1, :], fv[:, :, 1, :], mid, ALU.mult).then_inc(up_ev, 1)
                            dve.wait_ge(up_ev, l * B + b + 1)

        kt_mm, kt_ev, u_mm, u_ev, s_ev, i_mm, a_mm, o_ev, o2_ev, y_mm, y_ev, z_ev = (sem(n) for n in ("kt_mm", "kt_ready", "u_mm", "u_ready", "s_ready", "i_mm", "a_mm", "o_ready", "o2_ready", "y_mm", "y_ready", "s_zero"))
        NGB = NG // B
        with nc.Block() as block:
            @block.tensor
            def _(pe):
                for q in range(NG // 4):
                    if q >= 2:
                        pe.wait_ge(kt_ev, q - 1)
                    for a in range(4):
                        last = nc.tensor.transpose(bank[q % 2][:, a * 128:(a + 1) * 128], kB[:, (4 * q + a) * 128:(4 * q + a + 1) * 128], g.ident[:, :])
                    last.then_inc(kt_mm, 1)
                pe.wait_ge(kt_ev, NG // 4)
                pe.wait_ge(z_ev, 1)

                def update(n):
                    gr, c = divmod(n, 4)
                    if n >= 2:
                        pe.wait_ge(u_ev, n - 1)
                    for b in range(B):
                        i = b * NGB + gr
                        last = mm(bank[2 + n % 2][:, b * 128:(b + 1) * 128], kBr[32 * c:32 * c + 32, i, :], V[32 * c:32 * c + 32, i, :], start=True, stop=True)
                    last.then_inc(u_mm, 1)

                update(0)
                for gr in range(NGB):
                    if gr >= 2:
                        pe.wait_ge(o_ev, gr - 1)
                    for b in range(B):
                        i = b * NGB + gr
                        for h in range(2):
                            last = mm(bank[4 + gr % 2][64 * h:64 * h + 64, b * 128:(b + 1) * 128], V[:, i, 64 * h:64 * h + 64], P[:, i, h, :], start=True, stop=True)
                    last.then_inc(a_mm, 1)
                    for c in range(4):
                        n = 4 * gr + c
                        if n + 1 < 4 * NGB:
                            update(n + 1)
                        if n:
                            pe.wait_ge(s_ev, n)
                        if c == 0 and gr:
                            pe.wait_ge(o2_ev, gr)
                        for b in range(B):
                            last = mm(bank[6][:, b * 128 + 32 * c:b * 128 + 32 * c + 32], S[:, n % 2, b, :], rF[:, b * T + 32 * n:b * T + 32 * n + 32], start=True, stop=True)
                        last.then_inc(i_mm, 1)
                    pe.wait_ge(o2_ev, gr + 1)
                    if gr:
                        pe.wait_ge(y_ev, gr)
                    mm(bank[7][:, :], w[:, 5, :], oT[:, gr % 2, :, :].rearrange("p b t -> p (b t)"), start=True, stop=True).then_inc(y_mm, 1)

            @block.scalar
            def _(act):
                for q in range(NG // 4):
                    act.wait_ge(kt_mm, q + 1)
                    nc.scalar.activation(kBr[:, 4 * q:4 * q + 4, :], bank[q % 2][:, :].rearrange("p (a n) -> p a n", a=4), ACT.Copy).then_inc(kt_ev, 1)
                for gr in range(NGB):
                    act.wait_ge(a_mm, gr + 1)
                    if gr >= 2:
                        act.wait_ge(y_mm, gr - 1)
                    nc.scalar.activation(oT[:, gr % 2, :, :].rearrange("p b t -> p (b t)"), bank[4 + gr % 2][:, :], ACT.Copy).then_inc(o_ev, 1)

            @block.vector
            def _(dve):
                nc.vector.memset(S[:, 0, :, :], 0.0).then_inc(z_ev, 1)
                dve.wait_ge(z_ev, 1)
                for n in range(4 * NGB):
                    if n + 1 < 4 * NGB:
                        dve.wait_ge(u_mm, n + 1)
                        nc.vector.tensor_tensor(uS[:, n % 2, :, :], bank[2 + n % 2][:, :].rearrange("p (b e) -> p b e", b=B),
                                                bmask[:, :].unsqueeze(1).broadcast_to([128, B, 128]), ALU.mult).then_inc(u_ev, 1)
                        dve.wait_ge(u_ev, n + 1)
                        if n:
                            dve.wait_ge(s_ev, n)
                            dve.wait_ge(i_mm, n)
                        for b in range(B):
                            end = b * T + 32 * n + 31
                            last = nc.vector.scalar_tensor_tensor(S[:, (n + 1) % 2, b, :], S[:, n % 2, b, :], F[:, end:end + 1], uS[:, n % 2, b, :], ALU.mult, ALU.add)
                        last.then_inc(s_ev, 1)
                    if n % 4 == 3:
                        gr = n // 4
                        dve.wait_ge(i_mm, n + 1)
                        dve.wait_ge(o_ev, gr + 1)
                        o = oT[:, gr % 2, :, :].rearrange("p b t -> p (b t)")
                        nc.vector.tensor_tensor(o, bank[6][:, :], o, ALU.add).then_inc(o2_ev, 1)
                        dve.wait_ge(y_mm, gr + 1)
                        x = g.xT[:, :, gr * 128:(gr + 1) * 128]
                        nc.vector.tensor_tensor(x, bank[7][:, :].rearrange("p (b t) -> p b t", b=B), x, ALU.add).then_inc(y_ev, 1)



INS = [("x", "L0_attn_a_x")] + [(n, "L0_attn_a_" + n) for n in ("Wq", "Wk", "Wv", "Wb", "Wa", "A_log", "dt_bias", "conv_q", "conv_k", "conv_v", "Wg", "rms_weight", "Wo")] + [
    ("b_" + n, "L0_attn_b_" + n) for n in ("ln_g", "ln_b", "Wx", "Ww", "bw", "Wk", "Wv", "Wr", "Wo")] + [
    (n, "L0_ffn_" + n) for n in ("router_W", "router_b", "sW1", "sb1", "sW2", "sb2", "eW1", "eb1", "eW2", "eb2")]


def build(nc, dram, phases="abcd"):
    with ExitStack() as ctx:
        sb = lambda n, s, dt=F32: ctx.enter_context(nc.sbuf_tensor(n, s, dt))
        g = Shared()
        g.dram = dram
        g.xT = sb("xT", [128, B, T])
        g.xn = sb("xn", [128, B, PAD + T])
        g.ident = sb("ident", [128, 128])
        g.mean = sb("mean", [128, 128])
        g.ones = sb("ones", [128, 128])
        g.half = sb("half", [128, U])
        g.minus_half = sb("minus_half", [128, 1])
        zeroed = ctx.enter_context(nc.semaphore("zeroed"))
        g.rms_sem = ctx.enter_context(nc.semaphore("rms_in"))
        with ExitStack() as a:
            sa = lambda n, s: a.enter_context(nc.sbuf_tensor(n, s, F32))
            g.mask4 = sa("mask4", [R, 128])
            g.lev = sa("lev", [R, (LEVELS + 1) * R])
            g.after = sa("after", [TC, R])
            g.upto = sa("upto", [TC, TC])
            g.beta = sa("beta", [R, NH + 1, NTOK // TC])
            g.gt = sa("gt", [TC, NTOK // TC, NH + 1])
            g.rms_in = sa("rms_w", [128, 1])
            g.const_loads = [("c_ident", g.ident[:, :]), ("c_mean", g.mean[:, :]), ("c_mask4", g.mask4[:, :]), ("c_lev", g.lev[:, :]),
                             ("c_after", g.after[:, :]), ("c_upto", g.upto[:, :])]
            load_rows(nc, g)
            with nc.Block() as b:
                @b.vector
                def _(dve):
                    nc.vector.memset(g.xn[:, :, 0:PAD], 0.0)
                    nc.vector.memset(g.half[:, :], 0.5)
                    nc.vector.memset(g.minus_half[:, :], -0.5)
                    nc.vector.memset(g.ones[:, :], 1.0).then_inc(zeroed, 1)
                    dve.wait_ge(zeroed, 1)

                @b.sync
                def _(sp):
                    sp.dma_start(g.rms_in[:, :], dram["rms_weight"].unsqueeze(1)).then_inc(g.rms_sem, 16)
                    sp.wait_ge(g.rms_sem, 16)
            layernorm(nc, g, "ln0", lambda i: g.xT[:, i // 2, TILE * (i % 2):TILE * (i % 2 + 1)])
            decay_gates(nc, g)
            delta_attention(nc, g)
        x_tile = lambda i: g.xT[:, i // 2, TILE * (i % 2):TILE * (i % 2 + 1)]
        n_tile = lambda i: g.xn[:, i // 2, PAD + TILE * (i % 2):PAD + TILE * (i % 2 + 1)]
        layernorm(nc, g, "ln1", x_tile)
        mixture(nc, g, "f1")
        layernorm(nc, g, "ln2", x_tile)
        with ExitStack() as a:
            gain = a.enter_context(nc.sbuf_tensor("ln_gain", [128, 2], F32))
            gain_in = a.enter_context(nc.semaphore("ln_gain_in"))
            with nc.Block() as b:
                @b.sync
                def _(sp):
                    sp.dma_start(gain[:, 0:1], dram["b_ln_g"].unsqueeze(1)).then_inc(gain_in, 16)
                    sp.dma_start(gain[:, 1:2], dram["b_ln_b"].unsqueeze(1)).then_inc(gain_in, 16)
                    sp.wait_ge(gain_in, 32)
            layernorm(nc, g, "ln3", n_tile, (gain[:, 0:1], gain[:, 1:2]))
            decay_attention(nc, g)
        layernorm(nc, g, "ln4", x_tile)
        mixture(nc, g, "f2")
        store_rows(nc, g)


def kernel(**inputs):
    import concourse.bacc as _bacc
    from concourse.bass_utils import run_bass_kernel_spmd as _run

    nc = _bacc.Bacc("TRN2", target_bir_lowering=False, num_devices=1)
    arrays, dram = {}, {}
    named = [(s, np.ascontiguousarray(inputs[n])) for s, n in INS] + list(constants().items())
    for name, a in named:
        arrays[f"in_{name}_dram"] = a
        dram[name] = nc.dram_tensor(f"in_{name}_dram", a.shape, mybir.dt.from_np(a.dtype), kind="ExternalInput").ap()
    dram["out"] = nc.dram_tensor("out_0_dram", (B, T, D), F32, kind="ExternalOutput").ap()
    build(nc, dram)
    r = _run(nc, [arrays], core_ids=[0])
    return r.results[0]["out_0_dram"]
```
